# Optimizing a Trainium2 kernel written in Bass

```python
import numpy as np
import jax
import jax.numpy as jnp

def _softmax(x, axis=-1):
    return jax.nn.softmax(x, axis=axis)

def _gelu(x):
    return jax.nn.gelu(x, approximate=True)

def _silu(x):
    return jax.nn.silu(x)

def _sigmoid(x):
    return jax.nn.sigmoid(x)

def _layernorm(x, axis=-1, eps=1e-05):
    m = jnp.mean(x, axis=axis, keepdims=True)
    v = jnp.var(x, axis=axis, keepdims=True)
    return (x - m) / jnp.sqrt(v + eps)

def _scatter_add(tgt, idx, src, axis=0):
    return tgt.at[idx].add(src)

def _segment_sum(src, seg, n):
    return jax.ops.segment_sum(src, seg, n)
kernel_name = 'mk_xattn_ffn_d4_seqx_r8_8599fb'

def setup_inputs(seed: int=0):
    np.random.seed(seed)
    _w = jnp.asarray

    def _rec_inputs():
        import jax
        import jax.numpy as jnp
        _rk = jax.random.key(seed)
        x = -0.0005146 + 1 * jax.random.normal(jax.random.fold_in(_rk, 1), (16, 64, 512), jnp.float32)
        _lenS = 64 - jax.random.randint(jax.random.fold_in(_rk, 7), (16,), 0, max(1, 64 // 4) + 1, jnp.int32)
        _lenS2 = 64 - jax.random.randint(jax.random.fold_in(_rk, 8), (16,), 0, max(1, 64 // 4) + 1, jnp.int32)
        _ctx_4096P = jax.random.normal(jax.random.fold_in(_rk, 11), (16, 16, 512), jnp.float32)
        _ctx_4096c = jax.random.dirichlet(jax.random.fold_in(_rk, 511), 0.3 * jnp.ones((16,), jnp.float32), (16, 64))
        _ctx_4096t = jnp.einsum('bsk,bkd->bsd', _ctx_4096c, _ctx_4096P)
        _ctx_4096t = _ctx_4096t * jax.lax.rsqrt(jnp.mean(jnp.square(_ctx_4096t)) + 1e-12) * 0.953939
        ctx_4096 = -0.000520686 + 1.00062 * (_ctx_4096t + 0.3 * jax.random.normal(jax.random.fold_in(_rk, 611), (16, 64, 512), jnp.float32))
        _validS = jnp.arange(64)[None, :] < _lenS[:, None]
        _validS2 = jnp.arange(64)[None, :] < _lenS2[:, None]
        _causal = jnp.tril(jnp.ones((64, 64), dtype=bool))
        mask_1x1xSxS2_bk0 = jnp.logical_not(jnp.broadcast_to(_validS2[0:1, None, None, :], (1, 1, 64, 64)))
        return (x, ctx_4096, mask_1x1xSxS2_bk0)
    x, ctx_4096, mask_1x1xSxS2_bk0 = _rec_inputs()

    def _L0_xattn_setup():
        import jax, jax.numpy as jnp
        import numpy as np
        B, C, N = (8, 64, 512)
        key = jax.random.key(seed)
        k1, k2, k3 = jax.random.split(key, 3)
        k = jax.random.normal(k1, (B, C, N), dtype=jnp.float32)
        q = jax.random.normal(k2, (B, C, N), dtype=jnp.float32)
        v = jax.random.normal(k3, (B, C, N), dtype=jnpp.float32) if False else jax.random.normal(k3, (B, C, N), dtype=jnp.float32)
        return {'k': k, 'q': q, 'v': v}
    _L0_xattn_all = _L0_xattn_setup()
    _L0_xattn_in = {k: v for k, v in _L0_xattn_all.items() if k in ()}
    del _L0_xattn_all

    def _L0_ffn_setup():
        import jax, jax.numpy as jnp
        import numpy as np
        IN_F = 512
        OUT_F = 512
        N_CLUSTERS = 64
        THRESHOLD = 0.01
        TEMPERATURE = 0.1
        BATCH, SEQ = (4, 256)
        key = jax.random.key(seed)
        k1, k2, k3, k4, k5 = jax.random.split(key, 5)
        s = 1.0 / np.sqrt(IN_F)
        return {'input': jax.random.normal(k1, (BATCH, SEQ, IN_F), dtype=jnp.float32), 'weight': jax.random.normal(k2, (OUT_F, IN_F), dtype=jnp.float32) * s, 'bias': jax.random.uniform(k3, (OUT_F,), dtype=jnp.float32, minval=-s, maxval=s), 'centroids': jax.random.normal(k4, (N_CLUSTERS, IN_F), dtype=jnp.float32) * s, 'assignments': jax.random.randint(k5, (OUT_F,), 0, N_CLUSTERS, dtype=jnp.int32)}
    _L0_ffn_all = _L0_ffn_setup()
    _L0_ffn_in = {k: v for k, v in _L0_ffn_all.items() if k in ('weight', 'bias', 'centroids', 'assignments')}
    del _L0_ffn_all

    def _L1_xattn_setup():
        import jax, jax.numpy as jnp
        import numpy as np
        HEADS = 32
        KV_HEADS = 8
        HEAD_DIM = 128
        EPS = 1e-06

        def rms_norm(x, w):
            var = jnp.mean(jnp.square(x.astype(jnp.float32)), axis=-1, keepdims=True)
            return (x.astype(jnp.float32) * jax.lax.rsqrt(var + EPS)).astype(x.dtype) * w
        key = jax.random.key(seed)
        ks = jax.random.split(key, 6)
        bsz, n_lat, seq, hidden = (8, 64, 512, 512)
        return {'latents': jax.random.normal(ks[0], (bsz, n_lat, hidden), jnp.float32), 'context': jax.random.normal(ks[1], (bsz, seq, hidden), jnp.float32), 'Wq': jax.random.normal(ks[2], (hidden, HEADS * HEAD_DIM), jnp.float32) * 0.02, 'Wk': jax.random.normal(ks[3], (hidden, KV_HEADS * HEAD_DIM), jnp.float32) * 0.02, 'Wv': jax.random.normal(ks[4], (hidden, KV_HEADS * HEAD_DIM), jnp.float32) * 0.02, 'Wo': jax.random.normal(ks[5], (HEADS * HEAD_DIM, hidden), jnp.float32) * 0.02, 'q_norm_w': jnp.ones((HEAD_DIM,), jnp.float32), 'k_norm_w': jnp.ones((HEAD_DIM,), jnp.float32)}
    _L1_xattn_all = _L1_xattn_setup()
    _L1_xattn_in = {k: v for k, v in _L1_xattn_all.items() if k in ('Wq', 'Wk', 'Wv', 'Wo', 'q_norm_w', 'k_norm_w')}
    del _L1_xattn_all

    def _L1_ffn_setup():
        import jax, jax.numpy as jnp
        import numpy as np
        RANKS = (8, 16, 32, 64)
        TOPK = 1
        SCALING = 1.0 / 4
        key = jax.random.key(seed)
        ks = jax.random.split(key, 7)
        D_IN, D_OUT, MAX_R, N_RANKS = (512, 512, 64, len(RANKS))
        B_, S_ = (4, 256)
        return {'hidden_states': jax.random.normal(ks[0], (B_, S_, D_IN), jnp.float32), 'W': jax.random.normal(ks[1], (D_OUT, D_IN), jnp.float32) * 0.02, 'b': jax.random.normal(ks[2], (D_OUT,), jnp.float32) * 0.02, 'A': jax.random.normal(ks[3], (MAX_R, D_IN), jnp.float32) * 0.02, 'B': jnp.zeros((D_OUT, MAX_R), jnp.float32) + jax.random.normal(ks[4], (D_OUT, MAX_R), jnp.float32) * 0.02, 'gate_w': jax.random.normal(ks[5], (N_RANKS, D_IN), jnp.float32) * 0.02, 'gate_b': jax.random.normal(ks[6], (N_RANKS,), jnp.float32) * 0.02}
    _L1_ffn_all = _L1_ffn_setup()
    _L1_ffn_in = {k: v for k, v in _L1_ffn_all.items() if k in ('W', 'b', 'A', 'B', 'gate_w', 'gate_b')}
    del _L1_ffn_all

    def _L2_xattn_setup():
        import jax, jax.numpy as jnp
        import numpy as np
        B, T, D_MODEL = (1, 256, 512)
        NUM_Q_HEADS, NUM_KV_HEADS, KEY_SIZE = (32, 8, 128)
        ATTN_MULT = 0.08838834764831845
        MAX_ATTN_VAL = 30.0

        def rotate_half(x):
            x1, x2 = jnp.split(x, 2, axis=-1)
            return jnp.concatenate((-x2, x1), axis=-1)

        def apply_rope(x):
            b, t, h, d = x.shape
            exponents = jnp.arange(0, d, 2, dtype=jnp.float32)
            inv_freq = 1.0 / 10000.0 ** (exponents / d)
            pos = jnp.arange(t, dtype=jnp.float32)
            phase = pos[:, None] * inv_freq[None, :]
            phase = jnp.tile(phase, (1, 2))[None, :, None, :]
            return (x * jnp.cos(phase) + rotate_half(x) * jnp.sin(phase)).astype(x.dtype)
        key = jax.random.key(seed)
        ks = jax.random.split(key, 8)
        query = jax.random.normal(ks[0], (B, T, D_MODEL), dtype=jnp.float32)
        kk = jax.random.normal(ks[1], (B, T, D_MODEL), dtype=jnp.float32)
        vv = jax.random.normal(ks[2], (B, T, D_MODEL), dtype=jnp.float32)
        mask = jnp.tril(jnp.ones((T, T), dtype=bool))[None, None, :, :]
        s = 0.02
        Wq = jax.random.normal(ks[3], (D_MODEL, NUM_Q_HEADS * KEY_SIZE), dtype=jnp.float32) * s
        Wk = jax.random.normal(ks[4], (D_MODEL, NUM_KV_HEADS * KEY_SIZE), dtype=jnp.float32) * s
        Wv = jax.random.normal(ks[5], (D_MODEL, NUM_KV_HEADS * KEY_SIZE), dtype=jnp.float32) * s
        Wo = jax.random.normal(ks[6], (NUM_Q_HEADS * KEY_SIZE, D_MODEL), dtype=jnp.float32) * s
        return {'query': query, 'key': kk, 'value': vv, 'mask': mask, 'Wq': Wq, 'Wk': Wk, 'Wv': Wv, 'Wo': Wo}
    _L2_xattn_all = _L2_xattn_setup()
    _L2_xattn_in = {k: v for k, v in _L2_xattn_all.items() if k in ('Wq', 'Wk', 'Wv', 'Wo')}
    del _L2_xattn_all

    def _L2_ffn_setup():
        import jax, jax.numpy as jnp
        import numpy as np
        D_MODEL = 512
        D_FF = 1376
        key = jax.random.key(seed)
        k1, k2, k3, k4 = jax.random.split(key, 4)
        x = jax.random.normal(k1, (2, 256, D_MODEL), dtype=jnp.float32)
        W_gate = jax.random.normal(k2, (D_FF, D_MODEL), dtype=jnp.float32) * D_MODEL ** (-0.5)
        W_up = jax.random.normal(k3, (D_FF, D_MODEL), dtype=jnp.float32) * D_MODEL ** (-0.5)
        W_down = jax.random.normal(k4, (D_MODEL, D_FF), dtype=jnp.float32) * D_FF ** (-0.5)
        return {'x': x, 'W_gate': W_gate, 'W_up': W_up, 'W_down': W_down}
    _L2_ffn_all = _L2_ffn_setup()
    _L2_ffn_in = {k: v for k, v in _L2_ffn_all.items() if k in ('W_gate', 'W_up', 'W_down')}
    del _L2_ffn_all

    def _L3_xattn_setup():
        import jax, jax.numpy as jnp
        import numpy as np
        EMB_DIM = 64
        HEADS = 8
        key = jax.random.key(seed)
        kq, kk, kv = jax.random.split(key, 3)
        B, C, N = (8, EMB_DIM, 512)
        q = jax.random.normal(kq, (B, C, N), dtype=jnp.float32)
        k = jax.random.normal(kk, (B, C, N), dtype=jnp.float32)
        v = jax.random.normal(kv, (B, C, N), dtype=jnp.float32)
        return {'q': q, 'k': k, 'v': v}
    _L3_xattn_all = _L3_xattn_setup()
    _L3_xattn_in = {k: v for k, v in _L3_xattn_all.items() if k in ()}
    del _L3_xattn_all

    def _L3_ffn_setup():
        import jax, jax.numpy as jnp
        import numpy as np
        GROUP_SIZE = 128

        def dequantize(imatrix, scales, zeros, group_size, out_dtype):
            rs = jnp.repeat(scales, group_size, axis=0)
            rz = jnp.repeat(zeros, group_size, axis=0)
            return ((imatrix.astype(rs.dtype) - rz.astype(rs.dtype)) * rs).astype(out_dtype)
        key = jax.random.key(seed)
        ks = jax.random.split(key, 10)
        H, I, G = (512, 1792, GROUP_SIZE)
        B, S = (4, 256)
        x = jax.random.normal(ks[0], (B, S, H), dtype=jnp.float32)
        gate_w = jax.random.randint(ks[1], (H, I), 0, 16, dtype=jnp.int32)
        gate_z = jax.random.randint(ks[2], (H // G, I), 0, 16, dtype=jnp.int32)
        gate_s = jax.random.uniform(ks[3], (H // G, I), dtype=jnp.float32) * 0.01
        up_w = jax.random.randint(ks[4], (H, I), 0, 16, dtype=jnp.int32)
        up_z = jax.random.randint(ks[5], (H // G, I), 0, 16, dtype=jnp.int32)
        up_s = jax.random.uniform(ks[6], (H // G, I), dtype=jnp.float32) * 0.01
        down_w = jax.random.randint(ks[7], (I, H), 0, 16, dtype=jnp.int32)
        down_z = jax.random.randint(ks[8], (I // G, H), 0, 16, dtype=jnp.int32)
        down_s = jax.random.uniform(ks[9], (I // G, H), dtype=jnp.float32) * 0.01
        return {'x': x, 'gate_w': gate_w, 'gate_z': gate_z, 'gate_s': gate_s, 'up_w': up_w, 'up_z': up_z, 'up_s': up_s, 'down_w': down_w, 'down_z': down_z, 'down_s': down_s}
    _L3_ffn_all = _L3_ffn_setup()
    _L3_ffn_in = {k: v for k, v in _L3_ffn_all.items() if k in ('gate_w', 'gate_z', 'gate_s', 'up_w', 'up_z', 'up_s', 'down_w', 'down_z', 'down_s')}
    del _L3_ffn_all
    return {'x': x, 'ctx_4096': ctx_4096, 'mask_1x1xSxS2_bk0': mask_1x1xSxS2_bk0, 'L0_ffn_weight': _L0_ffn_in['weight'], 'L0_ffn_bias': _L0_ffn_in['bias'], 'L0_ffn_centroids': _L0_ffn_in['centroids'], 'L0_ffn_assignments': _L0_ffn_in['assignments'], 'L1_xattn_Wq': _L1_xattn_in['Wq'], 'L1_xattn_Wk': _L1_xattn_in['Wk'], 'L1_xattn_Wv': _L1_xattn_in['Wv'], 'L1_xattn_Wo': _L1_xattn_in['Wo'], 'L1_xattn_q_norm_w': _L1_xattn_in['q_norm_w'], 'L1_xattn_k_norm_w': _L1_xattn_in['k_norm_w'], 'L1_ffn_W': _L1_ffn_in['W'], 'L1_ffn_b': _L1_ffn_in['b'], 'L1_ffn_A': _L1_ffn_in['A'], 'L1_ffn_B': _L1_ffn_in['B'], 'L1_ffn_gate_w': _L1_ffn_in['gate_w'], 'L1_ffn_gate_b': _L1_ffn_in['gate_b'], 'L2_xattn_Wq': _L2_xattn_in['Wq'], 'L2_xattn_Wk': _L2_xattn_in['Wk'], 'L2_xattn_Wv': _L2_xattn_in['Wv'], 'L2_xattn_Wo': _L2_xattn_in['Wo'], 'L2_ffn_W_gate': _L2_ffn_in['W_gate'], 'L2_ffn_W_up': _L2_ffn_in['W_up'], 'L2_ffn_W_down': _L2_ffn_in['W_down'], 'L3_ffn_gate_w': _L3_ffn_in['gate_w'], 'L3_ffn_gate_z': _L3_ffn_in['gate_z'], 'L3_ffn_gate_s': _L3_ffn_in['gate_s'], 'L3_ffn_up_w': _L3_ffn_in['up_w'], 'L3_ffn_up_z': _L3_ffn_in['up_z'], 'L3_ffn_up_s': _L3_ffn_in['up_s'], 'L3_ffn_down_w': _L3_ffn_in['down_w'], 'L3_ffn_down_z': _L3_ffn_in['down_z'], 'L3_ffn_down_s': _L3_ffn_in['down_s']}

def reference(x, ctx_4096, mask_1x1xSxS2_bk0, L0_ffn_weight, L0_ffn_bias, L0_ffn_centroids, L0_ffn_assignments, L1_xattn_Wq, L1_xattn_Wk, L1_xattn_Wv, L1_xattn_Wo, L1_xattn_q_norm_w, L1_xattn_k_norm_w, L1_ffn_W, L1_ffn_b, L1_ffn_A, L1_ffn_B, L1_ffn_gate_w, L1_ffn_gate_b, L2_xattn_Wq, L2_xattn_Wk, L2_xattn_Wv, L2_xattn_Wo, L2_ffn_W_gate, L2_ffn_W_up, L2_ffn_W_down, L3_ffn_gate_w, L3_ffn_gate_z, L3_ffn_gate_s, L3_ffn_up_w, L3_ffn_up_z, L3_ffn_up_s, L3_ffn_down_w, L3_ffn_down_z, L3_ffn_down_s):
    import jax
    import jax.numpy as jnp

    def _L0_xattn_ref(k, q, v):
        import jax, jax.numpy as jnp
        import numpy as np
        B, C, N = (8, 64, 512)
        input_dim = k.shape[1]
        scores = jnp.einsum('bcn,bcm->bnm', k, q) / jnp.sqrt(jnp.float32(input_dim))
        attn = jax.nn.softmax(scores, axis=-1)
        out = jnp.einsum('bnm,bcm->bcn', attn, v)
        return out

    def _L0_ffn_ref(input, weight, bias, centroids, assignments):
        import jax, jax.numpy as jnp
        import numpy as np
        IN_F = 512
        OUT_F = 512
        N_CLUSTERS = 64
        THRESHOLD = 0.01
        TEMPERATURE = 0.1
        BATCH, SEQ = (4, 256)
        shape = input.shape
        x = input.reshape(-1, shape[-1])
        dots = jax.nn.softmax(x @ centroids.T / TEMPERATURE, axis=-1)
        hits = dots > THRESHOLD
        query_sel = jnp.any(hits, axis=1)
        cluster_sel = jnp.any(hits, axis=0)
        row_sel = cluster_sel[assignments]
        dense = x @ weight.T + bias
        out = jnp.where(query_sel[:, None] & row_sel[None, :], dense, jnp.zeros((), dense.dtype))
        return out.reshape(*shape[:-1], -1)

    def _L1_xattn_ref(latents, context, Wq, Wk, Wv, Wo, q_norm_w, k_norm_w):
        import jax, jax.numpy as jnp
        import numpy as np
        HEADS = 32
        KV_HEADS = 8
        HEAD_DIM = 128
        EPS = 1e-06

        def rms_norm(x, w):
            var = jnp.mean(jnp.square(x.astype(jnp.float32)), axis=-1, keepdims=True)
            return (x.astype(jnp.float32) * jax.lax.rsqrt(var + EPS)).astype(x.dtype) * w
        bsz, q_len, hidden = latents.shape
        kv = jnp.concatenate([context, latents], axis=1)
        kv_len = kv.shape[1]
        groups = HEADS // KV_HEADS
        q = (latents @ Wq).reshape(bsz, q_len, HEADS, HEAD_DIM).transpose(0, 2, 1, 3)
        k = (kv @ Wk).reshape(bsz, kv_len, KV_HEADS, HEAD_DIM).transpose(0, 2, 1, 3)
        v = (kv @ Wv).reshape(bsz, kv_len, KV_HEADS, HEAD_DIM).transpose(0, 2, 1, 3)
        q = rms_norm(q, q_norm_w)
        k = rms_norm(k, k_norm_w)
        qg = q.reshape(bsz, KV_HEADS, groups, q_len, HEAD_DIM)
        scale = 1.0 / np.sqrt(HEAD_DIM)
        scores = jnp.einsum('bhgqd,bhkd->bhgqk', qg, k) * scale
        probs = jax.nn.softmax(scores.astype(jnp.float32), axis=-1).astype(q.dtype)
        out = jnp.einsum('bhgqk,bhkd->bhgqd', probs, v)
        out = out.reshape(bsz, HEADS, q_len, HEAD_DIM).transpose(0, 2, 1, 3)
        out = out.reshape(bsz, q_len, HEADS * HEAD_DIM)
        return out @ Wo

    def _L1_ffn_ref(hidden_states, W, b, A, B, gate_w, gate_b):
        import jax, jax.numpy as jnp
        import numpy as np
        RANKS = (8, 16, 32, 64)
        TOPK = 1
        SCALING = 1.0 / 4
        bsz, seq, d_in = hidden_states.shape
        out = jnp.einsum('bsd,od->bso', hidden_states, W) + b
        x = hidden_states.reshape(-1, d_in)
        scores = x @ gate_w.T + gate_b
        probs = jax.nn.softmax(scores, axis=-1)
        routing_weights, selected = jax.lax.top_k(probs, TOPK)
        routing_weights = routing_weights / jnp.sum(routing_weights, axis=-1, keepdims=True)
        lora_outputs = jnp.stack([x @ A[:r, :].T @ B[:, :r].T for r in RANKS], axis=1)
        sel = jnp.take_along_axis(lora_outputs, selected[:, :, None], axis=1)
        final = jnp.sum(sel * routing_weights[:, :, None], axis=1)
        return out + final.reshape(bsz, seq, -1)

    def _L2_xattn_ref(query, key, value, mask, Wq, Wk, Wv, Wo):
        import jax, jax.numpy as jnp
        import numpy as np
        B, T, D_MODEL = (1, 256, 512)
        NUM_Q_HEADS, NUM_KV_HEADS, KEY_SIZE = (32, 8, 128)
        ATTN_MULT = 0.08838834764831845
        MAX_ATTN_VAL = 30.0

        def rotate_half(x):
            x1, x2 = jnp.split(x, 2, axis=-1)
            return jnp.concatenate((-x2, x1), axis=-1)

        def apply_rope(x):
            b, t, h, d = x.shape
            exponents = jnp.arange(0, d, 2, dtype=jnp.float32)
            inv_freq = 1.0 / 10000.0 ** (exponents / d)
            pos = jnp.arange(t, dtype=jnp.float32)
            phase = pos[:, None] * inv_freq[None, :]
            phase = jnp.tile(phase, (1, 2))[None, :, None, :]
            return (x * jnp.cos(phase) + rotate_half(x) * jnp.sin(phase)).astype(x.dtype)
        b, t, _ = query.shape
        d = KEY_SIZE
        h, kv_h = (NUM_Q_HEADS, NUM_KV_HEADS)
        g = h // kv_h
        q = (query @ Wq).reshape(b, t, h, d)
        k = (key @ Wk).reshape(b, t, kv_h, d)
        v = (value @ Wv).reshape(b, t, kv_h, d)
        q = apply_rope(q)
        k = apply_rope(k)
        q = q.reshape(b, t, kv_h, g, d)
        logits = jnp.einsum('btkgd,bTkd->bkgtT', q, k).astype(jnp.float32)
        logits = logits * ATTN_MULT
        logits = MAX_ATTN_VAL * jnp.tanh(logits / MAX_ATTN_VAL)
        m = mask[:, :, None, :, :]
        logits = jnp.where(m, logits, -1e+30)
        weights = jax.nn.softmax(logits, axis=-1).astype(query.dtype)
        attn = jnp.einsum('bkgtT,bTkd->btkgd', weights, v)
        attn = attn.reshape(b, t, h * d)
        return attn @ Wo

    def _L2_ffn_ref(x, W_gate, W_up, W_down):
        import jax, jax.numpy as jnp
        import numpy as np
        D_MODEL = 512
        D_FF = 1376
        out_shape = x.shape[:-1] + (W_down.shape[0],)
        xf = x.reshape(-1, x.shape[-1])
        up = jnp.einsum('td,fd->tf', xf, W_up)
        gate = jax.nn.silu(jnp.einsum('td,fd->tf', xf, W_gate))
        h = gate * up
        y = jnp.einsum('tf,df->td', h, W_down)
        return y.reshape(out_shape)

    def _L3_xattn_ref(q, k, v):
        import jax, jax.numpy as jnp
        import numpy as np
        EMB_DIM = 64
        HEADS = 8
        B, C, N = q.shape
        H = HEADS
        dh = C // H
        qh = q.transpose(0, 2, 1).reshape(B, N, H, dh)
        kh = k.transpose(0, 2, 1).reshape(B, N, H, dh)
        vh = v.transpose(0, 2, 1).reshape(B, N, H, dh)
        qh = jax.nn.softmax(qh, axis=3)
        kh = jax.nn.softmax(kh, axis=1)
        kvs = jnp.einsum('bnhd,bnhe->bhde', kh, vh)
        out = jnp.einsum('bnhd,bhde->bnhe', qh, kvs)
        return out.transpose(0, 2, 3, 1).reshape(B, C, N)

    def _L3_ffn_ref(x, gate_w, gate_z, gate_s, up_w, up_z, up_s, down_w, down_z, down_s):
        import jax, jax.numpy as jnp
        import numpy as np
        GROUP_SIZE = 128

        def dequantize(imatrix, scales, zeros, group_size, out_dtype):
            rs = jnp.repeat(scales, group_size, axis=0)
            rz = jnp.repeat(zeros, group_size, axis=0)
            return ((imatrix.astype(rs.dtype) - rz.astype(rs.dtype)) * rs).astype(out_dtype)
        dt = x.dtype
        gate_proj = dequantize(gate_w, gate_s, gate_z, GROUP_SIZE, dt)
        up_proj = dequantize(up_w, up_s, up_z, GROUP_SIZE, dt)
        down_proj = dequantize(down_w, down_s, down_z, GROUP_SIZE, dt)
        gate = jax.nn.silu(jnp.dot(x, gate_proj))
        up = jnp.dot(x, up_proj)
        return jnp.dot(gate * up, down_proj)
    x = x + _L0_xattn_ref(ctx_4096, _layernorm(x, axis=-1), ctx_4096)
    x = x + _L0_ffn_ref(_layernorm(x, axis=-1), L0_ffn_weight, L0_ffn_bias, L0_ffn_centroids, L0_ffn_assignments)
    x = x + _L1_xattn_ref(_layernorm(x, axis=-1), ctx_4096, L1_xattn_Wq, L1_xattn_Wk, L1_xattn_Wv, L1_xattn_Wo, L1_xattn_q_norm_w, L1_xattn_k_norm_w)
    x = x + _L1_ffn_ref(_layernorm(x, axis=-1), L1_ffn_W, L1_ffn_b, L1_ffn_A, L1_ffn_B, L1_ffn_gate_w, L1_ffn_gate_b)
    x = x + _L2_xattn_ref(_layernorm(x, axis=-1), ctx_4096, ctx_4096, mask_1x1xSxS2_bk0, L2_xattn_Wq, L2_xattn_Wk, L2_xattn_Wv, L2_xattn_Wo)
    x = x + _L2_ffn_ref(_layernorm(x, axis=-1), L2_ffn_W_gate, L2_ffn_W_up, L2_ffn_W_down)
    x = x + _L3_xattn_ref(_layernorm(x, axis=-1), ctx_4096, ctx_4096)
    x = x + _L3_ffn_ref(_layernorm(x, axis=-1), L3_ffn_gate_w, L3_ffn_gate_z, L3_ffn_gate_s, L3_ffn_up_w, L3_ffn_up_z, L3_ffn_up_s, L3_ffn_down_w, L3_ffn_down_z, L3_ffn_down_s)
    return x

_drawn_inputs = setup_inputs


def setup_inputs(seed=0):
    import zlib

    import numpy as np

    out = dict(_drawn_inputs(seed))
    spreads = {'L1_xattn_q_norm_w': (1.0, 0.6), 'L1_xattn_k_norm_w': (1.0, 0.6)}
    factors = {'L0_ffn_bias': 3.775,
     'L1_ffn_b': 5.157,
     'L1_ffn_gate_w': 3.318,
     'L1_ffn_gate_b': 8.0,
     'L2_xattn_Wq': 3.035,
     'L2_xattn_Wk': 3.044}
    for name, (base, spread) in spreads.items():
        noise = np.random.default_rng([zlib.crc32(name.encode()), seed]).standard_normal(out[name].shape)
        drawn = base * np.exp(spread * noise) if base else spread * noise
        out[name] = jnp.asarray(drawn.astype(out[name].dtype))
    for name, factor in factors.items():
        out[name] = (out[name] * factor).astype(out[name].dtype)
    return out
```

```python
from contextlib import ExitStack

import numpy as np

import concourse.bass as bass
from concourse import mybir

F32 = mybir.dt.float32
F32R = mybir.dt.float32r
I32 = mybir.dt.int32
ALU = mybir.AluOpType
ACT = mybir.ActivationFunctionType
AX = mybir.AxisListType

P = 128
B, C, N = 16, 64, 512
D = N
KT = D // P
T = B * C
NT = T // P
EPS_LN = 1e-5
MAGIC = 0x5F3759DF


class Phase:

    def __init__(self):
        nothing = lambda eng: None
        self.sync = self.scalar = self.vector = self.gpsimd = self.tensor = nothing


class Order:

    def __init__(self, eng, sem):
        self.eng, self.sem, self.count, self.turn = eng, sem, 0, 0

    def wait(self):
        self.eng.wait_ge(self.sem, self.turn + self.count)

    def done(self, ins):
        ins.then_inc(self.sem, 1)
        self.count += 1

    def link(self, ins):
        self.done(ins)
        self.wait()

    def loop(self, i, per):
        self.before, self.per = self.count, per
        self.turn = i * per

    def end(self, turns):
        assert self.count - self.before == self.per, (self.count - self.before, self.per)
        self.count = self.before + turns * self.per
        self.turn = 0


def rsqrt(ve, order, y, v, bits, half, t):
    order.link(ve.tensor_scalar(bits, v.bitcast(I32), 1, None, ALU.logical_shift_right))
    order.link(ve.tensor_scalar(y.bitcast(I32), bits, -1.0, float(MAGIC), ALU.mult, ALU.add))
    order.link(ve.tensor_scalar(half, v, -0.5, None, ALU.mult))
    for _ in range(3):
        order.link(ve.tensor_tensor(t, y, y, ALU.mult))
        order.link(ve.tensor_tensor(t, t, half, ALU.mult))
        order.link(ve.scalar_tensor_tensor(y, t, 1.5, y, ALU.add, ALU.mult))


RSQRT_LINKS = 12


def products(pe, out, lhs, rhs, first=True, last=True):
    pe.matmul(out, lhs[0], rhs[0], start=first, stop=False)
    pe.matmul(out, lhs[0], rhs[1], start=False, stop=False)
    return pe.matmul(out, lhs[1], rhs[0], start=False, stop=last)


def tile_stats(ve, order, m, t):
    order.done(ve.bn_stats(m.stats[:, bass.ds(t, 1), :].rearrange("p o s -> p (o s)"),
                           m.x[:, bass.ds(t, 1), :].rearrange("p o n -> p (o n)")))


def finish_stats(ve, order, m, ready):
    order.wait()
    for t in range(NT):
        order.done(ve.bn_aggr(m.mean_var[:, t, :], m.stats[:, t, :]))
    order.wait()
    order.link(ve.tensor_scalar(m.var[:], m.mean_var[:, :, 1], EPS_LN, None, ALU.add))
    rsqrt(ve, order, m.rstd[:], m.var[:], m.bits[:, 0:NT], m.half[:, 0:NT], m.tmp[:, 0:NT])
    ve.tensor_copy(m.mean[:], m.mean_var[:, :, 0]).then_inc(ready, 1)
    ve.wait_ge(ready, 1)


def normalise(eng, m, out, t):
    return eng.tensor_scalar(out, m.x[:, t, :], m.mean[:, t:t + 1], m.rstd[:, t:t + 1], ALU.subtract, ALU.mult)


def context_attention(m):
    ph, nc = Phase(), m.nc
    SCALE = 1.0 / 8.0
    BODY = 2
    TURNS = NT // BODY
    STEPS = BODY * 2 * KT
    NB = BODY * 2
    xn = m.sb("l0_xn", [P, 2, D])
    xn_s = [m.sb(f"l0_xn_{h}", [P, 2, D], F32R) for h in ("high", "low")]
    ctx_raw = m.sb("l0_ctx_raw", [P, 2, D])
    ctx_s = [m.sb(f"l0_ctx_{h}", [P, 2, D], F32R) for h in ("high", "low")]
    ctxT_raw = m.sb("l0_ctxT_raw", [P, KT, T])
    val_s = [m.sb(f"l0_val_{h}", [P, 2, KT, P], F32R) for h in ("high", "low")]
    prob = m.sb("l0_prob", [P, 4, D])
    probT_s = [m.sb(f"l0_probT_{h}", [P, 2, KT, D], F32R) for h in ("high", "low")]
    mx, nbias, total, rtotal = (m.sb(f"l0_{n}", [P, STEPS]) for n in ("max", "nbias", "total", "rtotal"))
    score_ps, probT_ps, out_ps = m.ps[0:4], m.ps[4:6], m.ps[6:8]

    s_x, s_ctxT = m.layer_sem("l0_x_loaded"), m.layer_sem("l0_ctxT_loaded")
    s_ctx = [m.layer_sem(f"l0_ctx_loaded_{u}") for u in range(BODY)]
    s_xn, s_high, s_low = m.layer_sem("l0_xn_done"), m.layer_sem("l0_high_parts"), m.layer_sem("l0_low_parts")
    s_score, s_nbias, s_exp, s_rt = m.layer_sem("l0_scores"), m.layer_sem("l0_nbias"), m.layer_sem("l0_exp"), m.layer_sem("l0_rtotal")
    s_prob, s_probT, s_hi, s_lo = m.layer_sem("l0_probs"), m.layer_sem("l0_probT"), m.layer_sem("l0_probT_high"), m.layer_sem("l0_probT_low")
    s_out, s_add = m.layer_sem("l0_out"), m.layer_sem("l0_added")
    s_ord, s_ln, s_kv = m.layer_sem("l0_dve_order"), m.layer_sem("l0_stats_ready"), m.s_kv_ctx
    m.kv_ctx_all = 2 * NT

    def sync(sp):
        sp.dma_start(m.x[:, :, :], m.d["x"].rearrange("(t p) n -> p t n", p=P)).then_inc(s_x, 16)
        sp.dma_start(m.ident[:, :], m.d["ident"]).then_inc(m.s_ident, 16)
        sp.dma_start(ctxT_raw[:, :, :], m.d["ctxT"].rearrange("(k p) t -> p k t", p=P)).then_inc(s_ctxT, 16)
        ctx_d = m.d["ctx"].rearrange("(t p) n -> p t n", p=P)
        with sp.Fori(0, TURNS) as i:
            for u in range(BODY):
                sp.wait_ge(s_low, i * BODY + u + 1)
                sp.dma_start(ctx_raw[:, u, :], ctx_d[:, bass.ds(i * BODY + u, 1), :].rearrange("p o n -> p (o n)")).then_inc(s_ctx[u], 16)
    ph.sync = sync

    def scalar(act):
        with act.Fori(0, TURNS) as i:
            def operands(u):
                act.wait_ge(s_ctx[u], (i + 1) * 16)
                act.activation(ctx_s[0][:, u, :], ctx_raw[:, u, :], ACT.Copy)
                act.wait_ge(s_xn, i * BODY + u + 1)
                act.activation(xn_s[0][:, u, :], xn[:, u, :], ACT.Copy)
                act.wait_ge(s_ctxT, 16)
                act.activation(val_s[0][:, u, :, :], ctxT_raw[:, :, bass.ds((i * BODY + u) * P, P)], ACT.Copy).then_inc(s_high, 1)
            act.wait_ge(s_out, i * NB + 1)
            for u in range(BODY):
                operands(u)
            for j in range(STEPS + 2):
                if j < STEPS:
                    act.wait_ge(s_nbias, i * STEPS + j + 1)
                    if j >= 4:
                        act.wait_ge(s_probT, i * STEPS + j - 3)
                    act.activation(prob[:, j % 4, :], score_ps[j % 4][:, :], ACT.Exp, bias=nbias[:, j:j + 1],
                                   scale=SCALE, accum_out=total[:, j:j + 1]).then_inc(s_exp, 1)
                if j >= 2:
                    k = j - 2
                    act.wait_ge(s_probT, i * STEPS + k + 1)
                    if k >= 8:
                        act.wait_ge(s_out, i * NB + k // 4)
                    act.activation(probT_s[0][:, (k // 4) % 2, :, (k % 4) * P:(k % 4 + 1) * P],
                                   probT_ps[k % 2][:, :].rearrange("p (k n) -> p k n", k=KT), ACT.Copy).then_inc(s_hi, 1)
    ph.scalar = scalar

    def gpsimd(pool):
        pool.sem_inc(s_low, BODY)
        with pool.Fori(0, TURNS) as i:
            for u in range(BODY):
                pool.wait_ge(s_high, i * BODY + u + 1)
                pool.tensor_tensor(ctx_s[1][:, u, :], ctx_raw[:, u, :], ctx_s[0][:, u, :].bitcast(F32), ALU.subtract)
                pool.tensor_tensor(xn_s[1][:, u, :], xn[:, u, :], xn_s[0][:, u, :].bitcast(F32), ALU.subtract)
                pool.tensor_tensor(val_s[1][:, u, :, :], ctxT_raw[:, :, bass.ds((i * BODY + u) * P, P)],
                                   val_s[0][:, u, :, :].bitcast(F32), ALU.subtract).then_inc(s_low, 1)
            for j in range(STEPS):
                pool.wait_ge(s_rt, i * STEPS + j + 1)
                pool.tensor_tensor(prob[:, j % 4, :], prob[:, j % 4, :], rtotal[:, j:j + 1].to_broadcast([P, D]), ALU.mult).then_inc(s_prob, 1)
                if j == 0:
                    for u in range(BODY):
                        for h in range(2):
                            if h == 1:
                                pool.wait_ge(s_low, BODY + i * BODY + u + 1)
                            pool.tensor_copy(m.kvT[h][:, :, bass.ds((i * BODY + u) * P, P), 0],
                                             val_s[h][:, u, :, :].bitcast(F32)).then_inc(s_kv, 1)
    ph.gpsimd = gpsimd

    def vector(ve):
        order = Order(ve, s_ord)
        ve.wait_ge(s_x, 16)
        for t in range(NT):
            order.done(ve.bn_stats(m.stats[:, t, :], m.x[:, t, :]))
        finish_stats(ve, order, m, s_ln)
        with ve.Fori(0, TURNS) as i:
            order.loop(i, STEPS + NB)
            for u in range(BODY):
                t = i * BODY + u
                ve.wait_ge(s_low, i * BODY + u + 1)
                ve.tensor_scalar(xn[:, u, :], m.x[:, bass.ds(t, 1), :].rearrange("p o n -> p (o n)"),
                                 m.mean[:, bass.ds(t, 1)], m.rstd[:, bass.ds(t, 1)],
                                 ALU.subtract, ALU.mult).then_inc(s_xn, 1)
            for j in range(STEPS + 5):
                if j < STEPS:
                    ve.wait_ge(s_score, i * STEPS + j + 1)
                    order.link(ve.tensor_reduce(mx[:, j:j + 1], score_ps[j % 4][:, :], AX.X, ALU.max))
                    ve.tensor_scalar(nbias[:, j:j + 1], mx[:, j:j + 1], -SCALE, None, ALU.mult).then_inc(s_nbias, 1)
                if 1 <= j <= STEPS:
                    ve.wait_ge(s_exp, i * STEPS + j)
                    ve.reciprocal(rtotal[:, j - 1:j], total[:, j - 1:j]).then_inc(s_rt, 1)
                if 3 <= j < STEPS + 3:
                    k = j - 3
                    ve.wait_ge(s_hi, i * STEPS + k + 1)
                    ve.tensor_tensor(probT_s[1][:, (k // 4) % 2, :, (k % 4) * P:(k % 4 + 1) * P],
                                     probT_ps[k % 2][:, :].rearrange("p (k n) -> p k n", k=KT),
                                     probT_s[0][:, (k // 4) % 2, :, (k % 4) * P:(k % 4 + 1) * P].bitcast(F32),
                                     ALU.subtract).then_inc(s_lo, 1)
                if j >= 8 and j % 4 == 0:
                    b = j // 4 - 2
                    rows = slice((b % 2) * C, (b % 2 + 1) * C)
                    t = i * BODY + b // 2
                    xt = m.x[rows, bass.ds(t, 1), :].rearrange("p o n -> p (o n)")
                    ve.wait_ge(s_out, i * NB + b + 2)
                    ve.tensor_tensor(xt, out_ps[b % 2][rows, :], xt, ALU.add).then_inc(s_add, 1)
                    ve.wait_ge(s_add, i * NB + b + 1)
                    order.done(ve.bn_stats(m.stats[rows, bass.ds(t, 1), :].rearrange("p o s -> p (o s)"), xt))
            order.end(TURNS)
        finish_stats(ve, order, m, m.s_ln[1])
    ph.vector = vector

    def tensor(pe):
        pe.wait_ge(m.s_ident, 16)
        pe.sem_inc(s_out, 1)
        with pe.Fori(0, TURNS) as i:
            def scores(j):
                b, r = j // 4, j % 4
                u, rows = b // 2, slice((b % 2) * C, (b % 2 + 1) * C)
                if j % 8 == 0:
                    pe.wait_ge(s_low, BODY + i * BODY + u + 1)
                if j >= 4:
                    pe.wait_ge(s_exp, i * STEPS + j - 3)
                products(pe, score_ps[j % 4][:, :], [c[rows, u, r * P:(r + 1) * P] for c in ctx_s],
                         [a[rows, u, :] for a in xn_s]).then_inc(s_score, 1)

            def transposes(j):
                pe.wait_ge(s_prob, i * STEPS + j + 1)
                if j >= 2:
                    pe.wait_ge(s_lo, i * STEPS + j - 1)
                for k in range(KT):
                    last = pe.transpose(probT_ps[j % 2][:, k * P:(k + 1) * P], prob[:, j % 4, k * P:(k + 1) * P], m.ident[:, :])
                last.then_inc(s_probT, 1)

            def values(b):
                pe.wait_ge(s_lo, i * STEPS + 4 * b + 4)
                if b >= 2:
                    pe.wait_ge(s_add, i * NB + b - 1)
                for k in range(KT):
                    last = products(pe, out_ps[b % 2][:, :], [v[:, b // 2, k, :] for v in val_s],
                                    [p[:, b % 2, k, :] for p in probT_s], first=(k == 0), last=(k == KT - 1))
                last.then_inc(s_out, 1)

            for j in range(3):
                scores(j)
            for j in range(STEPS):
                if j + 3 < STEPS:
                    scores(j + 3)
                transposes(j)
                if j % 4 == 0 and j:
                    values(j // 4 - 1)
            values(NB - 1)
    ph.tensor = tensor
    return ph


class TileFeed:

    def __init__(self, m, name, layer):
        self.m, self.layer = m, layer
        self.xn = m.sb(f"{name}_xn", [P, 2, D])
        self.xT = [m.sb(f"{name}_xT_{h}", [P, 2, KT, P], F32R) for h in ("high", "low")]
        self.ps = m.ps[0:2]
        self.s_xn, self.s_T = m.layer_sem(f"{name}_xn"), m.layer_sem(f"{name}_xn_turned")
        self.s_hi, self.s_lo = m.layer_sem(f"{name}_xT_high"), m.layer_sem(f"{name}_xT_low")
        self.s_used = m.layer_sem(f"{name}_xT_used")

    def normalise(self, ve, i, u):
        t = i * 2 + u
        ve.tensor_scalar(self.xn[:, u, :], self.m.x[:, bass.ds(t, 1), :].rearrange("p o n -> p (o n)"),
                         self.m.mean[:, bass.ds(t, 1)], self.m.rstd[:, bass.ds(t, 1)],
                         ALU.subtract, ALU.mult).then_inc(self.s_xn, 1)

    def low(self, ve, i, u):
        ve.wait_ge(self.s_hi, i * 2 + u + 1)
        ve.tensor_tensor(self.xT[1][:, u, :, :], self.ps[u][:, :].rearrange("p (k n) -> p k n", k=KT),
                         self.xT[0][:, u, :, :].bitcast(F32), ALU.subtract).then_inc(self.s_lo, 1)

    def high(self, act, i, u):
        act.wait_ge(self.s_T, i * 2 + u + 1)
        act.wait_ge(self.s_used, i * 2 + u + 1)
        act.activation(self.xT[0][:, u, :, :], self.ps[u][:, :].rearrange("p (k n) -> p k n", k=KT),
                       ACT.Copy).then_inc(self.s_hi, 1)

    def turn(self, pe, i, u):
        pe.wait_ge(self.s_xn, i * 2 + u + 1)
        for k in range(KT):
            last = pe.transpose(self.ps[u][:, k * P:(k + 1) * P], self.xn[:, u, k * P:(k + 1) * P], self.m.ident[:, :])
        last.then_inc(self.s_T, 1)


def clustered_linear(m):
    ph = Phase()
    NC, THRESHOLD, SHARPNESS = 64, 0.01, 10.0
    feed = TileFeed(m, "c0", 0)
    raw = m.raw[:, 0:KT * D].rearrange("p (k n) -> p k n", k=KT)
    rawc = m.raw[:, KT * D:KT * (D + NC)].rearrange("p (k n) -> p k n", k=KT)
    w = [m.sb(f"c0_w_{h}", [P, KT, D], F32R) for h in ("high", "low")]
    cen = [m.sb(f"c0_centroids_{h}", [P, KT, NC], F32R) for h in ("high", "low")]
    brow = m.sb("c0_bias_row", [1, D])
    bias = [m.sb(f"c0_bias_{h}", [1, D], F32R) for h in ("high", "low")]
    dense = m.sb("c0_dense", [P, NT, D])
    dots = m.sb("c0_dots", [P, NT, NC])
    prob = m.sb("c0_prob", [P, NT, NC])
    mx, tot, qsel = (m.sb(f"c0_{n}", [P, NT]) for n in ("max", "total", "row_hit"))
    owner = m.sb("c0_owner", [NC, D], I32)
    ownerf = m.sb("c0_owner_f", [NC, D])
    mine = m.sb("c0_partition", [NC, 1], I32)
    minef = m.sb("c0_partition_f", [NC, 1])
    onehot = m.sb("c0_onehot", [NC, D])
    chit = m.sb("c0_cluster_hit", [NC, 1])
    chitb = m.sb("c0_cluster_hit_wide", [NC, P])
    colsel = m.sb("c0_column_hit", [P, D])
    dot_ps, dense_ps, count_ps, col_ps = m.ps[2:4], m.ps[4:6], m.ps[6], m.ps[7]
    s_w, s_small, s_split, s_iota = m.layer_sem("c0_w_loaded"), m.layer_sem("c0_small_loaded"), m.layer_sem("c0_split"), m.layer_sem("c0_iota")
    s_dots, s_dotc, s_dense, s_densec = m.layer_sem("c0_dots_ready"), m.layer_sem("c0_dots_out"), m.layer_sem("c0_dense_ready"), m.layer_sem("c0_dense_out")
    s_ord, s_shift, s_exp, s_hits = m.layer_sem("c0_dve_order"), m.layer_sem("c0_shifted"), m.layer_sem("c0_exp"), m.layer_sem("c0_hits")
    s_count, s_chit, s_col, s_colc, s_add = m.layer_sem("c0_count"), m.layer_sem("c0_chit"), m.layer_sem("c0_col"), m.layer_sem("c0_col_out"), m.layer_sem("c0_added")
    m.s_raw_free[1] = s_split

    def sync(sp):
        sp.dma_start(raw, m.d["c0_w"].rearrange("(k p) n -> p k n", p=P)).then_inc(s_w, 16)
        sp.dma_start(rawc, m.d["c0_centroids"].rearrange("(k p) n -> p k n", p=P)).then_inc(s_w, 16)
        sp.wait_ge(m.s_ln[1], 1)
        sp.dma_start(brow[:, :], m.d["c0_bias"]).then_inc(s_small, 16)
        sp.dma_start(owner[:, :], m.d["c0_owner"].to_broadcast([NC, D])).then_inc(s_small, 16)
    ph.sync = sync

    def gpsimd(pool):
        pool.wait_ge(m.s_ln[1], 1)
        pool.iota(mine[:, :], [[0, 1]], base=0, channel_multiplier=1).then_inc(s_iota, 1)
        pool.wait_ge(s_w, 32)
        pool.tensor_copy(w[0][:, :, :], raw).then_inc(s_split, 1)
        pool.tensor_copy(cen[0][:, :, :], rawc).then_inc(s_split, 1)
        pool.wait_ge(s_split, 2)
        pool.tensor_tensor(w[1][:, :, :], raw, w[0][:, :, :].bitcast(F32), ALU.subtract).then_inc(s_split, 1)
        pool.tensor_tensor(cen[1][:, :, :], rawc, cen[0][:, :, :].bitcast(F32), ALU.subtract).then_inc(s_split, 1)
        pool.wait_ge(s_small, 32)
        pool.tensor_copy(bias[0][:, :], brow[:, :]).then_inc(s_split, 1)
        pool.wait_ge(s_split, 5)
        pool.tensor_tensor(bias[1][:, :], brow[:, :], bias[0][:, :].bitcast(F32), ALU.subtract).then_inc(s_split, 1)
        pool.tensor_copy(ownerf[:, :], owner[:, :]).then_inc(s_split, 1)
    ph.gpsimd = gpsimd

    def scalar(act):
        with act.Fori(0, NT // 2) as i:
            for u in range(2):
                feed.high(act, i, u)
            for u in range(2):
                act.wait_ge(s_dense, i * 2 + u + 1)
                act.activation(dense[:, bass.ds(i * 2 + u, 1), :].rearrange("p o n -> p (o n)"), dense_ps[u][:, :], ACT.Copy).then_inc(s_densec, 1)
        act.wait_ge(s_shift, 1)
        act.activation(prob[:, :, :], prob[:, :, :], ACT.Exp, scale=SHARPNESS).then_inc(s_exp, 1)
        act.wait_ge(s_col, 1)
        act.activation(colsel[:, :], col_ps[:, :], ACT.Copy).then_inc(s_colc, 1)
    ph.scalar = scalar

    def vector(ve):
        order = Order(ve, s_ord)
        wide = lambda a: a[:, :].unsqueeze(2).broadcast_to([P, NT, NC])
        with ve.Fori(0, NT // 2) as i:
            order.loop(i, 0)
            for u in range(2):
                feed.normalise(ve, i, u)
            for u in range(2):
                feed.low(ve, i, u)
            for u in range(2):
                ve.wait_ge(s_dots, i * 2 + u + 1)
                ve.tensor_copy(dots[:, bass.ds(i * 2 + u, 1), :].rearrange("p o n -> p (o n)"), dot_ps[u][:, 0:NC]).then_inc(s_dotc, 1)
            order.end(NT // 2)
        ve.wait_ge(s_dotc, NT)
        order.link(ve.tensor_reduce(mx[:, :], dots[:, :, :], AX.X, ALU.max))
        ve.tensor_tensor(prob[:, :, :], dots[:, :, :], wide(mx), ALU.subtract).then_inc(s_shift, 1)
        ve.wait_ge(s_exp, 1)
        order.link(ve.tensor_reduce(tot[:, :], prob[:, :, :], AX.X, ALU.add))
        order.link(ve.reciprocal(mx[:, :], tot[:, :]))
        order.link(ve.tensor_tensor(prob[:, :, :], prob[:, :, :], wide(mx), ALU.mult))
        ve.tensor_scalar(prob[:, :, :], prob[:, :, :], THRESHOLD, None, ALU.is_gt).then_inc(s_hits, 1)
        ve.wait_ge(s_hits, 1)
        order.link(ve.tensor_reduce(qsel[:, :], prob[:, :, :], AX.X, ALU.max))
        ve.wait_ge(s_iota, 1)
        ve.wait_ge(s_split, 7)
        order.link(ve.tensor_copy(minef[:, :], mine[:, :]))
        ve.tensor_scalar(onehot[:, :], ownerf[:, :], minef[:, 0:1], None, ALU.is_equal).then_inc(s_chit, 1)
        ve.wait_ge(s_count, 1)
        order.link(ve.tensor_scalar(chit[:, :], count_ps[0:NC, 0:1], 0.5, None, ALU.is_gt))
        ve.tensor_copy(chitb[:, :], chit[:, 0:1].to_broadcast([NC, P])).then_inc(s_chit, 1)
        ve.wait_ge(s_colc, 1)
        ve.wait_ge(s_densec, NT)
        with ve.Fori(0, NT) as i:
            order.loop(i, 2)
            y = dense[:, bass.ds(i, 1), :].rearrange("p o n -> p (o n)")
            xt = m.x[:, bass.ds(i, 1), :].rearrange("p o n -> p (o n)")
            order.link(ve.scalar_tensor_tensor(y, y, qsel[:, bass.ds(i, 1)], colsel[:, :], ALU.mult, ALU.mult))
            ve.tensor_tensor(xt, xt, y, ALU.add).then_inc(s_add, 1)
            ve.wait_ge(s_add, i + 1)
            tile_stats(ve, order, m, i)
            order.end(NT)
        finish_stats(ve, order, m, m.s_ln[2])
    ph.vector = vector

    def tensor(pe):
        pe.sem_inc(feed.s_used, 2)
        pe.wait_ge(s_split, 6)
        with pe.Fori(0, NT // 2) as i:
            for u in range(2):
                feed.turn(pe, i, u)
            for u in range(2):
                pe.wait_ge(feed.s_lo, i * 2 + u + 1)
                for k in range(KT):
                    last = products(pe, dot_ps[u][:, 0:NC], [a[:, u, k, :] for a in feed.xT], [c[:, k, :] for c in cen],
                                    first=(k == 0), last=(k == KT - 1))
                last.then_inc(s_dots, 1)
                for k in range(KT):
                    products(pe, dense_ps[u][:, :], [a[:, u, k, :] for a in feed.xT], [c[:, k, :] for c in w],
                             first=(k == 0), last=False)
                pe.matmul(dense_ps[u][:, :], m.ones_row[:, :], bias[0][:, :], start=False, stop=False)
                pe.matmul(dense_ps[u][:, :], m.ones_row[:, :], bias[1][:, :], start=False, stop=True).then_inc(s_dense, 1)
                pe.wait_ge(s_dense, i * 2 + u + 1)
                pe.sem_inc(feed.s_used, 1)
        pe.wait_ge(s_hits, 1)
        for t in range(NT):
            last = pe.matmul(count_ps[0:NC, 0:1], prob[:, t, :], m.ones_col[:, :], start=(t == 0), stop=(t == NT - 1))
        last.then_inc(s_count, 1)
        pe.wait_ge(s_chit, 2)
        pe.matmul(col_ps[:, :], chitb[:, :], onehot[:, :], start=True, stop=True).then_inc(s_col, 1)
    ph.tensor = tensor
    return ph


def attention(m, rotary, n, layer):
    ph = Phase()
    G, HD, HG, KV = 8, 128, 4, 256
    STEPS = NT
    HB = B // 2
    KW = 64 if rotary else 128
    EPS, ROOT = 1e-6, float(HD) ** -0.5
    MULT, CAP = 0.08838834764831845, 30.0

    q = [m.sb(f"{n}_q_{h}", [P, 2, HB, 2, P], F32R) for h in ("high", "low")]
    if rotary:
        qa, qb = (m.sb(f"{n}_q_{h}", [P, 2, HB * C]) for h in ("cos", "sin"))
        xn = qa
    else:
        qsq = m.sb(f"{n}_q_squared", [P, 2, HB, 2, P])
        xn = qsq[:, 0, 0:4, :, :].rearrange("p b h r -> p (b h r)").rearrange("p (u n) -> p u n", u=2)
    wq = [m.sb(f"{n}_wq_{h}", [P, KT, HG * HD], F32R) for h in ("high", "low")]
    wkv = [m.sb(f"{n}_wkv_{h}", [P, KT, KV], F32R) for h in ("high", "low")]
    wo = [m.sb(f"{n}_wo_{h}", [P, HG, D], F32R) for h in ("high", "low")]
    kn = m.sb(f"{n}_k", [P, 2, HD])
    kT = [m.sb(f"{n}_kT_{h}", [P, 2, P], F32R) for h in ("high", "low")]
    v = [m.sb(f"{n}_v_{h}", [P, 2, 2, HD], F32R) for h in ("high", "low")]
    prob = m.sb(f"{n}_prob", [P, 4, KW])
    pT = [m.sb(f"{n}_probT_{h}", [P, 512], F32R) for h in ("high", "low")]
    o = [m.sb(f"{n}_heads_{h}", [P, HG, 2, C], F32R) for h in ("high", "low")]
    vark, rk, halfk, tmpk = (m.sb(f"{n}_k_{h}", [P, 2]) for h in ("var", "rms", "half", "tmp"))
    varq, rq, halfq, tmpq = (m.sb(f"{n}_q_{h}", [P, 4]) for h in ("var", "rms", "half", "tmp"))
    mx, nb, tot, rt = (m.sb(f"{n}_{h}", [P, 4]) for h in ("max", "nbias", "total", "rtotal"))
    q_ps, kv_ps, kT_ps, s_ps, pT_ps, o_ps, y_ps = m.ps[0:2], m.ps[2], m.ps[3], m.ps[4], m.ps[5], m.ps[6], m.ps[7]

    raw_wq = m.raw[:, 0:2048].rearrange("p (k n) -> p k n", k=KT)
    raw_wkv = m.raw[:, 2048:3072].rearrange("p (k n) -> p k n", k=KT)
    raw_wo = m.raw[:, 3072:5120].rearrange("p (k n) -> p k n", k=HG)

    S = lambda h: m.layer_sem(f"{n}_{h}")
    l_wq, l_wkv, l_wo = S("wq_loaded"), S("wkv_loaded"), S("wo_loaded")
    t_wq, t_wkv, t_wo = S("wq_split"), S("wkv_split"), S("wo_split")
    s_xn, s_xT, s_xh, s_xl = S("xn"), S("xn_turned"), S("xT_high"), S("xT_low")
    s_q, s_qh, s_qsq, s_ql = S("q"), S("q_high"), S("q_squared"), S("q_low")
    s_kv, s_kss, s_kn, s_vh, s_vl = S("kv"), S("k_sums"), S("k_normed"), S("v_high"), S("v_low")
    s_kt, s_kth, s_ktl, s_rq = S("kT"), S("kT_high"), S("kT_low"), S("q_rms")
    s_s, s_nb, s_e, s_rt, s_pn = S("scores"), S("nbias"), S("exp"), S("rtotal"), S("probs")
    s_pt, s_pth, s_ptl = S("probT"), S("probT_high"), S("probT_low")
    s_pv, s_pv0, s_oh, s_ol, s_wo, s_add = S("heads"), S("heads_first_batch"), S("heads_high"), S("heads_low"), S("projected"), S("added")
    s_ord = S("dve_order")
    s_th, s_mk, s_qc, s_qr = S("tanh"), S("masked"), S("q_cos_sin"), S("q_turned")
    m.s_raw_free[layer] = t_wo

    if rotary:
        cosT, sinT = (m.sb(f"{n}_{h}T", [P, C]) for h in ("cos", "sin"))
        cosk, sink = (m.sb(f"{n}_{h}", [P, HD]) for h in ("cos", "sin"))
        ka, kb = (m.sb(f"{n}_k_{h}", [P, HD]) for h in ("cos", "sin"))
        mask_in, mask = m.sb(f"{n}_mask_in", [P, C], mybir.dt.uint8), m.sb(f"{n}_mask", [P, C])
        maskT_in, maskT = m.sb(f"{n}_maskT_in", [C, C], mybir.dt.uint8), m.sb(f"{n}_maskT", [C, C])
        anyq, none = m.sb(f"{n}_any", [P, C]), m.sb(f"{n}_none", [P, 1])
        onesw = m.sb(f"{n}_ones", [C, P])
        s_tab, s_mT, s_any = S("tables_loaded"), S("maskT_ready"), S("any_key")
    else:
        nw = m.sb(f"{n}_norm_w", [P, 2])
        wqk = m.sb(f"{n}_norm_w_product", [P, 1])
        s_tab = S("norm_w_loaded")

    def step(g, s):
        return g * STEPS + s + 1

    def chunk(g, c):
        return g * 8 + c + 1

    def sync(sp):
        w_d = m.d[f"{n}_w"]
        if rotary:
            sp.wait_ge(m.s_ln[layer], 1)
            for dst, src in ((cosT, "cosT"), (sinT, "sinT"), (cosk, "cosk"), (sink, "sink")):
                sp.dma_start(dst[:, :], m.d[src]).then_inc(s_tab, 16)
            for r in range(2):
                sp.dma_start(mask_in[r * C:(r + 1) * C, :], m.d["mask"]).then_inc(s_tab, 16)
            sp.dma_start(maskT_in[:, :], m.d["maskT"]).then_inc(s_tab, 16)
        else:
            sp.wait_ge(m.s_ln[layer], 1)
            sp.dma_start(nw[:, :], m.d[f"{n}_norm_w"]).then_inc(s_tab, 16)

        def loads(g):
            for dst, a, b, done in ((raw_wq, 0, 2048, l_wq), (raw_wkv, 2048, 3072, l_wkv), (raw_wo, 3072, 5120, l_wo)):
                src = (w_d[g] if isinstance(g, int) else w_d[bass.ds(g, 1)].rearrange("o p n -> (o p) n"))[:, a:b]
                yield m.raw[:, a:b], src, done

        for dst, src, done in loads(0):
            sp.dma_start(dst, src).then_inc(done, 16)
        with sp.Fori(0, G - 1) as g:
            for (dst, src, done), (split, per) in zip(loads(g + 1), ((t_wq, 2 * HG), (t_wkv, 2), (t_wo, 2))):
                sp.wait_ge(split, (g + 1) * per)
                sp.dma_start(dst, src).then_inc(done, 16)
    ph.sync = sync

    def gpsimd(pool):
        def split_wq(g, h):
            c = slice(h * HD, (h + 1) * HD)
            if h == 0:
                pool.wait_ge(l_wq, (g + 1) * 16)
            pool.wait_ge(s_q, g * 8 + 5 + h)
            pool.tensor_tensor(wq[0][:, :, c], raw_wq[:, :, c], m.zero[:, 0:1].unsqueeze(2).broadcast_to([P, KT, HD]), ALU.add).then_inc(t_wq, 1)
            pool.wait_ge(t_wq, g * 2 * HG + 2 * h + 1)
            pool.tensor_tensor(wq[1][:, :, c], raw_wq[:, :, c], wq[0][:, :, c].bitcast(F32), ALU.subtract).then_inc(t_wq, 1)

        def split(g, w, raw, loaded, used, done):
            pool.wait_ge(loaded, (g + 1) * 16)
            pool.wait_ge(used, g * STEPS + STEPS)
            pool.tensor_tensor(w[0][:, :, :], raw, m.zero[:, 0:1].unsqueeze(2).broadcast_to([P, KT, raw.shape[2]]), ALU.add).then_inc(done, 1)
            pool.wait_ge(done, g * 2 + 1)
            pool.tensor_tensor(w[1][:, :, :], raw, w[0][:, :, :].bitcast(F32), ALU.subtract).then_inc(done, 1)

        def group(g, ahead):
            for s in range(STEPS):
                if rotary:
                    if s == 0:
                        for c in range(4):
                            turn_q(g, c)
                    pool.wait_ge(s_th, step(g, s))
                    pool.tensor_tensor(prob[:, :, :], prob[:, :, :], mask[:, :].unsqueeze(1).broadcast_to([P, 4, KW]), ALU.add).then_inc(s_mk, 1)
                pool.wait_ge(s_rt, step(g, s))
                pool.tensor_tensor(prob[:, :, :], prob[:, :, :], rt[:, :].unsqueeze(2).broadcast_to([P, 4, KW]), ALU.mult).then_inc(s_pn, 1)
                if rotary and s < 4:
                    turn_q(g, 4 + s)
                if ahead and s >= 3 and s < 7:
                    split_wq(g + 1, s - 3)
                if ahead and s == 7:
                    split(g + 1, wkv, raw_wkv, l_wkv, s_kv, t_wkv)
            if ahead:
                split(g + 1, wo, raw_wo, l_wo, s_wo, t_wo)

        def turn_q(g, c):
            half, h, k = c // 4, c % 4, c % 2
            qv = qa[:, k, :].rearrange("p (b r) -> p b r", b=HB)
            pool.wait_ge(s_qc, chunk(g, c))
            pool.tensor_tensor(qa[:, k, :], qa[:, k, :], qb[:, k, :], ALU.add).then_inc(s_qr, 1)
            pool.wait_ge(s_qh, chunk(g, c))
            dst = [a[:, half, :, h // 2, (h % 2) * C:(h % 2 + 1) * C] for a in q]
            pool.tensor_tensor(dst[1], qv, dst[0].bitcast(F32), ALU.subtract).then_inc(s_ql, 1)

        pool.wait_ge(m.s_ln[layer], 1)
        for h in range(HG):
            split_wq(0, h)
        split(0, wkv, raw_wkv, l_wkv, s_kv, t_wkv)
        split(0, wo, raw_wo, l_wo, s_wo, t_wo)
        if rotary:
            pool.wait_ge(s_any, 3)
        with pool.Fori(0, G - 1) as g:
            group(g, True)
        group(G - 1, False)
    ph.gpsimd = gpsimd

    def scalar(act):
        with act.Fori(0, NT // 2) as i:
            for u in range(2):
                act.wait_ge(s_xT, i * 2 + u + 1)
                act.activation(m.kvT[0][:, :, bass.ds((i * 2 + u) * P, P), 1], q_ps[u][:, :].rearrange("p (k t) -> p k t", k=KT),
                               ACT.Copy).then_inc(s_xh, 1)

        def high_q(g, c):
            half, h = c // 4, c % 4
            dst = q[0][:, half, :, h // 2, (h % 2) * C:(h % 2 + 1) * C]
            if rotary:
                act.wait_ge(s_qr, chunk(g, c))
                act.activation(dst, qa[:, c % 2, :].rearrange("p (b r) -> p b r", b=HB), ACT.Copy).then_inc(s_qh, 1)
            else:
                act.wait_ge(s_q, chunk(g, c) + 8)
                src = q_ps[c % 2][:, :].rearrange("p (b r) -> p b r", b=HB)
                act.activation(dst, src, ACT.Copy).then_inc(s_qh, 1)
                act.activation(qsq[:, half, :, h // 2, (h % 2) * C:(h % 2 + 1) * C], src, ACT.Square).then_inc(s_qsq, 1)

        def kv_parts(g, s):
            act.wait_ge(s_kv, step(g, s) + STEPS)
            if not rotary:
                for b in range(2):
                    last = act.activation(kn[:, b, :], kv_ps[:, b * KV:b * KV + HD], ACT.Square, accum_out=vark[:, b:b + 1])
                last.then_inc(s_kss, 1)
                src = kv_ps[:, :].rearrange("p (b w) -> p b w", b=2)[:, :, HD:KV]
                act.activation(v[0][:, s % 2, :, :], src, ACT.Copy).then_inc(s_vh, 1)
            else:
                act.activation(v[0][:, s % 2, 0, :], kv_ps[:, HD:KV], ACT.Copy).then_inc(s_vh, 1)

        def high_kT(g, s):
            act.wait_ge(s_kt, step(g, s))
            if rotary:
                act.activation(kT[0][:, 0, :], kT_ps[:, 0:P], ACT.Copy).then_inc(s_kth, 1)
            else:
                act.activation(kT[0][:, :, :], kT_ps[:, 0:2 * P].rearrange("p (b t) -> p b t", b=2), ACT.Copy,
                               scale=wqk[:, 0:1]).then_inc(s_kth, 1)

        if not rotary:
            act.wait_ge(s_rq, 1)
        with act.Fori(0, G) as g:
            for c in range(4):
                high_q(g, c)
            kv_parts(g, 0)
            high_kT(g, 0)
            for s in range(STEPS):
                if rotary:
                    act.wait_ge(s_s, step(g, s))
                    act.activation(prob[:, :, :], s_ps[:, 0:4 * KW].rearrange("p (j k) -> p j k", j=4), ACT.Tanh,
                                   scale=MULT / CAP).then_inc(s_th, 1)
                    act.wait_ge(s_mk, step(g, s))
                    act.activation(prob[:, :, :], prob[:, :, :], ACT.Exp, scale=CAP).then_inc(s_e, 1)
                else:
                    act.wait_ge(s_nb, step(g, s))
                    for j in range(4):
                        last = act.activation(prob[:, j, :], s_ps[:, j * KW:(j + 1) * KW], ACT.Exp, bias=nb[:, j:j + 1],
                                              scale=rq[:, j:j + 1], accum_out=tot[:, j:j + 1])
                    last.then_inc(s_e, 1)
                if s + 1 < STEPS:
                    kv_parts(g, s + 1)
                if s < 4:
                    high_q(g, 4 + s)
                cols = 4 * KW
                act.wait_ge(s_pt, step(g, s))
                act.activation(pT[0][:, 0:cols], pT_ps[:, 0:cols], ACT.Copy).then_inc(s_pth, 1)
                if s + 1 < STEPS:
                    high_kT(g, s + 1)
                act.wait_ge(s_pv, step(g, s))
                act.activation(o[0][:, :, :, :].rearrange("p h b r -> p b h r"),
                               o_ps[:, :].rearrange("p (b h r) -> p b h r", b=2, h=HG), ACT.Copy).then_inc(s_oh, 1)
    ph.scalar = scalar

    def vector(ve):
        order = Order(ve, s_ord)
        with ve.Fori(0, NT // 2) as i:
            order.loop(i, 0)
            for u in range(2):
                t = i * 2 + u
                ve.tensor_scalar(xn[:, u, :], m.x[:, bass.ds(t, 1), :].rearrange("p o n -> p (o n)"),
                                 m.mean[:, bass.ds(t, 1)], m.rstd[:, bass.ds(t, 1)], ALU.subtract, ALU.mult).then_inc(s_xn, 1)
            for u in range(2):
                ve.wait_ge(s_xh, i * 2 + u + 1)
                ve.tensor_tensor(m.kvT[1][:, :, bass.ds((i * 2 + u) * P, P), 1], q_ps[u][:, :].rearrange("p (k t) -> p k t", k=KT),
                                 m.kvT[0][:, :, bass.ds((i * 2 + u) * P, P), 1].bitcast(F32), ALU.subtract).then_inc(s_xl, 1)
            order.end(NT // 2)
        ve.wait_ge(s_tab, 16 * 7 if rotary else 16)
        if rotary:
            ve.memset(onesw[:, :], 1.0).then_inc(s_mT, 1)
            ve.tensor_copy(maskT[:, :], maskT_in[:, :]).then_inc(s_mT, 1)
            order.link(ve.tensor_copy(mask[:, :], mask_in[:, :]))
            order.link(ve.tensor_reduce(none[:, :], mask[:, :], AX.X, ALU.max))
            order.link(ve.tensor_scalar(none[:, :], none[:, :], -1.0, 1.0, ALU.mult, ALU.add))
            order.link(ve.tensor_scalar(mask[:, :], mask[:, :], none[:, 0:1], -1.0, ALU.max, ALU.add))
            ve.tensor_scalar(mask[:, :], mask[:, :], 1e30, None, ALU.mult).then_inc(s_any, 1)
            ve.wait_ge(s_any, 2)
            order.link(ve.tensor_scalar(anyq[:, :], kT_ps[:, 0:C], 0.5, None, ALU.is_gt))
            order.link(ve.tensor_tensor(cosT[:, :], cosT[:, :], anyq[:, :], ALU.mult))
            ve.tensor_tensor(sinT[:, :], sinT[:, :], anyq[:, :], ALU.mult).then_inc(s_any, 1)
            ve.wait_ge(s_any, 3)
        else:
            ve.scalar_tensor_tensor(wqk[:, :], nw[:, 0:1], ROOT, nw[:, 1:2], ALU.mult, ALU.mult).then_inc(s_rq, 1)

        def low_q(g, c):
            half, h = c // 4, c % 4
            src = q_ps[c % 2][:, :].rearrange("p (b r) -> p b r", b=HB)
            if rotary:
                low, high = slice(0, C), slice(C, P)
                a, b = (t[:, c % 2, :].rearrange("p (b r) -> p b r", b=HB) for t in (qa, qb))
                ve.wait_ge(s_q, chunk(g, c) + 8)
                ve.wait_ge(s_ql, chunk(g, c) - 2 + 2)
                ve.tensor_tensor(a, src, cosT[:, :].unsqueeze(1).broadcast_to([P, HB, C]), ALU.mult)
                ve.tensor_tensor(b[low], src[high], sinT[high, :].unsqueeze(1).broadcast_to([C, HB, C]), ALU.mult)
                ve.tensor_tensor(b[high], src[low], sinT[low, :].unsqueeze(1).broadcast_to([C, HB, C]), ALU.mult).then_inc(s_qc, 1)
            else:
                dst = [a[:, half, :, h // 2, (h % 2) * C:(h % 2 + 1) * C] for a in q]
                ve.wait_ge(s_qsq, chunk(g, c))
                ve.tensor_tensor(dst[1], src, dst[0].bitcast(F32), ALU.subtract).then_inc(s_ql, 1)

        def norm_k(g, s):
            if rotary:
                ve.wait_ge(s_vh, step(g, s))
                ve.tensor_tensor(ka[:, :], kv_ps[:, 0:HD], cosk[:, :], ALU.mult)
                half = HD // 2
                ve.tensor_tensor(kb[:, 0:half], kv_ps[:, half:HD], sink[:, 0:half], ALU.mult)
                order.link(ve.tensor_tensor(kb[:, half:HD], kv_ps[:, 0:half], sink[:, half:HD], ALU.mult))
                ve.tensor_tensor(kn[:, 0, :], ka[:, :], kb[:, :], ALU.add).then_inc(s_kn, 1)
                ve.tensor_tensor(v[1][:, s % 2, 0, :], kv_ps[:, HD:KV], v[0][:, s % 2, 0, :].bitcast(F32), ALU.subtract).then_inc(s_vl, 1)
            else:
                ve.wait_ge(s_kss, step(g, s))
                order.link(ve.tensor_scalar(vark[:, :], vark[:, :], 1.0 / HD, EPS, ALU.mult, ALU.add))
                rsqrt(ve, order, rk[:, :], vark[:, :], m.bits[:, 0:2], halfk[:, :], tmpk[:, :])
                src = kv_ps[:, :].rearrange("p (b w) -> p b w", b=2)
                ve.wait_ge(s_vh, step(g, s))
                ve.tensor_tensor(kn[:, :, :], src[:, :, 0:HD], rk[:, :].unsqueeze(2).broadcast_to([P, 2, HD]), ALU.mult).then_inc(s_kn, 1)
                ve.tensor_tensor(v[1][:, s % 2, :, :], src[:, :, HD:KV], v[0][:, s % 2, :, :].bitcast(F32), ALU.subtract).then_inc(s_vl, 1)

        def low_kT(g, s):
            ve.wait_ge(s_kth, step(g, s))
            if rotary:
                ve.tensor_tensor(kT[1][:, 0, :], kT_ps[:, 0:P], kT[0][:, 0, :].bitcast(F32), ALU.subtract).then_inc(s_ktl, 1)
            else:
                ve.scalar_tensor_tensor(kT[1][:, :, :], kT_ps[:, 0:2 * P].rearrange("p (b t) -> p b t", b=2), wqk[:, 0:1],
                                        kT[0][:, :, :].bitcast(F32), ALU.mult, ALU.subtract).then_inc(s_ktl, 1)
                order.link(ve.tensor_scalar(varq[:, :], kT_ps[:, 2 * P:2 * P + 4], 1.0 / HD, EPS, ALU.mult, ALU.add))
                rsqrt(ve, order, rq[:, :], varq[:, :], m.bits[:, 2:6], halfq[:, :], tmpq[:, :])

        def add(g, s):
            ve.wait_ge(s_wo, step(g, s) + STEPS)
            ve.tensor_tensor(m.x[:, s, :], m.x[:, s, :], y_ps[:, :], ALU.add).then_inc(s_add, 1)

        with ve.Fori(0, G) as g:
            order.loop(g, STEPS * (2 if rotary else 2 * RSQRT_LINKS + 3))
            for c in range(4):
                low_q(g, c)
            norm_k(g, 0)
            low_kT(g, 0)
            for s in range(STEPS):
                if rotary:
                    ve.wait_ge(s_e, step(g, s))
                    order.link(ve.tensor_reduce(tot[:, :], prob[:, :, :], AX.X, ALU.add))
                else:
                    ve.wait_ge(s_s, step(g, s))
                    order.link(ve.tensor_reduce(mx[:, :], s_ps[:, :].rearrange("p (j k) -> p j k", j=4), AX.X, ALU.max))
                    ve.scalar_tensor_tensor(nb[:, :], mx[:, :], -1.0, rq[:, :], ALU.mult, ALU.mult).then_inc(s_nb, 1)
                    ve.wait_ge(s_e, step(g, s))
                ve.reciprocal(rt[:, :], tot[:, :]).then_inc(s_rt, 1)
                if s + 1 < STEPS:
                    norm_k(g, s + 1)
                if s < 4:
                    low_q(g, 4 + s)
                cols = 4 * KW
                ve.wait_ge(s_pth, step(g, s))
                ve.tensor_tensor(pT[1][:, 0:cols], pT_ps[:, 0:cols], pT[0][:, 0:cols].bitcast(F32), ALU.subtract).then_inc(s_ptl, 1)
                if s + 1 < STEPS:
                    low_kT(g, s + 1)
                if s:
                    add(g, s - 1)
                ve.wait_ge(s_oh, step(g, s))
                ve.tensor_tensor(o[1][:, :, :, :].rearrange("p h b r -> p b h r"),
                                 o_ps[:, :].rearrange("p (b h r) -> p b h r", b=2, h=HG),
                                 o[0][:, :, :, :].rearrange("p h b r -> p b h r").bitcast(F32), ALU.subtract).then_inc(s_ol, 1)
            add(g, STEPS - 1)
            order.end(G)
        ve.wait_ge(s_add, G * STEPS)
        for t in range(NT):
            order.done(ve.bn_stats(m.stats[:, t, :], m.x[:, t, :]))
        finish_stats(ve, order, m, m.s_ln[layer + 1])
    ph.vector = vector

    def tensor(pe):
        pe.sem_inc(s_q, 8)
        pe.sem_inc(s_kv, STEPS)
        pe.sem_inc(s_wo, STEPS)
        with pe.Fori(0, NT // 2) as i:
            for u in range(2):
                pe.wait_ge(s_xn, i * 2 + u + 1)
                for k in range(KT):
                    last = pe.transpose(q_ps[u][:, k * P:(k + 1) * P], xn[:, u, k * P:(k + 1) * P], m.ident[:, :])
                last.then_inc(s_xT, 1)
        if rotary:
            pe.sem_inc(s_ql, 2)
            pe.wait_ge(s_mT, 2)
            pe.matmul(kT_ps[:, 0:C], onesw[:, :], maskT[:, :], start=True, stop=True).then_inc(s_any, 1)
            pe.wait_ge(s_any, 3)
        pe.wait_ge(s_xl, NT)
        pe.wait_ge(m.s_kv_ctx, m.kv_ctx_all)

        def queries(g, c):
            half, h = c // 4, c % 4
            if c < 4:
                pe.wait_ge(t_wq, g * 2 * HG + 2 * h + 2)
            if c >= 2:
                pe.wait_ge(s_qc if rotary else s_ql, chunk(g, c - 2))
            for k in range(KT):
                last = products(pe, q_ps[c % 2][:, :], [w[:, k, h * HD:(h + 1) * HD] for w in wq],
                                [a[:, k, half * 512:(half + 1) * 512, 1] for a in m.kvT], first=(k == 0), last=(k == KT - 1))
            last.then_inc(s_q, 1)

        def keys_values(g, s):
            if s == 0:
                pe.wait_ge(t_wkv, g * 2 + 2)
            else:
                pe.wait_ge(s_vl, step(g, s - 1))
            if rotary:
                for k in range(KT):
                    last = products(pe, kv_ps[:, 0:KV], [a[:, k, s * P:(s + 1) * P, 0] for a in m.kvT],
                                    [w[:, k, :] for w in wkv], first=(k == 0), last=(k == KT - 1))
            else:
                for b in range(2):
                    r = slice((2 * s + b) * C, (2 * s + b + 1) * C)
                    for k in range(KT):
                        last = products(pe, kv_ps[:, b * KV:(b + 1) * KV],
                                        [a[:, k, r, :].rearrange("p r j -> p (r j)") for a in m.kvT],
                                        [w[:, k, :] for w in wkv], first=(k == 0), last=(k == KT - 1))
            last.then_inc(s_kv, 1)

        def turn_keys(g, s):
            pe.wait_ge(s_kn, step(g, s))
            if rotary:
                pe.transpose(kT_ps[:, 0:P], kn[:, 0, :], m.ident[:, :]).then_inc(s_kt, 1)
            else:
                for b in range(2):
                    pe.transpose(kT_ps[:, b * P:(b + 1) * P], kn[:, b, :], m.ident[:, :])
                if s % 4 == 0:
                    pe.wait_ge(s_qsq, chunk(g, 4 * (s // 4) + 3))
                for j in range(4):
                    last = pe.matmul(kT_ps[:, 2 * P + j:2 * P + j + 1], qsq[:, s // 4, 2 * (s % 4) + j // 2, j % 2, :],
                                     m.ones_col[:, :], start=True, stop=True)
                last.then_inc(s_kt, 1)

        def scores(g, s):
            if s % 4 == 0:
                pe.wait_ge(s_ql, chunk(g, 4 * (s // 4) + 3) + (2 if rotary else 0))
            pe.wait_ge(s_ktl, step(g, s))
            for b in range(2):
                for hp in range(2):
                    at = (hp * 2 + b) if rotary else (b * 2 + hp)
                    last = products(pe, s_ps[:, at * KW:(at + 1) * KW], [a[:, s // 4, 2 * (s % 4) + b, hp, :] for a in q],
                                    [a[:, 0, b * C:(b + 1) * C] if rotary else a[:, b, :] for a in kT])
            last.then_inc(s_s, 1)

        def turn_probs(g, s):
            pe.wait_ge(s_pn, step(g, s))
            for j in range(2 if rotary else 4):
                src = prob[:, 2 * j:2 * j + 2, :].rearrange("p b k -> p (b k)") if rotary else prob[:, j, :]
                last = pe.transpose(pT_ps[:, j * P:(j + 1) * P], src, m.ident[:, :])
            last.then_inc(s_pt, 1)

        def heads(g, s):
            pe.wait_ge(s_vl, step(g, s))
            pe.wait_ge(s_ptl, step(g, s))
            for b in range(2):
                if rotary:
                    r = slice(b * C, (b + 1) * C)
                    if b:
                        pe.wait_ge(s_pv0, step(g, s))
                    last = products(pe, o_ps[:, b * 256:(b + 1) * 256], [a[r, s % 2, 0, :] for a in v], [a[r, 0:256] for a in pT])
                    if not b:
                        last.then_inc(s_pv0, 1)
                else:
                    last = products(pe, o_ps[:, b * 256:(b + 1) * 256], [a[:, s % 2, b, :] for a in v],
                                    [a[:, b * 256:(b + 1) * 256] for a in pT])
            last.then_inc(s_pv, 1)

        def project(g, s):
            if s == 0:
                pe.wait_ge(t_wo, g * 2 + 2)
            else:
                pe.wait_ge(s_add, step(g, s - 1))
            pe.wait_ge(s_ol, step(g, s))
            for h in range(HG):
                last = products(pe, y_ps[:, :], [a[:, h, :, :].rearrange("p b r -> p (b r)") for a in o],
                                [w[:, h, :] for w in wo], first=(h == 0), last=(h == HG - 1))
            last.then_inc(s_wo, 1)

        with pe.Fori(0, G) as g:
            for c in range(4):
                queries(g, c)
            keys_values(g, 0)
            turn_keys(g, 0)
            for s in range(STEPS):
                scores(g, s)
                if s + 1 < STEPS:
                    keys_values(g, s + 1)
                if s < 4:
                    queries(g, 4 + s)
                turn_probs(g, s)
                if s + 1 < STEPS:
                    turn_keys(g, s + 1)
                if s:
                    project(g, s - 1)
                heads(g, s)
            project(g, STEPS - 1)
    ph.tensor = tensor
    return ph


def latent_attention(m):
    return attention(m, False, "a1", 2)


def rotary_attention(m):
    return attention(m, True, "a2", 4)


def ranked_linear(m):
    ph = Phase()
    RANKS, RG = (0, 8, 16, 32, 64), 68
    MR = RANKS[-1]
    feed = TileFeed(m, "r1", 3)
    raw = m.raw[:, 0:KT * D].rearrange("p (k n) -> p k n", k=KT)
    rawa = m.raw[:, KT * D:KT * (D + RG)].rearrange("p (k n) -> p k n", k=KT)
    w = [m.sb(f"r1_w_{h}", [P, KT, D], F32R) for h in ("high", "low")]
    ag = [m.sb(f"r1_a_gate_{h}", [P, KT, RG], F32R) for h in ("high", "low")]
    rawb = m.sb("r1_b_raw", [MR + 1, D])
    bb = [m.sb(f"r1_b_{h}", [MR + 1, D], F32R) for h in ("high", "low")]
    gb = m.sb("r1_gate_b", [P, 4])
    sc, eq, cum, ex = (m.sb(f"r1_{n}", [P, 2, 4]) for n in ("scores", "is_best", "taken", "exp"))
    best, nbest, total, top, weight = (m.sb(f"r1_{n}", [P, 2]) for n in ("best", "nbest", "total", "top", "weight"))
    ranked = m.sb("r1_ranked", [P, 2, P])
    rT = [m.sb(f"r1_rankedT_{h}", [MR + 1, 2, P], F32R) for h in ("high", "low")]
    hg_ps, y_ps, rT_ps = m.ps[2:4], m.ps[4:6], m.ps[6:8]
    S = lambda h: m.layer_sem(f"r1_{h}")
    s_w, s_small, s_split, s_init = S("w_loaded"), S("small_loaded"), S("split"), S("init")
    s_hg, s_nb, s_ex, s_rk, s_rT, s_rh, s_rl = S("hg"), S("nbest"), S("exp"), S("ranked"), S("rankedT"), S("rankedT_high"), S("rankedT_low")
    s_y, s_add, s_ord = S("y"), S("added"), S("dve_order")

    def sync(sp):
        sp.wait_ge(m.s_ln[3], 1)
        sp.dma_start(raw, m.d["r1_w"].rearrange("(k p) n -> p k n", p=P)).then_inc(s_w, 16)
        sp.dma_start(rawa, m.d["r1_a_gate"].rearrange("(k p) n -> p k n", p=P)).then_inc(s_w, 16)
        sp.dma_start(rawb[:, :], m.d["r1_b"]).then_inc(s_small, 16)
        sp.dma_start(gb[:, :], m.d["r1_gate_b"].to_broadcast([P, 4])).then_inc(s_small, 16)
    ph.sync = sync

    def gpsimd(pool):
        pool.wait_ge(m.s_ln[3], 1)
        for h, value in ((0, 1.0), (1, 0.0)):
            pool.memset(rT[h][MR:MR + 1, :, :].bitcast(F32), value).then_inc(s_init, 1)
        pool.wait_ge(s_init, 2)
        pool.wait_ge(s_w, 32)
        pool.wait_ge(s_small, 32)
        pool.tensor_copy(ag[0][:, :, :], rawa).then_inc(s_split, 1)
        pool.tensor_copy(w[0][:, :, :], raw).then_inc(s_split, 1)
        pool.tensor_copy(bb[0][:, :], rawb[:, :]).then_inc(s_split, 1)
        pool.wait_ge(s_split, 3)
        pool.tensor_tensor(ag[1][:, :, :], rawa, ag[0][:, :, :].bitcast(F32), ALU.subtract).then_inc(s_split, 1)
        pool.tensor_tensor(w[1][:, :, :], raw, w[0][:, :, :].bitcast(F32), ALU.subtract).then_inc(s_split, 1)
        pool.tensor_tensor(bb[1][:, :], rawb[:, :], bb[0][:, :].bitcast(F32), ALU.subtract).then_inc(s_split, 1)
    ph.gpsimd = gpsimd

    def scalar(act):
        with act.Fori(0, NT // 2) as i:
            for u in range(2):
                feed.high(act, i, u)
            for u in range(2):
                act.wait_ge(s_nb, i * 2 + u + 1)
                act.activation(ex[:, u, :], sc[:, u, :], ACT.Exp, bias=nbest[:, u:u + 1], accum_out=total[:, u:u + 1]).then_inc(s_ex, 1)
            for u in range(2):
                act.wait_ge(s_rT, i * 2 + u + 1)
                act.activation(rT[0][0:MR, u, :], rT_ps[u][0:MR, 0:P], ACT.Copy).then_inc(s_rh, 1)
    ph.scalar = scalar

    def vector(ve):
        order = Order(ve, s_ord)
        ve.wait_ge(s_small, 32)
        order.link(ve.memset(cum[:, :, :], 0.0))
        order.link(ve.memset(ranked[:, :, :], 0.0))
        with ve.Fori(0, NT // 2) as i:
            order.loop(i, 2 * 12)
            for u in range(2):
                feed.normalise(ve, i, u)
            for u in range(2):
                feed.low(ve, i, u)
            for u in range(2):
                ve.wait_ge(s_hg, i * 2 + u + 1)
                order.link(ve.tensor_tensor(sc[:, u, :], hg_ps[u][:, MR:RG], gb[:, :], ALU.add))
                order.link(ve.tensor_reduce(best[:, u:u + 1], sc[:, u, :], AX.X, ALU.max))
                ve.tensor_scalar(nbest[:, u:u + 1], best[:, u:u + 1], -1.0, None, ALU.mult).then_inc(s_nb, 1)
                order.link(ve.tensor_scalar(eq[:, u, :], sc[:, u, :], best[:, u:u + 1], None, ALU.is_equal))
                order.link(ve.tensor_copy(cum[:, u, 1:2], eq[:, u, 0:1]))
                order.link(ve.tensor_tensor(cum[:, u, 2:3], cum[:, u, 1:2], eq[:, u, 1:2], ALU.max))
                order.link(ve.tensor_tensor(cum[:, u, 3:4], cum[:, u, 2:3], eq[:, u, 2:3], ALU.max))
            for u in range(2):
                ve.wait_ge(s_ex, i * 2 + u + 1)
                order.link(ve.reciprocal(top[:, u:u + 1], total[:, u:u + 1]))
                order.link(ve.reciprocal(weight[:, u:u + 1], top[:, u:u + 1]))
                order.link(ve.tensor_tensor(weight[:, u:u + 1], weight[:, u:u + 1], top[:, u:u + 1], ALU.mult))
                order.link(ve.tensor_scalar(eq[:, u, :], cum[:, u, :], -1.0, 1.0, ALU.mult, ALU.add))
                order.link(ve.tensor_scalar(eq[:, u, :], eq[:, u, :], weight[:, u:u + 1], None, ALU.mult))
                for r in range(4):
                    c = slice(RANKS[r], RANKS[r + 1])
                    last = ve.tensor_scalar(ranked[:, u, c], hg_ps[u][:, c], eq[:, u, r:r + 1], None, ALU.mult)
                    last.then_inc(s_rk, 1)
            for u in range(2):
                ve.wait_ge(s_rh, i * 2 + u + 1)
                ve.tensor_tensor(rT[1][0:MR, u, :], rT_ps[u][0:MR, 0:P], rT[0][0:MR, u, :].bitcast(F32), ALU.subtract).then_inc(s_rl, 1)
            for u in range(2):
                ve.wait_ge(s_y, i * 2 + u + 1)
                xt = m.x[:, bass.ds(i * 2 + u, 1), :].rearrange("p o n -> p (o n)")
                ve.tensor_tensor(xt, xt, y_ps[u][:, :], ALU.add).then_inc(s_add, 1)
                ve.wait_ge(s_add, i * 2 + u + 1)
                tile_stats(ve, order, m, i * 2 + u)
            order.end(NT // 2)
        finish_stats(ve, order, m, m.s_ln[4])
    ph.vector = vector

    def tensor(pe):
        pe.sem_inc(feed.s_used, 2)
        pe.wait_ge(s_split, 6)
        pe.wait_ge(s_init, 2)
        with pe.Fori(0, NT // 2) as i:
            for u in range(2):
                feed.turn(pe, i, u)
            for u in range(2):
                pe.wait_ge(feed.s_lo, i * 2 + u + 1)
                for k in range(KT):
                    last = products(pe, hg_ps[u][:, 0:RG], [a[:, u, k, :] for a in feed.xT], [c[:, k, :] for c in ag],
                                    first=(k == 0), last=(k == KT - 1))
                last.then_inc(s_hg, 1)
            for u in range(2):
                for k in range(KT):
                    products(pe, y_ps[u][:, :], [a[:, u, k, :] for a in feed.xT], [c[:, k, :] for c in w],
                             first=(k == 0), last=False)
                pe.wait_ge(s_rk, i * 8 + u * 4 + 4)
                pe.transpose(rT_ps[u][:, 0:P], ranked[:, u, :], m.ident[:, :]).then_inc(s_rT, 1)
            for u in range(2):
                pe.wait_ge(s_rl, i * 2 + u + 1)
                products(pe, y_ps[u][:, :], [a[:, u, :] for a in rT], [b[:, :] for b in bb], first=False, last=True).then_inc(s_y, 1)
            pe.wait_ge(s_y, i * 2 + 2)
            pe.sem_inc(feed.s_used, 2)
    ph.tensor = tensor
    return ph


def gated(m, n, layer, full, rest, quantised):
    ph = Phase()
    TURNS = full // 2
    HALF = T // 2
    GU, W3 = 2 * KT * P, 2 * KT * P + D
    wgu = [m.sb(f"{n}_gate_up_{h}", [P, 2, GU], F32R) for h in ("high", "low")]
    wd = [m.sb(f"{n}_down_{h}", [P, 2, D], F32R) for h in ("high", "low")]
    xn = m.sb(f"{n}_xn", [P, 2, D])
    act_out, hid = m.sb(f"{n}_silu", [P, 2, HALF]), m.sb(f"{n}_hidden", [P, 2, HALF])
    hs = [m.sb(f"{n}_hidden_{h}", [P, 2, T], F32R) for h in ("high", "low")]
    raw = [m.raw[:, u * W3:(u + 1) * W3] for u in range(2)]
    if quantised:
        raw = [r.bitcast(I32) for r in raw]
        zero, scale = m.sb(f"{n}_zero", [P, 2, W3], I32), m.sb(f"{n}_scale", [P, 2, W3])
        wf = m.sb(f"{n}_weight", [P, 2, W3])
    src = (lambda u: wf[:, u, :]) if quantised else (lambda u: raw[u])
    xT_ps, g_ps, u_ps, y_ps = m.ps[0:2], m.ps[0:2], m.ps[2:4], m.ps[4:8]
    S = lambda h: m.layer_sem(f"{n}_{h}")
    s_w, s_taken = [S(f"w_loaded_{u}") for u in range(2)], S("w_taken")
    s_wf, s_gh, s_gl, s_dh, s_dl = S("dequantised"), S("gate_up_high"), S("gate_up_low"), S("down_high"), S("down_low")
    s_d0 = S("minus_zero")
    s_xn, s_xT, s_xh, s_xl = S("xn"), S("xn_turned"), S("xT_high"), S("xT_low")
    s_gate, s_up, s_silu, s_hid, s_hh, s_hl = S("gate"), S("up"), S("silu"), S("hidden"), S("hidden_high"), S("hidden_low")
    s_y, s_add, s_ord = S("y"), S("added"), S("dve_order")
    last_layer = layer + 1 == 8
    PER = 3 if quantised else 1
    units = 2 * TURNS + (1 if rest else 0)

    def sync(sp):
        sp.wait_ge(m.s_ln[layer], 1)
        with sp.Fori(0, TURNS) as i:
            for u in range(2):
                t = i * 2 + u
                sp.wait_ge(s_taken, t + 1)
                one = lambda name: m.d[f"{n}_{name}"][bass.ds(t, 1)]
                sp.dma_start(raw[u], one("w").rearrange("o p n -> (o p) n")).then_inc(s_w[u], 16)
                if quantised:
                    sp.dma_start(zero[:, u, :], one("zero").to_broadcast([P, W3])).then_inc(s_w[u], 16)
                    sp.dma_start(scale[:, u, :], one("scale").to_broadcast([P, W3])).then_inc(s_w[u], 16)
        if rest:
            sp.wait_ge(s_taken, 2 * TURNS + 1)
            sp.dma_start(m.raw[:, 0:2 * KT * rest], m.d[f"{n}_rest_gate_up"]).then_inc(s_w[0], 16)
            sp.dma_start(m.raw[0:rest, GU:W3], m.d[f"{n}_rest_down"]).then_inc(s_w[0], 16)
    ph.sync = sync

    def gpsimd(pool):
        pool.wait_ge(m.s_ln[layer], 1)
        pool.sem_inc(s_taken, 2)

        def tile(i, u, width, prows):
            t = i * 2 + u
            gu = 2 * KT * width
            pool.wait_ge(s_gh, t + 1)
            pool.tensor_tensor(wgu[1][:, u, 0:gu], src(u)[:, 0:gu], wgu[0][:, u, 0:gu].bitcast(F32), ALU.subtract).then_inc(s_gl, 1)
            pool.wait_ge(s_dh, t + 1)
            pool.tensor_tensor(wd[1][0:prows, u, :], src(u)[0:prows, GU:W3], wd[0][0:prows, u, :].bitcast(F32), ALU.subtract).then_inc(s_dl, 1)
            pool.wait_ge(s_dl, t + 1)
            pool.wait_ge(s_gl, t + 1)
            pool.sem_inc(s_taken, 1)

        with pool.Fori(0, TURNS) as i:
            for u in range(2):
                tile(i, u, P, P)
        if rest:
            tile(TURNS, 0, rest, rest)
    ph.gpsimd = gpsimd

    def scalar(act):
        with act.Fori(0, NT // 2) as i:
            for u in range(2):
                act.wait_ge(s_xT, i * 2 + u + 1)
                act.activation(m.kvT[0][:, :, bass.ds((i * 2 + u) * P, P), 1], xT_ps[u][:, :].rearrange("p (k t) -> p k t", k=KT),
                               ACT.Copy).then_inc(s_xh, 1)

        def high_gate_up(i, u, width, loaded):
            t = i * 2 + u
            gu = 2 * KT * width
            if quantised:
                act.wait_ge(s_wf, t + 1)
            else:
                act.wait_ge(s_w[u], loaded)
            act.wait_ge(s_up, 2 * t + 1)
            act.activation(wgu[0][:, u, 0:gu], src(u)[:, 0:gu], ACT.Copy).then_inc(s_gh, 1)

        def high_down(i, u, prows):
            act.wait_ge(s_y, i * NT + 1)
            act.activation(wd[0][0:prows, u, :], src(u)[0:prows, GU:W3], ACT.Copy).then_inc(s_dh, 1)

        def silu(i, u, rows):
            t = i * 2 + u
            for h in range(2):
                act.wait_ge(s_gate, 2 * t + h + 1)
                act.activation(act_out[0:rows, h, :], g_ps[h][0:rows, :], ACT.Silu).then_inc(s_silu, 1)
                act.wait_ge(s_hid, 2 * t + h + 1)
                act.activation(hs[0][0:rows, u, h * HALF:(h + 1) * HALF], hid[0:rows, h, :], ACT.Copy).then_inc(s_hh, 1)

        high_gate_up(0, 0, P, 16)
        high_gate_up(0, 1, P, 16)
        high_down(0, 0, P)
        high_down(0, 1, P)
        with act.Fori(0, TURNS - 1) as i:
            for u in range(2):
                silu(i, u, P)
                high_gate_up(i + 1, u, P, (i + 2) * 16)
            for u in range(2):
                high_down(i + 1, u, P)
        silu(TURNS - 1, 0, P)
        if rest:
            high_gate_up(TURNS, 0, rest, TURNS * 16 + 32)
        silu(TURNS - 1, 1, P)
        if rest:
            high_down(TURNS, 0, rest)
            silu(TURNS, 0, rest)
    ph.scalar = scalar

    def vector(ve):
        order = Order(ve, s_ord)

        def dequantise(i, u):
            t = i * 2 + u
            ve.wait_ge(s_w[u], (i + 1) * 16 * PER)
            if not (isinstance(i, int) and i == 0):
                ve.wait_ge(s_gl, t - 1)
                ve.wait_ge(s_dl, t - 1)
            ve.tensor_tensor(wf[:, u, :], raw[u], zero[:, u, :], ALU.subtract).then_inc(s_d0, 1)
            ve.wait_ge(s_d0, t + 1)
            ve.tensor_tensor(wf[:, u, :], wf[:, u, :], scale[:, u, :], ALU.mult).then_inc(s_wf, 1)

        def hidden(i, u, rows):
            t = i * 2 + u
            for h in range(2):
                ve.wait_ge(s_silu, 2 * t + h + 1)
                ve.wait_ge(s_up, 2 * t + h + 5)
                ve.tensor_tensor(hid[0:rows, h, :], u_ps[h][0:rows, :], act_out[0:rows, h, :], ALU.mult).then_inc(s_hid, 1)
                ve.wait_ge(s_hh, 2 * t + h + 1)
                ve.tensor_tensor(hs[1][0:rows, u, h * HALF:(h + 1) * HALF], hid[0:rows, h, :],
                                 hs[0][0:rows, u, h * HALF:(h + 1) * HALF].bitcast(F32), ALU.subtract).then_inc(s_hl, 1)

        def add(i):
            for t in range(NT):
                ve.wait_ge(s_y, i * NT + t + 2)
                ve.tensor_tensor(m.x[:, t, :], m.x[:, t, :], y_ps[t % 4][:, :], ALU.add).then_inc(s_add, 1)

        with ve.Fori(0, NT // 2) as i:
            for u in range(2):
                t = i * 2 + u
                ve.tensor_scalar(xn[:, u, :], m.x[:, bass.ds(t, 1), :].rearrange("p o n -> p (o n)"),
                                 m.mean[:, bass.ds(t, 1)], m.rstd[:, bass.ds(t, 1)], ALU.subtract, ALU.mult).then_inc(s_xn, 1)
            for u in range(2):
                ve.wait_ge(s_xh, i * 2 + u + 1)
                ve.tensor_tensor(m.kvT[1][:, :, bass.ds((i * 2 + u) * P, P), 1], xT_ps[u][:, :].rearrange("p (k t) -> p k t", k=KT),
                                 m.kvT[0][:, :, bass.ds((i * 2 + u) * P, P), 1].bitcast(F32), ALU.subtract).then_inc(s_xl, 1)
        if quantised:
            dequantise(0, 0)
            dequantise(0, 1)
        with ve.Fori(0, TURNS - 1 if quantised else TURNS) as i:
            for u in range(2):
                hidden(i, u, P)
                if quantised:
                    dequantise(i + 1, u)
            add(i)
        if quantised:
            hidden(TURNS - 1, 0, P)
            hidden(TURNS - 1, 1, P)
            add(TURNS - 1)
        if rest:
            hidden(TURNS, 0, rest)
            add(TURNS)
        ve.wait_ge(s_add, NT * (TURNS + (1 if rest else 0)))
        if last_layer:
            ve.tensor_copy(m.mean[:, :], m.mean_var[:, :, 0]).then_inc(m.s_ln[8], 1)
            return
        for t in range(NT):
            order.done(ve.bn_stats(m.stats[:, t, :], m.x[:, t, :]))
        finish_stats(ve, order, m, m.s_ln[layer + 1])
    ph.vector = vector

    def tensor(pe):
        pe.sem_inc(s_up, 4)
        pe.sem_inc(s_y, 1)
        with pe.Fori(0, NT // 2) as i:
            for u in range(2):
                pe.wait_ge(s_xn, i * 2 + u + 1)
                for k in range(KT):
                    last = pe.transpose(xT_ps[u][:, k * P:(k + 1) * P], xn[:, u, k * P:(k + 1) * P], m.ident[:, :])
                last.then_inc(s_xT, 1)
        pe.wait_ge(s_xl, NT)

        def gate_up(i, u, width, peeled=False):
            t = i * 2 + u
            pe.wait_ge(s_gl, t + 1)
            for h in range(2):
                if not (isinstance(i, int) and i == 0 and u == 0):
                    pass
                for j, (ps, done) in enumerate(((g_ps, s_gate), (u_ps, s_up))):
                    if u or peeled:
                        pe.wait_ge(s_silu if j == 0 else s_hid, 2 * t + h - 1)
                    for k in range(KT):
                        c = slice((j * KT + k) * width, (j * KT + k + 1) * width)
                        last = products(pe, ps[h][0:width, :], [w[:, u, c] for w in wgu],
                                        [a[:, k, h * HALF:(h + 1) * HALF, 1] for a in m.kvT], first=(k == 0), last=(k == KT - 1))
                    last.then_inc(done, 1)

        def down(i, rows, us):
            for t in range(NT):
                if t % 4 == 0:
                    pe.wait_ge(s_hl, i * 4 + 2 * us[-1] + t // 4 + 1)
                if t == 0:
                    pe.wait_ge(s_dl, i * 2 + us[-1] + 1)
                if t >= 4:
                    pe.wait_ge(s_add, i * NT + t - 3)
                for u in us:
                    last = products(pe, y_ps[t % 4][:, :], [a[0:rows, u, t * P:(t + 1) * P] for a in hs],
                                    [w[0:rows, u, :] for w in wd], first=(u == us[0]), last=(u == us[-1]))
                last.then_inc(s_y, 1)

        with pe.Fori(0, TURNS) as i:
            for u in range(2):
                gate_up(i, u, P)
            down(i, P, (0, 1))
            pe.wait_ge(s_add, (i + 1) * NT - 2)
        if rest:
            gate_up(TURNS, 0, rest, peeled=True)
            down(TURNS, rest, (0,))
    ph.tensor = tensor
    return ph


def gated_feedforward(m):
    return gated(m, "f2", 5, 10, 96, False)


def quantised_feedforward(m):
    return gated(m, "f3", 7, 14, 0, True)


def linear_attention(m):
    ph = Phase()
    ctx_raw = m.sb("n3_ctx", [P, 2, D])
    ek = m.sb("n3_k_exp", [P, 2, D])
    ekT = [m.sb(f"n3_kT_{h}", [P, 2, KT, P], F32R) for h in ("high", "low")]
    kvm = m.sb("n3_kv", [P, 2, P])
    kv = [m.sb(f"n3_kv_{h}", [P, 2, P], F32R) for h in ("high", "low")]
    xn = m.sb("n3_xn", [P, 2, D])
    eq = m.sb("n3_q_exp", [P, 2, D])
    qs = [m.sb(f"n3_q_{h}", [P, 2, D], F32R) for h in ("high", "low")]
    mx, nb, tot, rt = (m.sb(f"n3_{h}", [P, 2]) for h in ("max", "nbias", "total", "rtotal"))
    rden = m.sb("n3_rden", [P, 2, D])
    y = m.sb("n3_y", [P, 2, D])
    blocks = m.sb("n3_blocks", [P, P])
    blocks_r = m.sb("n3_blocks_r", [P, P], F32R)
    kT_ps, kv_ps, den_ps, y_ps = m.ps[0:2], m.ps[2:4], m.ps[4:6], m.ps[6:8]
    S = lambda h: m.layer_sem(f"n3_{h}")
    s_blk, s_c = S("blocks_loaded"), [S(f"ctx_loaded_{u}") for u in range(2)]
    s_nb, s_ek, s_rt, s_kt, s_kh, s_kl = S("nbias"), S("k_exp"), S("rtotal"), S("kT"), S("kT_high"), S("kT_low")
    s_kv, s_kvm, s_kvh, s_kvl = S("kv"), S("kv_masked"), S("kv_high"), S("kv_low")
    s_xn, s_eq, s_qh, s_ql = S("xn"), S("q_exp"), S("q_high"), S("q_low")
    s_den, s_y, s_ord, s_add, s_blkr = S("den"), S("y"), S("dve_order"), S("added"), S("blocks_ready")

    def sync(sp):
        sp.wait_ge(m.s_ln[6], 1)
        sp.dma_start(blocks[:, :], m.d["blocks"]).then_inc(s_blk, 16)
        ctx_d = m.d["ctx"].rearrange("(t p) n -> p t n", p=P)
        with sp.Fori(0, NT // 2) as i:
            for u in range(2):
                sp.wait_ge(s_ek, i * 2 + u + 1)
                sp.dma_start(ctx_raw[:, u, :], ctx_d[:, bass.ds(i * 2 + u, 1), :].rearrange("p o n -> p (o n)")).then_inc(s_c[u], 16)
    ph.sync = sync

    def gpsimd(pool):
        with pool.Fori(0, NT // 2) as i:
            for u in range(2):
                pool.wait_ge(s_qh, i * 2 + u + 1)
                pool.tensor_tensor(qs[1][:, u, :], eq[:, u, :], qs[0][:, u, :].bitcast(F32), ALU.subtract).then_inc(s_ql, 1)
            for u in range(2):
                pool.wait_ge(s_kvh, i * 2 + u + 1)
                pool.tensor_tensor(kv[1][:, u, :], kvm[:, u, :], kv[0][:, u, :].bitcast(F32), ALU.subtract).then_inc(s_kvl, 1)
    ph.gpsimd = gpsimd

    def scalar(act):
        act.sem_inc(s_ek, 2)
        act.wait_ge(m.s_ln[6], 1)
        with act.Fori(0, NT // 2) as i:
            for u in range(2):
                act.wait_ge(s_nb, i * 2 + u + 1)
                act.activation(ek[:, u, :], ctx_raw[:, u, :], ACT.Exp, bias=nb[:, u:u + 1], accum_out=tot[:, u:u + 1]).then_inc(s_ek, 1)
            for u in range(2):
                act.wait_ge(s_xn, i * 2 + u + 1)
                act.activation(eq[:, u, :], xn[:, u, :], ACT.Exp).then_inc(s_eq, 1)
            for u in range(2):
                act.wait_ge(s_eq, i * 2 + u + 1)
                act.activation(qs[0][:, u, :], eq[:, u, :], ACT.Copy).then_inc(s_qh, 1)
            for u in range(2):
                act.wait_ge(s_kt, i * 2 + u + 1)
                act.activation(ekT[0][:, u, :, :], kT_ps[u][:, :].rearrange("p (k c) -> p k c", k=KT), ACT.Copy).then_inc(s_kh, 1)
            for u in range(2):
                act.wait_ge(s_kvm, i * 2 + u + 1)
                act.activation(kv[0][:, u, :], kvm[:, u, :], ACT.Copy).then_inc(s_kvh, 1)
    ph.scalar = scalar

    def vector(ve):
        order = Order(ve, s_ord)
        ve.wait_ge(s_blk, 16)
        ve.tensor_copy(blocks_r[:, :], blocks[:, :]).then_inc(s_blkr, 1)
        with ve.Fori(0, NT // 2) as i:
            order.loop(i, 2 * 4)
            for u in range(2):
                ve.wait_ge(s_c[u], (i + 1) * 16)
                order.link(ve.tensor_reduce(mx[:, u:u + 1], ctx_raw[:, u, :], AX.X, ALU.max))
                ve.tensor_scalar(nb[:, u:u + 1], mx[:, u:u + 1], -1.0, None, ALU.mult).then_inc(s_nb, 1)
            for u in range(2):
                t = i * 2 + u
                ve.tensor_scalar(xn[:, u, :], m.x[:, bass.ds(t, 1), :].rearrange("p o n -> p (o n)"),
                                 m.mean[:, bass.ds(t, 1)], m.rstd[:, bass.ds(t, 1)], ALU.subtract, ALU.mult).then_inc(s_xn, 1)
            for u in range(2):
                ve.wait_ge(s_ek, i * 2 + u + 3)
                order.link(ve.reciprocal(rt[:, u:u + 1], tot[:, u:u + 1]))
            for u in range(2):
                ve.wait_ge(s_kh, i * 2 + u + 1)
                ve.tensor_tensor(ekT[1][:, u, :, :], kT_ps[u][:, :].rearrange("p (k c) -> p k c", k=KT),
                                 ekT[0][:, u, :, :].bitcast(F32), ALU.subtract).then_inc(s_kl, 1)
            for u in range(2):
                ve.wait_ge(s_kv, i * 2 + u + 1)
                ve.scalar_tensor_tensor(kvm[:, u, :], kv_ps[u][:, 0:P], rt[:, u:u + 1], blocks[:, :], ALU.mult, ALU.mult).then_inc(s_kvm, 1)
            for u in range(2):
                ve.wait_ge(s_den, i * 2 + u + 1)
                order.done(ve.reciprocal(rden[:, u, :], den_ps[u][:, :]))
            for u in range(2):
                t = i * 2 + u
                xt = m.x[:, bass.ds(t, 1), :].rearrange("p o n -> p (o n)")
                ve.wait_ge(s_y, t + 1)
                if u == 0:
                    order.wait()
                ve.tensor_tensor(y[:, u, :], y_ps[u][:, :], rden[:, u, :], ALU.mult).then_inc(s_add, 1)
                ve.wait_ge(s_add, i * 4 + u * 2 + 1)
                ve.tensor_tensor(xt, xt, y[:, u, :], ALU.add).then_inc(s_add, 1)
                ve.wait_ge(s_add, i * 4 + u * 2 + 2)
                tile_stats(ve, order, m, t)
            order.end(NT // 2)
        finish_stats(ve, order, m, m.s_ln[7])
    ph.vector = vector

    def tensor(pe):
        pe.wait_ge(s_blkr, 1)
        with pe.Fori(0, NT // 2) as i:
            for u in range(2):
                pe.wait_ge(s_ek, i * 2 + u + 3)
                for k in range(KT):
                    last = pe.transpose(kT_ps[u][:, k * P:(k + 1) * P], ek[:, u, k * P:(k + 1) * P], m.ident[:, :])
                last.then_inc(s_kt, 1)
            for u in range(2):
                pe.wait_ge(s_ql, i * 2 + u + 1)
                pe.matmul(den_ps[u][:, :], blocks_r[:, :], qs[0][:, u, :], start=True, stop=False)
                pe.matmul(den_ps[u][:, :], blocks_r[:, :], qs[1][:, u, :], start=False, stop=True).then_inc(s_den, 1)
            for u in range(2):
                pe.wait_ge(s_kl, i * 2 + u + 1)
                for k in range(KT):
                    last = products(pe, kv_ps[u][:, 0:P], [a[:, u, k, :] for a in ekT],
                                    [a[:, k, bass.ds((i * 2 + u) * P, P), 0] for a in m.kvT], first=(k == 0), last=(k == KT - 1))
                last.then_inc(s_kv, 1)
            for u in range(2):
                pe.wait_ge(s_kvl, i * 2 + u + 1)
                products(pe, y_ps[u][:, :], [a[:, u, :] for a in kv], [a[:, u, :] for a in qs]).then_inc(s_y, 1)
    ph.tensor = tensor
    return ph


LAYERS = [context_attention, clustered_linear, latent_attention, ranked_linear, rotary_attention, gated_feedforward, linear_attention, quantised_feedforward]


class Memory:

    def __init__(self, nc, ctx, dram):
        self.nc, self.ctx, self.d = nc, ctx, dram
        self.layer = ExitStack()
        self.layer_sems = [ExitStack()]
        keep = lambda n, s, dt=F32: ctx.enter_context(nc.sbuf_tensor(n, s, dt))
        self.x = keep("x_rows", [P, NT, D])
        self.kvT = [keep(f"kvT_{h}", [P, KT, T, 2], F32R) for h in ("high", "low")]
        self.ident = keep("ident", [P, P])
        self.stats = keep("ln_stats", [P, NT, 6])
        self.mean_var = keep("ln_mean_var", [P, NT, 2])
        self.var, self.rstd, self.mean = (keep(f"ln_{n}", [P, NT]) for n in ("var", "rstd", "mean"))
        self.bits = keep("rsqrt_bits", [P, 16], I32)
        self.half, self.tmp = keep("rsqrt_half", [P, 16]), keep("rsqrt_tmp", [P, 16])
        self.ps = [ctx.enter_context(nc.psum_tensor(f"bank{i}", [P, 512], F32)) for i in range(8)]
        self.s_ident = self.sem("ident_loaded")
        self.s_ln = {k: self.sem(f"l{k}_stats_ready") for k in range(1, len(LAYERS) + 1)}
        self.s_kv_ctx = self.sem("kvT_ctx_ready")
        self.s_left = [self.sem(f"layer_{k}_left") for k in range(len(LAYERS) - 2)]
        self.s_cleared, self.s_stored = self.sem("layer_semaphores_cleared"), self.sem("stored")
        self.raw = keep("raw_weights", [P, 5120])
        self.ones_row, self.ones_col = keep("ones_row", [1, P], F32R), keep("ones_col", [P, 1])
        self.zero = keep("zero", [P, 1])
        self.s_raw_free, self.s_ones = {}, self.sem("ones")
        self.own = [[]]

    def sb(self, name, shape, dt=F32):
        return self.layer.enter_context(self.nc.sbuf_tensor(name, shape, dt))

    def sem(self, name):
        return self.ctx.enter_context(self.nc.semaphore(name))

    def layer_sem(self, name):
        sem = self.layer_sems[-1].enter_context(self.nc.semaphore(name))
        self.own[-1].append(sem)
        return sem

    def next_layer(self):
        self.layer.close()
        self.layer_sems.append(ExitStack())
        self.own.append([])
        if len(self.layer_sems) >= 3:
            self.layer_sems[-3].close()


def build(nc, dram, out):
    with ExitStack() as ctx:
        m = Memory(nc, ctx, dram)
        layers = []
        for make in LAYERS:
            layers.append(make(m))
            m.next_layer()
        s_left, s_cleared, s_stored = m.s_left, m.s_cleared, m.s_stored

        def run(eng, part):
            for k, layer in enumerate(layers):
                if k >= 2:
                    eng.wait_ge(s_cleared, k - 1)
                part(layer)(eng)
                if k + 2 < len(layers):
                    eng.sem_inc(s_left[k], 1)

        block = ctx.enter_context(nc.Block())

        @block.sync
        def _(sp):
            for k, layer in enumerate(layers):
                if k >= 2:
                    sp.wait_ge(s_left[k - 2], 5)
                    for sem in m.own[k - 2]:
                        sp.sem_clear(sem)
                    sp.sem_inc(s_cleared, 1)
                layer.sync(sp)
                if k + 2 < len(layers):
                    sp.sem_inc(s_left[k], 1)
            sp.wait_ge(m.s_ln[len(LAYERS)], 1)
            sp.dma_start(out.rearrange("(t p) n -> p t n", p=P), m.x[:, :, :]).then_inc(s_stored, 16)
            sp.wait_ge(s_stored, 16)

        @block.scalar
        def _(act):
            run(act, lambda layer: layer.scalar)

        @block.vector
        def _(ve):
            ve.memset(m.ones_row[:, :].bitcast(F32), 1.0).then_inc(m.s_ones, 1)
            ve.memset(m.ones_col[:, :], 1.0).then_inc(m.s_ones, 1)
            ve.memset(m.zero[:, :], 0.0).then_inc(m.s_ones, 1)
            run(ve, lambda layer: layer.vector)

        @block.gpsimd
        def _(pool):
            pool.wait_ge(m.s_ones, 3)
            run(pool, lambda layer: layer.gpsimd)

        @block.tensor
        def _(pe):
            pe.wait_ge(m.s_ones, 3)
            run(pe, lambda layer: layer.tensor)


def lay_out(v):
    c = np.ascontiguousarray
    a = {k: np.asarray(x) for k, x in v.items()}
    rows = lambda z: c(z.reshape(T, D))
    d = {"x": rows(a["x"]), "ctx": rows(a["ctx_4096"]), "ctxT": c(a["ctx_4096"].reshape(T, D).T),
         "ident": np.eye(P, dtype=np.float32)}
    one_row = lambda z: c(z.reshape(1, -1))
    d["c0_w"], d["c0_centroids"] = c(a["L0_ffn_weight"].T), c(a["L0_ffn_centroids"].T)
    d["c0_bias"], d["c0_owner"] = one_row(a["L0_ffn_bias"]), one_row(a["L0_ffn_assignments"])
    for name, layer in (("a1", "L1"), ("a2", "L2")):
        wq, wk, wv, wo = (a[f"{layer}_xattn_W{s}"] for s in "qkvo")
        by_group = lambda w: w.reshape(KT, P, 8, -1).transpose(2, 1, 0, 3)
        wkv = np.concatenate([by_group(wk), by_group(wv)], axis=3)
        wog = wo.reshape(8, 4, P, D).transpose(0, 2, 1, 3)
        d[f"{name}_w"] = np.concatenate([by_group(wq).reshape(8, P, -1), wkv.reshape(8, P, -1), wog.reshape(8, P, -1)], axis=2)
    d["a1_norm_w"] = np.stack([a["L1_xattn_q_norm_w"], a["L1_xattn_k_norm_w"]], axis=1)
    f32 = np.float32
    phase = np.arange(C, dtype=f32)[:, None] * (f32(1.0) / f32(10000.0) ** (np.arange(0, P, 2, dtype=f32) / f32(P)))[None, :]
    cos, sin = np.tile(np.cos(phase), (1, 2)), np.sin(phase)
    d["cosT"], d["sinT"] = c(cos.T), c(np.concatenate([sin, -sin], axis=1).T)
    d["cosk"], d["sink"] = np.tile(cos, (2, 1)), np.tile(np.concatenate([-sin, sin], axis=1), (2, 1))
    mask = a["mask_1x1xSxS2_bk0"].reshape(C, C)
    d["mask"], d["maskT"] = c(mask), c(mask.T)
    d["r1_w"], d["r1_a_gate"] = c(a["L1_ffn_W"].T), c(np.concatenate([a["L1_ffn_A"].T, a["L1_ffn_gate_w"].T], axis=1))
    d["r1_b"], d["r1_gate_b"] = np.concatenate([a["L1_ffn_B"].T, one_row(a["L1_ffn_b"])]), one_row(a["L1_ffn_gate_b"])
    def tiles(w, k):
        return w.reshape(KT, P, k, P).transpose(2, 1, 0, 3).reshape(k, P, D)
    gate, up, down = a["L2_ffn_W_gate"].T, a["L2_ffn_W_up"].T, a["L2_ffn_W_down"].T
    full = gate.shape[1] // P
    edge = full * P
    d["f2_w"] = np.concatenate([tiles(gate[:, :edge], full), tiles(up[:, :edge], full), down[:edge].reshape(full, P, D)], axis=2)
    last = lambda w: w[:, edge:].reshape(KT, P, -1).transpose(1, 0, 2).reshape(P, -1)
    d["f2_rest_gate_up"], d["f2_rest_down"] = np.concatenate([last(gate), last(up)], axis=1), c(down[edge:])
    q = lambda name: a[f"L3_ffn_{name}"]
    full = q("gate_w").shape[1] // P
    d["f3_w"] = np.concatenate([tiles(q("gate_w"), full), tiles(q("up_w"), full), q("down_w").reshape(full, P, D)], axis=2)
    columns = lambda z: z.reshape(KT, full, P).transpose(1, 0, 2).reshape(full, D)
    for name, s in (("zero", "z"), ("scale", "s")):
        d[f"f3_{name}"] = np.concatenate([columns(q(f"gate_{s}")), columns(q(f"up_{s}")), q(f"down_{s}")], axis=1)
    d["blocks"] = np.kron(np.eye(P // 8, dtype=np.float32), np.ones((8, 8), np.float32))
    return d


def kernel(**inputs):
    import concourse.bacc as bacc
    from concourse.bass_utils import run_bass_kernel_spmd

    nc = bacc.Bacc("TRN2", target_bir_lowering=False, num_devices=1)
    arrays = {f"in_{name}": a for name, a in lay_out(inputs).items()}
    dram = {name[3:]: nc.dram_tensor(name, a.shape, mybir.dt.from_np(a.dtype), kind="ExternalInput").ap()
            for name, a in arrays.items()}
    out = nc.dram_tensor("out", (T, D), F32, kind="ExternalOutput").ap()
    build(nc, dram, out)
    r = run_bass_kernel_spmd(nc, [arrays], core_ids=[0])
    return r.results[0]["out"].reshape(B, C, N)
```

```python
from contextlib import ExitStack

import numpy as np

import concourse.bass as bass
from concourse import mybir

F32 = mybir.dt.float32
F32R = mybir.dt.float32r
I32 = mybir.dt.int32
ALU = mybir.AluOpType
ACT = mybir.ActivationFunctionType
AX = mybir.AxisListType

P = 128
B, C, N = 16, 64, 512
D = N
KT = D // P
T = B * C
NT = T // P
EPS_LN = 1e-5
MAGIC = 0x5F3759DF


class Phase:

    def __init__(self):
        nothing = lambda eng: None
        self.sync = self.scalar = self.vector = self.gpsimd = self.tensor = nothing


class Order:

    def __init__(self, eng, sem):
        self.eng, self.sem, self.count, self.turn = eng, sem, 0, 0

    def wait(self):
        self.eng.wait_ge(self.sem, self.turn + self.count)

    def done(self, ins):
        ins.then_inc(self.sem, 1)
        self.count += 1

    def link(self, ins):
        self.done(ins)
        self.wait()

    def loop(self, i, per, start=0):
        self.before, self.per, self.start = self.count, per, start
        self.count -= start * per
        self.turn = i * per

    def end(self, turns):
        assert self.count - self.before == self.per * (1 - self.start), (self.count - self.before, self.per)
        self.count = self.before + turns * self.per
        self.turn = 0


def rsqrt(ve, order, y, v, bits, half, t):
    order.link(ve.tensor_scalar(bits, v.bitcast(I32), 1, None, ALU.logical_shift_right))
    order.link(ve.tensor_scalar(y.bitcast(I32), bits, -1.0, float(MAGIC), ALU.mult, ALU.add))
    order.link(ve.tensor_scalar(half, v, -0.5, None, ALU.mult))
    for _ in range(3):
        order.link(ve.tensor_tensor(t, y, y, ALU.mult))
        order.link(ve.tensor_tensor(t, t, half, ALU.mult))
        order.link(ve.scalar_tensor_tensor(y, t, 1.5, y, ALU.add, ALU.mult))


RSQRT_LINKS = 12


def products(pe, out, lhs, rhs, first=True, last=True):
    pe.matmul(out, lhs[0], rhs[0], start=first, stop=False)
    pe.matmul(out, lhs[0], rhs[1], start=False, stop=False)
    return pe.matmul(out, lhs[1], rhs[0], start=False, stop=last)


def tile_stats(ve, order, m, t):
    stats, xt = (m.stats[:, t, :], m.x[:, t, :]) if isinstance(t, int) else \
        (m.stats[:, bass.ds(t, 1), :].rearrange("p o s -> p (o s)"), m.x[:, bass.ds(t, 1), :].rearrange("p o n -> p (o n)"))
    order.done(ve.bn_stats(stats, xt))


def finish_stats(ve, order, m, ready):
    order.wait()
    for t in range(NT):
        order.done(ve.bn_aggr(m.mean_var[:, t, :], m.stats[:, t, :]))
    order.wait()
    order.link(ve.tensor_scalar(m.var[:], m.mean_var[:, :, 1], EPS_LN, None, ALU.add))
    rsqrt(ve, order, m.rstd[:], m.var[:], m.bits[:, 0:NT], m.half[:, 0:NT], m.tmp[:, 0:NT])
    ve.tensor_copy(m.mean[:], m.mean_var[:, :, 0]).then_inc(ready, 1)
    ve.wait_ge(ready, 1)


def context_attention(m):
    ph = Phase()
    SCALE = 1.0 / 8.0
    BODY = 4
    TURNS = NT // BODY
    STEPS = BODY * 2 * KT
    NB = BODY * 2
    spare = m.raw[:, 5120 - 5 * D:].rearrange("p (u n) -> p u n", u=5)
    XS = 3
    xn, ctx_raw = spare[:, 0:XS, :], spare[:, XS:5, :]
    xn_s = [m.sb(f"l0_xn_{h}", [P, BODY, D], F32R) for h in ("high", "low")]
    ctx_s = [m.sb(f"l0_ctx_{h}", [P, BODY, D], F32R) for h in ("high", "low")]
    ctxT_raw = m.sb("l0_ctxT_raw", [P, KT, T])
    val_s = [m.sb(f"l0_val_{h}", [P, BODY, KT, P], F32R) for h in ("high", "low")]
    prob = m.sb("l0_prob", [P, 4, D])
    probT_s = [m.sb(f"l0_probT_{h}", [P, 2, KT, D], F32R) for h in ("high", "low")]
    mx, nbias, total, rtotal = (m.sb(f"l0_{n}", [P, STEPS]) for n in ("max", "nbias", "total", "rtotal"))
    score_ps, probT_ps, out_ps = m.ps[0:4], m.ps[4:6], m.ps[6:8]

    s_x, s_ctxT = m.layer_sem("l0_x_loaded"), m.layer_sem("l0_ctxT_loaded")
    s_ctx = [m.layer_sem(f"l0_ctx_loaded_{u}") for u in range(BODY)]
    s_xn, s_high, s_low = m.layer_sem("l0_xn_done"), m.layer_sem("l0_high_parts"), m.layer_sem("l0_low_parts")
    s_score, s_nbias, s_exp, s_rt = m.layer_sem("l0_scores"), m.layer_sem("l0_nbias"), m.layer_sem("l0_exp"), m.layer_sem("l0_rtotal")
    s_prob, s_probT, s_hi, s_lo = m.layer_sem("l0_probs"), m.layer_sem("l0_probT"), m.layer_sem("l0_probT_high"), m.layer_sem("l0_probT_low")
    s_out, s_add = m.layer_sem("l0_out"), m.layer_sem("l0_added")
    s_ord, s_ln, s_kv = m.layer_sem("l0_dve_order"), m.layer_sem("l0_stats_ready"), m.s_kv_ctx
    m.kv_ctx_all = 2 * NT

    def sync(sp):
        sp.dma_start(m.x[:, :, :], m.d["x"].rearrange("(t p) n -> p t n", p=P)).then_inc(s_x, 16)
        sp.dma_start(m.ident[:, :], m.d["ident"]).then_inc(m.s_ident, 16)
        sp.dma_start(ctxT_raw[:, :, :], m.d["ctxT"].rearrange("(k p) t -> p k t", p=P)).then_inc(s_ctxT, 16)
        ctx_d = m.d["ctx"].rearrange("(t p) n -> p t n", p=P)
        with sp.Fori(0, TURNS) as i:
            for u in range(BODY):
                sp.wait_ge(s_low, (i + 1) * BODY + u - 1)
                sp.dma_start(ctx_raw[:, u % 2, :], ctx_d[:, bass.ds(i * BODY + u, 1), :].rearrange("p o n -> p (o n)")).then_inc(s_ctx[u], 16)
    ph.sync = sync

    def scalar(act):
        with act.Fori(0, TURNS) as i:
            def operands(u):
                act.wait_ge(s_ctx[u], (i + 1) * 16)
                act.activation(ctx_s[0][:, u, :], ctx_raw[:, u % 2, :], ACT.Copy)
                act.wait_ge(s_xn, i * BODY + u + 1)
                act.activation(xn_s[0][:, u, :], xn[:, u % XS, :], ACT.Copy)
                act.wait_ge(s_ctxT, 16)
                act.activation(val_s[0][:, u, :, :], ctxT_raw[:, :, bass.ds((i * BODY + u) * P, P)], ACT.Copy).then_inc(s_high, 1)
            act.wait_ge(s_out, i * NB + 1)
            operands(0)
            for j in range(STEPS + 2):
                if j < STEPS:
                    act.wait_ge(s_nbias, i * STEPS + j + 1)
                    if j >= 4:
                        act.wait_ge(s_probT, i * STEPS + j - 3)
                    act.activation(prob[:, j % 4, :], score_ps[j % 4][:, :], ACT.Exp, bias=nbias[:, j:j + 1],
                                   scale=SCALE, accum_out=total[:, j:j + 1]).then_inc(s_exp, 1)
                if j % 8 == 0 and j // 8 + 1 < BODY:
                    operands(j // 8 + 1)
                if j >= 2:
                    k = j - 2
                    act.wait_ge(s_probT, i * STEPS + k + 1)
                    if k >= 8:
                        act.wait_ge(s_out, i * NB + k // 4)
                    act.activation(probT_s[0][:, (k // 4) % 2, :, (k % 4) * P:(k % 4 + 1) * P],
                                   probT_ps[k % 2][:, :].rearrange("p (k n) -> p k n", k=KT), ACT.Copy).then_inc(s_hi, 1)
    ph.scalar = scalar

    def gpsimd(pool):
        pool.sem_inc(s_low, BODY)
        with pool.Fori(0, TURNS) as i:
            def low(u, part):
                if part == 0:
                    pool.wait_ge(s_high, i * BODY + u + 1)
                    pool.tensor_tensor(ctx_s[1][:, u, :], ctx_raw[:, u % 2, :], ctx_s[0][:, u, :].bitcast(F32), ALU.subtract)
                elif part == 1:
                    pool.tensor_tensor(xn_s[1][:, u, :], xn[:, u % XS, :], xn_s[0][:, u, :].bitcast(F32), ALU.subtract)
                else:
                    pool.tensor_tensor(val_s[1][:, u, :, :], ctxT_raw[:, :, bass.ds((i * BODY + u) * P, P)],
                                       val_s[0][:, u, :, :].bitcast(F32), ALU.subtract).then_inc(s_low, 1)

            def keep(u, h):
                if h == 1:
                    pool.wait_ge(s_low, BODY + i * BODY + u + 1)
                pool.tensor_copy(m.kvT[h][:, :, bass.ds((i * BODY + u) * P, P), 0], val_s[h][:, u, :, :].bitcast(F32)).then_inc(s_kv, 1)

            for part in range(3):
                low(0, part)
            for j in range(STEPS):
                pool.wait_ge(s_rt, i * STEPS + j + 1)
                pool.tensor_tensor(prob[:, j % 4, :], prob[:, j % 4, :], rtotal[:, j:j + 1].to_broadcast([P, D]), ALU.mult).then_inc(s_prob, 1)
                u, at = j // 8, j % 8
                if u + 1 < BODY and 1 <= at <= 3:
                    low(u + 1, at - 1)
                if at >= 6:
                    keep(u, at - 6)
    ph.gpsimd = gpsimd

    def vector(ve):
        order = Order(ve, s_ord)
        ve.wait_ge(s_x, 16)
        for t in range(NT):
            order.done(ve.bn_stats(m.stats[:, t, :], m.x[:, t, :]))
        finish_stats(ve, order, m, s_ln)
        with ve.Fori(0, TURNS) as i:
            order.loop(i, STEPS + NB)
            for u in range(BODY):
                t = i * BODY + u
                ve.wait_ge(s_low, (i + 1) * BODY + max(0, u - XS + 1))
                ve.tensor_scalar(xn[:, u % XS, :], m.x[:, bass.ds(t, 1), :].rearrange("p o n -> p (o n)"),
                                 m.mean[:, bass.ds(t, 1)], m.rstd[:, bass.ds(t, 1)],
                                 ALU.subtract, ALU.mult).then_inc(s_xn, 1)
            for j in range(STEPS + 5):
                if j < STEPS:
                    ve.wait_ge(s_score, i * STEPS + j + 1)
                    order.link(ve.tensor_reduce(mx[:, j:j + 1], score_ps[j % 4][:, :], AX.X, ALU.max))
                    ve.tensor_scalar(nbias[:, j:j + 1], mx[:, j:j + 1], -SCALE, None, ALU.mult).then_inc(s_nbias, 1)
                if 1 <= j <= STEPS:
                    ve.wait_ge(s_exp, i * STEPS + j)
                    ve.reciprocal(rtotal[:, j - 1:j], total[:, j - 1:j]).then_inc(s_rt, 1)
                if 3 <= j < STEPS + 3:
                    k = j - 3
                    ve.wait_ge(s_hi, i * STEPS + k + 1)
                    ve.tensor_tensor(probT_s[1][:, (k // 4) % 2, :, (k % 4) * P:(k % 4 + 1) * P],
                                     probT_ps[k % 2][:, :].rearrange("p (k n) -> p k n", k=KT),
                                     probT_s[0][:, (k // 4) % 2, :, (k % 4) * P:(k % 4 + 1) * P].bitcast(F32),
                                     ALU.subtract).then_inc(s_lo, 1)
                if j >= 10 and j % 4 == 2 or j == STEPS + 4:
                    b = (j - 9) // 4 if j < STEPS + 4 else NB - 1
                    rows = slice((b % 2) * C, (b % 2 + 1) * C)
                    t = i * BODY + b // 2
                    xt = m.x[rows, bass.ds(t, 1), :].rearrange("p o n -> p (o n)")
                    ve.wait_ge(s_out, i * NB + b + 2)
                    ve.tensor_tensor(xt, out_ps[b % 2][rows, :], xt, ALU.add).then_inc(s_add, 1)
                    ve.wait_ge(s_add, i * NB + b + 1)
                    order.done(ve.bn_stats(m.stats[rows, bass.ds(t, 1), :].rearrange("p o s -> p (o s)"), xt))
            order.end(TURNS)
        finish_stats(ve, order, m, m.s_ln[1])
    ph.vector = vector

    def tensor(pe):
        pe.wait_ge(m.s_ident, 16)
        pe.sem_inc(s_out, 1)
        with pe.Fori(0, TURNS) as i:
            def scores(j):
                b, r = j // 4, j % 4
                u, rows = b // 2, slice((b % 2) * C, (b % 2 + 1) * C)
                if j % 8 == 0:
                    pe.wait_ge(s_low, BODY + i * BODY + u + 1)
                if j >= 4:
                    pe.wait_ge(s_exp, i * STEPS + j - 3)
                products(pe, score_ps[j % 4][:, :], [c[rows, u, r * P:(r + 1) * P] for c in ctx_s],
                         [a[rows, u, :] for a in xn_s]).then_inc(s_score, 1)

            def transposes(j):
                pe.wait_ge(s_prob, i * STEPS + j + 1)
                if j >= 2:
                    pe.wait_ge(s_lo, i * STEPS + j - 1)
                for k in range(KT):
                    last = pe.transpose(probT_ps[j % 2][:, k * P:(k + 1) * P], prob[:, j % 4, k * P:(k + 1) * P], m.ident[:, :])
                last.then_inc(s_probT, 1)

            def values(b, k):
                if k == 0:
                    pe.wait_ge(s_lo, i * STEPS + 4 * b + 4)
                    if b >= 2:
                        pe.wait_ge(s_add, i * NB + b - 1)
                last = products(pe, out_ps[b % 2][:, :], [v[:, b // 2, k, :] for v in val_s],
                                [p[:, b % 2, k, :] for p in probT_s], first=(k == 0), last=(k == KT - 1))
                if k == KT - 1:
                    last.then_inc(s_out, 1)

            for j in range(3):
                scores(j)
            for j in range(STEPS):
                if j + 3 < STEPS:
                    scores(j + 3)
                transposes(j)
                if j >= 5:
                    values((j - 5) // 4, (j - 5) % 4)
            for j in range(STEPS - 5, STEPS):
                values(j // 4, j % 4)
    ph.tensor = tensor
    return ph


class TileFeed:

    def __init__(self, m, name, layer):
        self.m, self.layer = m, layer
        self.xn = m.sb(f"{name}_xn", [P, 2, D])
        self.xT = [m.sb(f"{name}_xT_{h}", [P, 2, KT, P], F32R) for h in ("high", "low")]
        self.ps = m.ps[0:2]
        self.s_xn, self.s_T = m.layer_sem(f"{name}_xn"), m.layer_sem(f"{name}_xn_turned")
        self.s_hi, self.s_lo = m.layer_sem(f"{name}_xT_high"), m.layer_sem(f"{name}_xT_low")
        self.s_used = m.layer_sem(f"{name}_xT_used")

    def normalise(self, ve, i, u):
        t = i * 2 + u
        ve.tensor_scalar(self.xn[:, u, :], self.m.x[:, bass.ds(t, 1), :].rearrange("p o n -> p (o n)"),
                         self.m.mean[:, bass.ds(t, 1)], self.m.rstd[:, bass.ds(t, 1)],
                         ALU.subtract, ALU.mult).then_inc(self.s_xn, 1)

    def low(self, ve, i, u):
        ve.wait_ge(self.s_hi, i * 2 + u + 1)
        ve.tensor_tensor(self.xT[1][:, u, :, :], self.ps[u][:, :].rearrange("p (k n) -> p k n", k=KT),
                         self.xT[0][:, u, :, :].bitcast(F32), ALU.subtract).then_inc(self.s_lo, 1)

    def high(self, act, i, u):
        act.wait_ge(self.s_T, i * 2 + u + 1)
        act.wait_ge(self.s_used, i * 2 + u + 1)
        act.activation(self.xT[0][:, u, :, :], self.ps[u][:, :].rearrange("p (k n) -> p k n", k=KT),
                       ACT.Copy).then_inc(self.s_hi, 1)

    def turn(self, pe, i, u):
        pe.wait_ge(self.s_xn, i * 2 + u + 1)
        for k in range(KT):
            last = pe.transpose(self.ps[u][:, k * P:(k + 1) * P], self.xn[:, u, k * P:(k + 1) * P], self.m.ident[:, :])
        last.then_inc(self.s_T, 1)


def clustered_linear(m):
    ph = Phase()
    NC, THRESHOLD, SHARPNESS = 64, 0.01, 10.0
    feed = TileFeed(m, "c0", 0)
    raw = m.raw[:, 0:KT * D].rearrange("p (k n) -> p k n", k=KT)
    rawc = m.raw[:, KT * D:KT * (D + NC)].rearrange("p (k n) -> p k n", k=KT)
    w = [m.sb(f"c0_w_{h}", [P, KT, D], F32R) for h in ("high", "low")]
    cen = [m.sb(f"c0_centroids_{h}", [P, KT, NC], F32R) for h in ("high", "low")]
    brow = m.sb("c0_bias_row", [1, D])
    bias = [m.sb(f"c0_bias_{h}", [1, D], F32R) for h in ("high", "low")]
    dense = m.sb("c0_dense", [P, NT, D])
    dots = m.sb("c0_dots", [P, NT, NC])
    prob = m.sb("c0_prob", [P, NT, NC])
    mx, tot, qsel = (m.sb(f"c0_{n}", [P, NT]) for n in ("max", "total", "row_hit"))
    owner = m.sb("c0_owner", [NC, D], I32)
    ownerf = m.sb("c0_owner_f", [NC, D])
    mine = m.sb("c0_partition", [NC, 1], I32)
    minef = m.sb("c0_partition_f", [NC, 1])
    onehot = m.sb("c0_onehot", [NC, D])
    chit = m.sb("c0_cluster_hit", [NC, 1])
    chitb = m.sb("c0_cluster_hit_wide", [NC, P])
    colsel = m.sb("c0_column_hit", [P, D])
    dot_ps, dense_ps, count_ps, col_ps = m.ps[2:4], m.ps[4:6], m.ps[6], m.ps[7]
    s_w, s_small, s_split, s_iota = m.layer_sem("c0_w_loaded"), m.layer_sem("c0_small_loaded"), m.layer_sem("c0_split"), m.layer_sem("c0_iota")
    s_dots, s_dotc, s_dense, s_densec = m.layer_sem("c0_dots_ready"), m.layer_sem("c0_dots_out"), m.layer_sem("c0_dense_ready"), m.layer_sem("c0_dense_out")
    s_wh = m.layer_sem("c0_weights_high")
    s_ord, s_shift, s_exp, s_hits = m.layer_sem("c0_dve_order"), m.layer_sem("c0_shifted"), m.layer_sem("c0_exp"), m.layer_sem("c0_hits")
    s_count, s_chit, s_col, s_colc, s_add = m.layer_sem("c0_count"), m.layer_sem("c0_chit"), m.layer_sem("c0_col"), m.layer_sem("c0_col_out"), m.layer_sem("c0_added")

    def sync(sp):
        sp.dma_start(raw, m.d["c0_w"].rearrange("(k p) n -> p k n", p=P)).then_inc(s_w, 16)
        sp.dma_start(rawc, m.d["c0_centroids"].rearrange("(k p) n -> p k n", p=P)).then_inc(s_w, 16)
        sp.wait_ge(m.s_ln[1], 1)
        sp.dma_start(brow[:, :], m.d["c0_bias"]).then_inc(s_small, 16)
        sp.dma_start(owner[:, :], m.d["c0_owner"].to_broadcast([NC, D])).then_inc(s_small, 16)
    ph.sync = sync

    def gpsimd(pool):
        pool.wait_ge(m.s_ln[1], 1)
        pool.iota(mine[:, :], [[0, 1]], base=0, channel_multiplier=1).then_inc(s_iota, 1)
        pool.wait_ge(s_wh, 1)
        pool.tensor_tensor(cen[1][:, :, :], rawc, cen[0][:, :, :].bitcast(F32), ALU.subtract).then_inc(s_split, 1)
        pool.wait_ge(s_wh, 2)
        pool.tensor_tensor(w[1][:, :, :], raw, w[0][:, :, :].bitcast(F32), ALU.subtract).then_inc(s_split, 1)
        pool.wait_ge(s_small, 32)
        pool.tensor_copy(bias[0][:, :], brow[:, :]).then_inc(s_split, 1)
        pool.wait_ge(s_split, 3)
        pool.tensor_tensor(bias[1][:, :], brow[:, :], bias[0][:, :].bitcast(F32), ALU.subtract).then_inc(s_split, 1)
        pool.tensor_copy(ownerf[:, :], owner[:, :]).then_inc(s_split, 1)
    ph.gpsimd = gpsimd

    def scalar(act):
        act.wait_ge(m.s_ln[1], 1)
        act.wait_ge(s_w, 32)
        act.activation(cen[0][:, :, :], rawc, ACT.Copy).then_inc(s_wh, 1)
        act.activation(w[0][:, :, :], raw, ACT.Copy).then_inc(s_wh, 1)
        with act.Fori(0, NT // 2) as i:
            for u in range(2):
                feed.high(act, i, u)
            for u in range(2):
                act.wait_ge(s_dense, i * 2 + u + 1)
                act.activation(dense[:, bass.ds(i * 2 + u, 1), :].rearrange("p o n -> p (o n)"), dense_ps[u][:, :], ACT.Copy).then_inc(s_densec, 1)
        act.wait_ge(s_shift, 1)
        act.activation(prob[:, :, :], prob[:, :, :], ACT.Exp, scale=SHARPNESS).then_inc(s_exp, 1)
        act.wait_ge(s_col, 1)
        act.activation(colsel[:, :], col_ps[:, :], ACT.Copy).then_inc(s_colc, 1)
    ph.scalar = scalar

    def vector(ve):
        order = Order(ve, s_ord)
        wide = lambda a: a[:, :].unsqueeze(2).broadcast_to([P, NT, NC])
        with ve.Fori(0, NT // 2) as i:
            order.loop(i, 0)
            for u in range(2):
                feed.normalise(ve, i, u)
            for u in range(2):
                feed.low(ve, i, u)
            for u in range(2):
                ve.wait_ge(s_dots, i * 2 + u + 1)
                ve.tensor_copy(dots[:, bass.ds(i * 2 + u, 1), :].rearrange("p o n -> p (o n)"), dot_ps[u][:, 0:NC]).then_inc(s_dotc, 1)
            order.end(NT // 2)
        ve.wait_ge(s_dotc, NT)
        order.link(ve.tensor_reduce(mx[:, :], dots[:, :, :], AX.X, ALU.max))
        ve.tensor_tensor(prob[:, :, :], dots[:, :, :], wide(mx), ALU.subtract).then_inc(s_shift, 1)
        ve.wait_ge(s_exp, 1)
        order.link(ve.tensor_reduce(tot[:, :], prob[:, :, :], AX.X, ALU.add))
        order.link(ve.reciprocal(mx[:, :], tot[:, :]))
        order.link(ve.tensor_tensor(prob[:, :, :], prob[:, :, :], wide(mx), ALU.mult))
        ve.tensor_scalar(prob[:, :, :], prob[:, :, :], THRESHOLD, None, ALU.is_gt).then_inc(s_hits, 1)
        ve.wait_ge(s_hits, 1)
        order.link(ve.tensor_reduce(qsel[:, :], prob[:, :, :], AX.X, ALU.max))
        ve.wait_ge(s_iota, 1)
        ve.wait_ge(s_split, 5)
        order.link(ve.tensor_copy(minef[:, :], mine[:, :]))
        ve.tensor_scalar(onehot[:, :], ownerf[:, :], minef[:, 0:1], None, ALU.is_equal).then_inc(s_chit, 1)
        ve.wait_ge(s_count, 1)
        order.link(ve.tensor_scalar(chit[:, :], count_ps[0:NC, 0:1], 0.5, None, ALU.is_gt))
        ve.tensor_copy(chitb[:, :], chit[:, 0:1].to_broadcast([NC, P])).then_inc(s_chit, 1)
        ve.wait_ge(s_colc, 1)
        ve.wait_ge(s_densec, NT)
        with ve.Fori(0, NT) as i:
            order.loop(i, 2)
            y = dense[:, bass.ds(i, 1), :].rearrange("p o n -> p (o n)")
            xt = m.x[:, bass.ds(i, 1), :].rearrange("p o n -> p (o n)")
            order.link(ve.scalar_tensor_tensor(y, y, qsel[:, bass.ds(i, 1)], colsel[:, :], ALU.mult, ALU.mult))
            ve.tensor_tensor(xt, xt, y, ALU.add).then_inc(s_add, 1)
            ve.wait_ge(s_add, i + 1)
            tile_stats(ve, order, m, i)
            order.end(NT)
        finish_stats(ve, order, m, m.s_ln[2])
    ph.vector = vector

    def tensor(pe):
        pe.sem_inc(feed.s_used, 2)
        with pe.Fori(0, NT // 2) as i:
            for u in range(2):
                feed.turn(pe, i, u)
            for u in range(2):
                pe.wait_ge(feed.s_lo, i * 2 + u + 1)
                pe.wait_ge(s_split, 1)
                for k in range(KT):
                    last = products(pe, dot_ps[u][:, 0:NC], [a[:, u, k, :] for a in feed.xT], [c[:, k, :] for c in cen],
                                    first=(k == 0), last=(k == KT - 1))
                last.then_inc(s_dots, 1)
                pe.wait_ge(s_split, 2)
                for k in range(KT):
                    products(pe, dense_ps[u][:, :], [a[:, u, k, :] for a in feed.xT], [c[:, k, :] for c in w],
                             first=(k == 0), last=False)
                pe.wait_ge(s_split, 4)
                pe.matmul(dense_ps[u][:, :], m.ones_row[:, :], bias[0][:, :], start=False, stop=False)
                pe.matmul(dense_ps[u][:, :], m.ones_row[:, :], bias[1][:, :], start=False, stop=True).then_inc(s_dense, 1)
                pe.wait_ge(s_dense, i * 2 + u + 1)
                pe.sem_inc(feed.s_used, 1)
        pe.wait_ge(s_hits, 1)
        for t in range(NT):
            last = pe.matmul(count_ps[0:NC, 0:1], prob[:, t, :], m.ones_col[:, :], start=(t == 0), stop=(t == NT - 1))
        last.then_inc(s_count, 1)
        pe.wait_ge(s_chit, 2)
        pe.matmul(col_ps[:, :], chitb[:, :], onehot[:, :], start=True, stop=True).then_inc(s_col, 1)
    ph.tensor = tensor
    return ph


def attention(m, rotary, n, layer):
    ph = Phase()
    G, HD, HG, KV = 8, 128, 4, 256
    STEPS = NT
    HALF = STEPS // 2
    HB = B // 2
    KW = 64 if rotary else 128
    EPS, ROOT = 1e-6, float(HD) ** -0.5
    MULT, CAP = 0.08838834764831845, 30.0

    q = [m.sb(f"{n}_q_{h}", [P, 2, HB, 2, P], F32R) for h in ("high", "low")]
    if rotary:
        qa, qb = (m.sb(f"{n}_q_{h}", [P, 2, HB * C]) for h in ("cos", "sin"))
        xn = qa
    else:
        qsq = m.sb(f"{n}_q_squared", [P, 2, HB, 2, P])
        xn = qsq[:, 0, 0:4, :, :].rearrange("p b h r -> p (b h r)").rearrange("p (u n) -> p u n", u=2)
    wq = [m.sb(f"{n}_wq_{h}", [P, KT, HG * HD], F32R) for h in ("high", "low")]
    wkv = [m.sb(f"{n}_wkv_{h}", [P, KT, KV], F32R) for h in ("high", "low")]
    wo = [m.sb(f"{n}_wo_{h}", [P, HG, D], F32R) for h in ("high", "low")]
    kn = m.sb(f"{n}_k", [P, 2, HD])
    kT = [m.sb(f"{n}_kT_{h}", [P, 2, P], F32R) for h in ("high", "low")]
    v = [m.sb(f"{n}_v_{h}", [P, 2, 2, HD], F32R) for h in ("high", "low")]
    prob = m.sb(f"{n}_prob", [P, 4, KW])
    pT = [m.sb(f"{n}_probT_{h}", [P, 512], F32R) for h in ("high", "low")]
    o = [m.sb(f"{n}_heads_{h}", [P, HG, 2, C], F32R) for h in ("high", "low")]
    vark, rk, halfk, tmpk = (m.sb(f"{n}_k_{h}", [P, 2]) for h in ("var", "rms", "half", "tmp"))
    if not rotary:
        varq, rq, halfq, tmpq = (m.sb(f"{n}_q_{h}", [P, HALF, 4]) for h in ("var", "rms", "half", "tmp"))
        bitsq = m.sb(f"{n}_q_bits", [P, HALF, 4], I32)
    mx, nb, tot, rt = (m.sb(f"{n}_{h}", [P, 4]) for h in ("max", "nbias", "total", "rtotal"))
    q_ps, kv_ps, kT_ps, s_ps, pT_ps, o_ps, y_ps = m.ps[0:2], m.ps[2], m.ps[3], m.ps[4], m.ps[5], m.ps[6], m.ps[7]

    raw_wq = m.raw[:, 0:2048].rearrange("p (k n) -> p k n", k=KT)
    raw_wkv = m.raw[:, 2048:3072].rearrange("p (k n) -> p k n", k=KT)
    raw_wo = m.raw[:, 3072:5120].rearrange("p (k n) -> p k n", k=HG)

    S = lambda h: m.layer_sem(f"{n}_{h}")
    l_wq, l_wkv, l_wo = S("wq_loaded"), S("wkv_loaded"), S("wo_loaded")
    t_wq = S("wq_split")
    t_wkv, t_wkvl = S("wkv_high"), S("wkv_low")
    t_wo, t_wol = S("wo_high"), S("wo_low")
    s_xn, s_xT, s_xh, s_xl = S("xn"), S("xn_turned"), S("xT_high"), S("xT_low")
    s_q, s_qh, s_qsq, s_ql = S("q"), S("q_high"), S("q_squared"), S("q_low")
    s_kv, s_kss, s_kn, s_vh, s_vl = S("kv"), S("k_sums"), S("k_normed"), S("v_high"), S("v_low")
    s_kt, s_kth, s_ktl, s_rq = S("kT"), S("kT_high"), S("kT_low"), S("q_rms")
    s_s, s_nb, s_e, s_rt, s_pn = S("scores"), S("nbias"), S("exp"), S("rtotal"), S("probs")
    s_pt, s_pth, s_ptl = S("probT"), S("probT_high"), S("probT_low")
    s_pv, s_pv0, s_oh, s_ol, s_wo, s_add = S("heads"), S("heads_first_batch"), S("heads_high"), S("heads_low"), S("projected"), S("added")
    s_ord, s_vq, s_qs = S("dve_order"), S("q_var"), S("q_sums")
    s_th, s_mk, s_qc, s_qr = S("tanh"), S("masked"), S("q_cos_sin"), S("q_turned")

    if rotary:
        cosT, sinT = (m.sb(f"{n}_{h}T", [P, C]) for h in ("cos", "sin"))
        cosk, sink = (m.sb(f"{n}_{h}", [P, HD]) for h in ("cos", "sin"))
        ka, kb = (m.sb(f"{n}_k_{h}", [P, HD]) for h in ("cos", "sin"))
        mask_in, mask = m.sb(f"{n}_mask_in", [P, C], mybir.dt.uint8), m.sb(f"{n}_mask", [P, C])
        maskT_in, maskT = m.sb(f"{n}_maskT_in", [C, C], mybir.dt.uint8), m.sb(f"{n}_maskT", [C, C])
        anyq, none = m.sb(f"{n}_any", [P, C]), m.sb(f"{n}_none", [P, 1])
        onesw = m.sb(f"{n}_ones", [C, P])
        s_tab, s_mT, s_any = S("tables_loaded"), S("maskT_ready"), S("any_key")
    else:
        nw = m.sb(f"{n}_norm_w", [P, 2])
        wqk = m.sb(f"{n}_norm_w_product", [P, 1])
        s_tab = S("norm_w_loaded")

    m.raw_taken = [(t_wq, G * 2 * HG), (t_wkvl, G)]

    def step(g, s):
        return g * STEPS + s + 1

    def chunk(g, c):
        return g * 8 + c + 1

    def next_step(g, s, more):
        return (g, s + 1) if s + 1 < STEPS else (g + 1, 0) if more else None

    def before(g, s, back, first):
        return (g, s - back) if s >= back else None if first else (g - 1, s - back + STEPS)

    def next_chunk(g, s, more):
        return (g, 4 + s) if s < 4 else (g + 1, s - 4) if more else None

    def divide(eng, g, s):
        eng.wait_ge(s_rt, step(g, s))
        eng.tensor_tensor(prob[:, :, :], prob[:, :, :], rt[:, :].unsqueeze(2).broadcast_to([P, 4, KW]), ALU.mult).then_inc(s_pn, 1)

    def sync(sp):
        w_d = m.d[f"{n}_w"]
        if rotary:
            sp.wait_ge(m.s_ln[layer], 1)
            for dst, src in ((cosT, "cosT"), (sinT, "sinT"), (cosk, "cosk"), (sink, "sink")):
                sp.dma_start(dst[:, :], m.d[src]).then_inc(s_tab, 16)
            for r in range(2):
                sp.dma_start(mask_in[r * C:(r + 1) * C, :], m.d["mask"]).then_inc(s_tab, 16)
            sp.dma_start(maskT_in[:, :], m.d["maskT"]).then_inc(s_tab, 16)
        else:
            sp.wait_ge(m.s_ln[layer], 1)
            sp.dma_start(nw[:, :], m.d[f"{n}_norm_w"]).then_inc(s_tab, 16)

        def loads(g):
            for a, b, done in ((0, 2048, l_wq), (2048, 3072, l_wkv), (3072, 5120, l_wo)):
                src = (w_d[g] if isinstance(g, int) else w_d[bass.ds(g, 1)].rearrange("o p n -> (o p) n"))[:, a:b]
                yield m.raw[:, a:b], src, done

        for dst, src, done in loads(0):
            sp.dma_start(dst, src).then_inc(done, 16)
        with sp.Fori(0, G - 1) as g:
            for (dst, src, done), (split, per) in zip(loads(g + 1), ((t_wq, 2 * HG), (t_wkvl, 1), (t_wol, HG))):
                sp.wait_ge(split, (g + 1) * per)
                sp.dma_start(dst, src).then_inc(done, 16)
    ph.sync = sync

    def gpsimd(pool):
        def split_wq(g, h):
            c = slice(h * HD, (h + 1) * HD)
            if h == 0:
                pool.wait_ge(l_wq, (g + 1) * 16)
            pool.wait_ge(s_q, g * 8 + 5 + h)
            pool.tensor_tensor(wq[0][:, :, c], raw_wq[:, :, c], m.zero[:, 0:1].unsqueeze(2).broadcast_to([P, KT, HD]), ALU.add).then_inc(t_wq, 1)
            pool.wait_ge(t_wq, g * 2 * HG + 2 * h + 1)
            pool.tensor_tensor(wq[1][:, :, c], raw_wq[:, :, c], wq[0][:, :, c].bitcast(F32), ALU.subtract).then_inc(t_wq, 1)

        def low_wkv(g):
            pool.wait_ge(t_wkv, g + 1)
            pool.tensor_tensor(wkv[1][:, :, :], raw_wkv, wkv[0][:, :, :].bitcast(F32), ALU.subtract).then_inc(t_wkvl, 1)

        def low_wo(g, h):
            pool.wait_ge(t_wo, g * HG + h + 1)
            pool.tensor_tensor(wo[1][:, h, :], raw_wo[:, h, :], wo[0][:, h, :].bitcast(F32), ALU.subtract).then_inc(t_wol, 1)

        def group(g, first=False, more=True):
            for s in range(STEPS):
                if s == 1 and not first:
                    low_wo(g, 0)
                if not rotary:
                    divide(pool, g, s)
                if s == 1 and not first:
                    for h in range(1, HG):
                        low_wo(g, h)
                if more and s == 6:
                    low_wkv(g + 1)
                if rotary and next_chunk(g, s, more):
                    turn_q(*next_chunk(g, s, more))
                if more and s < 4:
                    split_wq(g + 1, s)

        def turn_q(g, c):
            half, h, k = c // 4, c % 4, c % 2
            qv = qa[:, k, :].rearrange("p (b r) -> p b r", b=HB)
            pool.wait_ge(s_qc, chunk(g, c))
            pool.tensor_tensor(qa[:, k, :], qa[:, k, :], qb[:, k, :], ALU.add).then_inc(s_qr, 1)
            pool.wait_ge(s_qh, chunk(g, c))
            dst = [a[:, half, :, h // 2, (h % 2) * C:(h % 2 + 1) * C] for a in q]
            pool.tensor_tensor(dst[1], qv, dst[0].bitcast(F32), ALU.subtract).then_inc(s_ql, 1)

        pool.wait_ge(m.s_ln[layer], 1)
        for h in range(HG):
            split_wq(0, h)
        low_wkv(0)
        for h in range(HG):
            low_wo(0, h)
        if rotary:
            for c in range(4):
                turn_q(0, c)
        group(0, first=True)
        with pool.Fori(1, G - 1) as g:
            group(g)
        group(G - 1, more=False)
    ph.gpsimd = gpsimd

    def scalar(act):
        with act.Fori(0, NT // 2) as i:
            for u in range(2):
                act.wait_ge(s_xT, i * 2 + u + 1)
                act.activation(m.kvT[0][:, :, bass.ds((i * 2 + u) * P, P), 1], q_ps[u][:, :].rearrange("p (k t) -> p k t", k=KT),
                               ACT.Copy).then_inc(s_xh, 1)

        def high_q(g, c):
            half, h = c // 4, c % 4
            dst = q[0][:, half, :, h // 2, (h % 2) * C:(h % 2 + 1) * C]
            if rotary:
                act.wait_ge(s_qr, chunk(g, c))
                act.activation(dst, qa[:, c % 2, :].rearrange("p (b r) -> p b r", b=HB), ACT.Copy).then_inc(s_qh, 1)
            else:
                act.wait_ge(s_q, chunk(g, c) + 8)
                src = q_ps[c % 2][:, :].rearrange("p (b r) -> p b r", b=HB)
                act.activation(dst, src, ACT.Copy).then_inc(s_qh, 1)
                act.activation(qsq[:, half, :, h // 2, (h % 2) * C:(h % 2 + 1) * C], src, ACT.Square).then_inc(s_qsq, 1)

        def kv_parts(g, s):
            act.wait_ge(s_kv, step(g, s) + STEPS)
            if not rotary:
                for b in range(2):
                    last = act.activation(kn[:, b, :], kv_ps[:, b * KV:b * KV + HD], ACT.Square, accum_out=vark[:, b:b + 1])
                last.then_inc(s_kss, 1)
                src = kv_ps[:, :].rearrange("p (b w) -> p b w", b=2)[:, :, HD:KV]
                act.activation(v[0][:, s % 2, :, :], src, ACT.Copy).then_inc(s_vh, 1)
            else:
                act.activation(v[0][:, s % 2, 0, :], kv_ps[:, HD:KV], ACT.Copy).then_inc(s_vh, 1)

        def high_kT(g, s):
            act.wait_ge(s_kt, step(g, s))
            if rotary:
                act.activation(kT[0][:, 0, :], kT_ps[:, 0:P], ACT.Copy).then_inc(s_kth, 1)
            else:
                act.activation(kT[0][:, :, :], kT_ps[:, 0:2 * P].rearrange("p (b t) -> p b t", b=2), ACT.Copy,
                               scale=wqk[:, 0:1]).then_inc(s_kth, 1)

        if not rotary:
            act.wait_ge(s_rq, 1)
        def heads_high(g, s):
            act.wait_ge(s_pv, step(g, s))
            act.activation(o[0][:, :, :, :].rearrange("p h b r -> p b h r"),
                           o_ps[:, :].rearrange("p (b h r) -> p b h r", b=2, h=HG), ACT.Copy).then_inc(s_oh, 1)

        def high_wkv(g):
            act.wait_ge(l_wkv, (g + 1) * 16)
            act.activation(wkv[0][:, :, :], raw_wkv, ACT.Copy).then_inc(t_wkv, 1)

        def high_wo(g, heads):
            if heads[0] == 0:
                act.wait_ge(l_wo, (g + 1) * 16)
                act.wait_ge(s_wo, g * STEPS + STEPS)
            for h in heads:
                act.activation(wo[0][:, h, :], raw_wo[:, h, :], ACT.Copy).then_inc(t_wo, 1)

        def group(g, first=False, more=True):
            for s in range(STEPS):
                ahead, queries_of = next_step(g, s, more), next_chunk(g, s, more)
                if s == 1 and not first:
                    high_wo(g, (0, 1))
                if rotary:
                    act.wait_ge(s_s, step(g, s))
                    act.activation(prob[:, :, :], s_ps[:, 0:4 * KW].rearrange("p (j k) -> p j k", j=4), ACT.Tanh,
                                   scale=MULT / CAP).then_inc(s_th, 1)
                    act.wait_ge(s_mk, step(g, s))
                    act.activation(prob[:, :, :], prob[:, :, :], ACT.Exp, scale=CAP).then_inc(s_e, 1)
                else:
                    act.wait_ge(s_nb, step(g, s))
                    for j in range(4):
                        last = act.activation(prob[:, j, :], s_ps[:, j * KW:(j + 1) * KW], ACT.Exp, bias=nb[:, j:j + 1],
                                              scale=rq[:, s % HALF, j:j + 1], accum_out=tot[:, j:j + 1])
                    last.then_inc(s_e, 1)
                if s == 1 and not first:
                    high_wo(g, (2, 3))
                if ahead:
                    kv_parts(*ahead)
                if more and s == 6:
                    high_wkv(g + 1)
                if queries_of and not rotary:
                    high_q(*queries_of)
                cols = 4 * KW
                act.wait_ge(s_pt, step(g, s))
                act.activation(pT[0][:, 0:cols], pT_ps[:, 0:cols], ACT.Copy).then_inc(s_pth, 1)
                if ahead:
                    high_kT(*ahead)
                if queries_of and rotary:
                    high_q(*queries_of)
                heads_high(g, s)

        high_wkv(0)
        high_wo(0, range(HG))
        for c in range(4):
            high_q(0, c)
        kv_parts(0, 0)
        high_kT(0, 0)
        group(0, first=True)
        with act.Fori(1, G - 1) as g:
            group(g)
        group(G - 1, more=False)
    ph.scalar = scalar

    def vector(ve):
        order = Order(ve, s_ord)
        with ve.Fori(0, NT // 2) as i:
            order.loop(i, 0)
            for u in range(2):
                t = i * 2 + u
                ve.tensor_scalar(xn[:, u, :], m.x[:, bass.ds(t, 1), :].rearrange("p o n -> p (o n)"),
                                 m.mean[:, bass.ds(t, 1)], m.rstd[:, bass.ds(t, 1)], ALU.subtract, ALU.mult).then_inc(s_xn, 1)
            for u in range(2):
                ve.wait_ge(s_xh, i * 2 + u + 1)
                ve.tensor_tensor(m.kvT[1][:, :, bass.ds((i * 2 + u) * P, P), 1], q_ps[u][:, :].rearrange("p (k t) -> p k t", k=KT),
                                 m.kvT[0][:, :, bass.ds((i * 2 + u) * P, P), 1].bitcast(F32), ALU.subtract).then_inc(s_xl, 1)
            order.end(NT // 2)
        ve.wait_ge(s_tab, 16 * 7 if rotary else 16)
        if rotary:
            ve.memset(onesw[:, :], 1.0).then_inc(s_mT, 1)
            ve.tensor_copy(maskT[:, :], maskT_in[:, :]).then_inc(s_mT, 1)
            order.link(ve.tensor_copy(mask[:, :], mask_in[:, :]))
            order.link(ve.tensor_reduce(none[:, :], mask[:, :], AX.X, ALU.max))
            order.link(ve.tensor_scalar(none[:, :], none[:, :], -1.0, 1.0, ALU.mult, ALU.add))
            order.link(ve.tensor_scalar(mask[:, :], mask[:, :], none[:, 0:1], -1.0, ALU.max, ALU.add))
            ve.tensor_scalar(mask[:, :], mask[:, :], 1e30, None, ALU.mult).then_inc(s_any, 1)
            ve.wait_ge(s_any, 2)
            order.link(ve.tensor_scalar(anyq[:, :], kT_ps[:, 0:C], 0.5, None, ALU.is_gt))
            order.link(ve.tensor_tensor(cosT[:, :], cosT[:, :], anyq[:, :], ALU.mult))
            ve.tensor_tensor(sinT[:, :], sinT[:, :], anyq[:, :], ALU.mult).then_inc(s_any, 1)
            ve.wait_ge(s_any, 3)
        else:
            ve.scalar_tensor_tensor(wqk[:, :], nw[:, 0:1], ROOT, nw[:, 1:2], ALU.mult, ALU.mult).then_inc(s_rq, 1)

        def low_q(g, c):
            half, h = c // 4, c % 4
            src = q_ps[c % 2][:, :].rearrange("p (b r) -> p b r", b=HB)
            if rotary:
                low, high = slice(0, C), slice(C, P)
                a, b = (t[:, c % 2, :].rearrange("p (b r) -> p b r", b=HB) for t in (qa, qb))
                ve.wait_ge(s_q, chunk(g, c) + 8)
                ve.wait_ge(s_ql, chunk(g, c) - 2 + 2)
                ve.tensor_tensor(a, src, cosT[:, :].unsqueeze(1).broadcast_to([P, HB, C]), ALU.mult)
                ve.tensor_tensor(b[low], src[high], sinT[high, :].unsqueeze(1).broadcast_to([C, HB, C]), ALU.mult)
                ve.tensor_tensor(b[high], src[low], sinT[low, :].unsqueeze(1).broadcast_to([C, HB, C]), ALU.mult).then_inc(s_qc, 1)
            else:
                dst = [a[:, half, :, h // 2, (h % 2) * C:(h % 2 + 1) * C] for a in q]
                ve.wait_ge(s_qsq, chunk(g, c))
                ve.tensor_tensor(dst[1], src, dst[0].bitcast(F32), ALU.subtract).then_inc(s_ql, 1)

        def norm_k(g, s):
            if rotary:
                ve.wait_ge(s_vh, step(g, s))
                ve.tensor_tensor(ka[:, :], kv_ps[:, 0:HD], cosk[:, :], ALU.mult)
                half = HD // 2
                ve.tensor_tensor(kb[:, 0:half], kv_ps[:, half:HD], sink[:, 0:half], ALU.mult)
                order.link(ve.tensor_tensor(kb[:, half:HD], kv_ps[:, 0:half], sink[:, half:HD], ALU.mult))
                ve.tensor_tensor(kn[:, 0, :], ka[:, :], kb[:, :], ALU.add).then_inc(s_kn, 1)
                ve.tensor_tensor(v[1][:, s % 2, 0, :], kv_ps[:, HD:KV], v[0][:, s % 2, 0, :].bitcast(F32), ALU.subtract).then_inc(s_vl, 1)
            else:
                ve.wait_ge(s_kss, step(g, s))
                order.link(ve.tensor_scalar(vark[:, :], vark[:, :], 1.0 / HD, EPS, ALU.mult, ALU.add))
                rsqrt(ve, order, rk[:, :], vark[:, :], m.bits[:, 0:2], halfk[:, :], tmpk[:, :])
                src = kv_ps[:, :].rearrange("p (b w) -> p b w", b=2)
                ve.wait_ge(s_vh, step(g, s))
                ve.tensor_tensor(kn[:, :, :], src[:, :, 0:HD], rk[:, :].unsqueeze(2).broadcast_to([P, 2, HD]), ALU.mult).then_inc(s_kn, 1)
                ve.tensor_tensor(v[1][:, s % 2, :, :], src[:, :, HD:KV], v[0][:, s % 2, :, :].bitcast(F32), ALU.subtract).then_inc(s_vl, 1)

        def low_kT(g, s):
            ve.wait_ge(s_kth, step(g, s))
            if rotary:
                ve.tensor_tensor(kT[1][:, 0, :], kT_ps[:, 0:P], kT[0][:, 0, :].bitcast(F32), ALU.subtract).then_inc(s_ktl, 1)
            else:
                ve.scalar_tensor_tensor(kT[1][:, :, :], kT_ps[:, 0:2 * P].rearrange("p (b t) -> p b t", b=2), wqk[:, 0:1],
                                        kT[0][:, :, :].bitcast(F32), ALU.mult, ALU.subtract).then_inc(s_ktl, 1)

        def norm_q(g, half):
            ve.wait_ge(s_qs, g * 2 + half + 1)
            src = s_ps[:, 0:4 * HALF].rearrange("p (s j) -> p s j", j=4)
            ve.tensor_scalar(varq[:, :, :], src, 1.0 / HD, EPS, ALU.mult, ALU.add).then_inc(s_vq, 1)
            ve.wait_ge(s_vq, g * 2 + half + 1)
            rsqrt(ve, order, rq[:, :, :], varq[:, :, :], bitsq[:, :, :], halfq[:, :, :], tmpq[:, :, :])

        def heads_low(g, s):
            ve.wait_ge(s_oh, step(g, s))
            ve.tensor_tensor(o[1][:, :, :, :].rearrange("p h b r -> p b h r"),
                             o_ps[:, :].rearrange("p (b h r) -> p b h r", b=2, h=HG),
                             o[0][:, :, :, :].rearrange("p h b r -> p b h r").bitcast(F32), ALU.subtract).then_inc(s_ol, 1)

        def add(g, s):
            ve.wait_ge(s_wo, step(g, s) + STEPS)
            ve.tensor_tensor(m.x[:, s, :], m.x[:, s, :], y_ps[:, :], ALU.add).then_inc(s_add, 1)
            if isinstance(g, int) and g == G - 1:
                ve.wait_ge(s_add, step(g, s))
                tile_stats(ve, order, m, s)

        def group(g, first=False, more=True):
            for s in range(STEPS):
                ahead, queries_of = next_step(g, s, more), next_chunk(g, s, more)
                if not rotary:
                    ve.wait_ge(s_s, step(g, s))
                    order.link(ve.tensor_reduce(mx[:, :], s_ps[:, :].rearrange("p (j k) -> p j k", j=4), AX.X, ALU.max))
                    ve.scalar_tensor_tensor(nb[:, :], mx[:, :], -1.0, rq[:, s % HALF, :], ALU.mult, ALU.mult).then_inc(s_nb, 1)
                else:
                    ve.wait_ge(s_th, step(g, s))
                    ve.tensor_tensor(prob[:, :, :], prob[:, :, :], mask[:, :].unsqueeze(1).broadcast_to([P, 4, KW]), ALU.add).then_inc(s_mk, 1)
                if before(g, s, 1, first):
                    heads_low(*before(g, s, 1, first))
                if before(g, s, 2, first):
                    add(*before(g, s, 2, first))
                ve.wait_ge(s_e, step(g, s))
                if rotary:
                    order.link(ve.tensor_reduce(tot[:, :], prob[:, :, :], AX.X, ALU.add))
                ve.reciprocal(rt[:, :], tot[:, :]).then_inc(s_rt, 1)
                if rotary:
                    divide(ve, g, s)
                    if queries_of:
                        low_q(*queries_of)
                if ahead:
                    norm_k(*ahead)
                if queries_of and not rotary:
                    low_q(*queries_of)
                cols = 4 * KW
                ve.wait_ge(s_pth, step(g, s))
                ve.tensor_tensor(pT[1][:, 0:cols], pT_ps[:, 0:cols], pT[0][:, 0:cols].bitcast(F32), ALU.subtract).then_inc(s_ptl, 1)
                if ahead:
                    low_kT(*ahead)
                if not rotary and s == HALF - 1:
                    norm_q(g, 1)
                if not rotary and s == STEPS - 1 and more:
                    norm_q(g + 1, 0)

        for c in range(4):
            low_q(0, c)
        norm_k(0, 0)
        low_kT(0, 0)
        if not rotary:
            norm_q(0, 0)
        group(0, first=True)
        with ve.Fori(1, G - 1) as g:
            order.loop(g, STEPS * 2 if rotary else STEPS * (RSQRT_LINKS + 2) + 2 * RSQRT_LINKS, start=1)
            group(g)
            order.end(G - 2)
        group(G - 1, more=False)
        add(G - 1, STEPS - 2)
        heads_low(G - 1, STEPS - 1)
        add(G - 1, STEPS - 1)
        finish_stats(ve, order, m, m.s_ln[layer + 1])
    ph.vector = vector

    def tensor(pe):
        pe.sem_inc(s_q, 8)
        pe.sem_inc(s_kv, STEPS)
        pe.sem_inc(s_wo, STEPS)
        with pe.Fori(0, NT // 2) as i:
            for u in range(2):
                pe.wait_ge(s_xn, i * 2 + u + 1)
                for k in range(KT):
                    last = pe.transpose(q_ps[u][:, k * P:(k + 1) * P], xn[:, u, k * P:(k + 1) * P], m.ident[:, :])
                last.then_inc(s_xT, 1)
        if rotary:
            pe.sem_inc(s_ql, 2)
            pe.wait_ge(s_mT, 2)
            pe.matmul(kT_ps[:, 0:C], onesw[:, :], maskT[:, :], start=True, stop=True).then_inc(s_any, 1)
            pe.wait_ge(s_any, 3)
        pe.wait_ge(s_xl, NT)
        pe.wait_ge(m.s_kv_ctx, m.kv_ctx_all)

        def queries(g, c):
            half, h = c // 4, c % 4
            if c < 4:
                pe.wait_ge(t_wq, g * 2 * HG + 2 * h + 2)
            if c >= 2 or not (isinstance(g, int) and g == 0):
                pe.wait_ge(s_qc if rotary else s_ql, chunk(g, c - 2))
            for k in range(KT):
                last = products(pe, q_ps[c % 2][:, :], [w[:, k, h * HD:(h + 1) * HD] for w in wq],
                                [a[:, k, half * 512:(half + 1) * 512, 1] for a in m.kvT], first=(k == 0), last=(k == KT - 1))
            last.then_inc(s_q, 1)

        def keys_values(g, s):
            if s == 0:
                pe.wait_ge(t_wkvl, g + 1)
            if s or not (isinstance(g, int) and g == 0):
                pe.wait_ge(s_vl, step(g, s - 1))
            if rotary:
                for k in range(KT):
                    last = products(pe, kv_ps[:, 0:KV], [a[:, k, s * P:(s + 1) * P, 0] for a in m.kvT],
                                    [w[:, k, :] for w in wkv], first=(k == 0), last=(k == KT - 1))
            else:
                for b in range(2):
                    r = slice((2 * s + b) * C, (2 * s + b + 1) * C)
                    for k in range(KT):
                        last = products(pe, kv_ps[:, b * KV:(b + 1) * KV],
                                        [a[:, k, r, :].rearrange("p r j -> p (r j)") for a in m.kvT],
                                        [w[:, k, :] for w in wkv], first=(k == 0), last=(k == KT - 1))
            last.then_inc(s_kv, 1)

        def turn_keys(g, s):
            pe.wait_ge(s_kn, step(g, s))
            if rotary:
                pe.transpose(kT_ps[:, 0:P], kn[:, 0, :], m.ident[:, :]).then_inc(s_kt, 1)
            else:
                for b in range(2):
                    last = pe.transpose(kT_ps[:, b * P:(b + 1) * P], kn[:, b, :], m.ident[:, :])
                last.then_inc(s_kt, 1)

        def query_sums(g, half, of):
            if of == 0:
                pe.wait_ge(s_qsq, chunk(g, 4 * half + 3))
            for j in range(4):
                at = 4 * of + j
                last = pe.matmul(s_ps[:, at:at + 1], qsq[:, half, 2 * of + j // 2, j % 2, :], m.ones_col[:, :], start=True, stop=True)
            if of == HALF - 1:
                last.then_inc(s_qs, 1)

        def scores(g, s):
            if s % 4 == 0:
                pe.wait_ge(s_ql, chunk(g, 4 * (s // 4) + 3) + (2 if rotary else 0))
                if not rotary:
                    pe.wait_ge(s_vq, g * 2 + s // HALF + 1)
            pe.wait_ge(s_ktl, step(g, s))
            for b in range(2):
                for hp in range(2):
                    at = (hp * 2 + b) if rotary else (b * 2 + hp)
                    last = products(pe, s_ps[:, at * KW:(at + 1) * KW], [a[:, s // 4, 2 * (s % 4) + b, hp, :] for a in q],
                                    [a[:, 0, b * C:(b + 1) * C] if rotary else a[:, b, :] for a in kT])
            last.then_inc(s_s, 1)

        def turn_probs(g, s):
            pe.wait_ge(s_pn, step(g, s))
            for j in range(2 if rotary else 4):
                src = prob[:, 2 * j:2 * j + 2, :].rearrange("p b k -> p (b k)") if rotary else prob[:, j, :]
                last = pe.transpose(pT_ps[:, j * P:(j + 1) * P], src, m.ident[:, :])
            last.then_inc(s_pt, 1)

        def heads(g, s):
            pe.wait_ge(s_vl, step(g, s))
            pe.wait_ge(s_ptl, step(g, s))
            for b in range(2):
                if rotary:
                    r = slice(b * C, (b + 1) * C)
                    if b:
                        pe.wait_ge(s_pv0, step(g, s))
                    last = products(pe, o_ps[:, b * 256:(b + 1) * 256], [a[r, s % 2, 0, :] for a in v], [a[r, 0:256] for a in pT])
                    if not b:
                        last.then_inc(s_pv0, 1)
                else:
                    last = products(pe, o_ps[:, b * 256:(b + 1) * 256], [a[:, s % 2, b, :] for a in v],
                                    [a[:, b * 256:(b + 1) * 256] for a in pT])
            last.then_inc(s_pv, 1)

        def project(g, s, heads):
            if heads[0] == 0:
                pe.wait_ge(s_ol, step(g, s))
                if s or not (isinstance(g, int) and g == 0):
                    pe.wait_ge(s_add, step(g, s - 1))
            for h in heads:
                if s == 0:
                    pe.wait_ge(t_wol, g * HG + h + 1)
                last = products(pe, y_ps[:, :], [a[:, h, :, :].rearrange("p b r -> p (b r)") for a in o],
                                [w[:, h, :] for w in wo], first=(h == 0), last=(h == HG - 1))
            if heads[-1] == HG - 1:
                last.then_inc(s_wo, 1)

        def group(g, first=False, more=True):
            for s in range(STEPS):
                ahead, last_step, queries_of = next_step(g, s, more), before(g, s, 1, first), next_chunk(g, s, more)
                scores(g, s)
                if queries_of and rotary:
                    queries(*queries_of)
                if ahead:
                    keys_values(*ahead)
                if queries_of and not rotary:
                    queries(*queries_of)
                turn_probs(g, s)
                if last_step:
                    project(*last_step, (0, 1))
                if ahead:
                    turn_keys(*ahead)
                if not rotary and s % HALF == HALF - 1 and queries_of:
                    of = (g, 1) if s < HALF else (g + 1, 0)
                    query_sums(*of, 0)
                    project(*last_step, (2,))
                    query_sums(*of, 1)
                    query_sums(*of, 2)
                    project(*last_step, (3,))
                    query_sums(*of, 3)
                elif last_step:
                    project(*last_step, (2, 3))
                heads(g, s)

        for c in range(4):
            queries(0, c)
        keys_values(0, 0)
        turn_keys(0, 0)
        if not rotary:
            for of in range(HALF):
                query_sums(0, 0, of)
        group(0, first=True)
        with pe.Fori(1, G - 1) as g:
            group(g)
        group(G - 1, more=False)
        project(G - 1, STEPS - 1, range(HG))
    ph.tensor = tensor
    return ph


def latent_attention(m):
    return attention(m, False, "a1", 2)


def rotary_attention(m):
    return attention(m, True, "a2", 4)


def ranked_linear(m):
    ph = Phase()
    RANKS, RG = (0, 8, 16, 32, 64), 68
    MR = RANKS[-1]
    raw_taken = m.raw_taken
    feed = TileFeed(m, "r1", 3)
    raw = m.raw[:, 0:KT * D].rearrange("p (k n) -> p k n", k=KT)
    rawa = m.raw[:, KT * D:KT * (D + RG)].rearrange("p (k n) -> p k n", k=KT)
    w = [m.sb(f"r1_w_{h}", [P, KT, D], F32R) for h in ("high", "low")]
    ag = [m.sb(f"r1_a_gate_{h}", [P, KT, RG], F32R) for h in ("high", "low")]
    rawb = m.sb("r1_b_raw", [MR + 1, D])
    bb = [m.sb(f"r1_b_{h}", [MR + 1, D], F32R) for h in ("high", "low")]
    gb = m.sb("r1_gate_b", [P, 4])
    sc, eq, cum, ex = (m.sb(f"r1_{n}", [P, 2, 4]) for n in ("scores", "is_best", "taken", "exp"))
    best, nbest, total, top, weight = (m.sb(f"r1_{n}", [P, 2]) for n in ("best", "nbest", "total", "top", "weight"))
    ranked = m.sb("r1_ranked", [P, 2, P])
    rT = [m.sb(f"r1_rankedT_{h}", [MR + 1, 2, P], F32R) for h in ("high", "low")]
    hg_ps, y_ps, rT_ps = m.ps[2:4], m.ps[4:6], m.ps[6:8]
    S = lambda h: m.layer_sem(f"r1_{h}")
    s_w, s_small, s_split, s_init, s_wh = S("w_loaded"), S("small_loaded"), S("split"), S("init"), S("weights_high")
    s_hg, s_nb, s_ex, s_rk, s_rT, s_rh, s_rl = S("hg"), S("nbest"), S("exp"), S("ranked"), S("rankedT"), S("rankedT_high"), S("rankedT_low")
    s_y, s_add, s_ord = S("y"), S("added"), S("dve_order")

    def sync(sp):
        for taken, count in raw_taken:
            sp.wait_ge(taken, count)
        sp.dma_start(raw, m.d["r1_w"].rearrange("(k p) n -> p k n", p=P)).then_inc(s_w, 16)
        sp.dma_start(rawa, m.d["r1_a_gate"].rearrange("(k p) n -> p k n", p=P)).then_inc(s_w, 16)
        sp.wait_ge(m.s_ln[3], 1)
        sp.dma_start(rawb[:, :], m.d["r1_b"]).then_inc(s_small, 16)
        sp.dma_start(gb[:, :], m.d["r1_gate_b"].to_broadcast([P, 4])).then_inc(s_small, 16)
    ph.sync = sync

    def gpsimd(pool):
        pool.wait_ge(m.s_ln[3], 1)
        for h, value in ((0, 1.0), (1, 0.0)):
            pool.memset(rT[h][MR:MR + 1, :, :].bitcast(F32), value).then_inc(s_init, 1)
        pool.wait_ge(s_init, 2)
        pool.wait_ge(s_wh, 1)
        pool.tensor_tensor(ag[1][:, :, :], rawa, ag[0][:, :, :].bitcast(F32), ALU.subtract).then_inc(s_split, 1)
        pool.wait_ge(s_wh, 2)
        pool.tensor_tensor(w[1][:, :, :], raw, w[0][:, :, :].bitcast(F32), ALU.subtract).then_inc(s_split, 1)
        pool.wait_ge(s_wh, 3)
        pool.tensor_tensor(bb[1][:, :], rawb[:, :], bb[0][:, :].bitcast(F32), ALU.subtract).then_inc(s_split, 1)
    ph.gpsimd = gpsimd

    def scalar(act):
        act.wait_ge(m.s_ln[3], 1)
        act.wait_ge(s_w, 32)
        act.activation(ag[0][:, :, :], rawa, ACT.Copy).then_inc(s_wh, 1)
        act.activation(w[0][:, :, :], raw, ACT.Copy).then_inc(s_wh, 1)
        act.wait_ge(s_small, 32)
        act.activation(bb[0][:, :], rawb[:, :], ACT.Copy).then_inc(s_wh, 1)
        with act.Fori(0, NT // 2) as i:
            for u in range(2):
                feed.high(act, i, u)
            for u in range(2):
                act.wait_ge(s_nb, i * 2 + u + 1)
                act.activation(ex[:, u, :], sc[:, u, :], ACT.Exp, bias=nbest[:, u:u + 1], accum_out=total[:, u:u + 1]).then_inc(s_ex, 1)
            for u in range(2):
                act.wait_ge(s_rT, i * 2 + u + 1)
                act.activation(rT[0][0:MR, u, :], rT_ps[u][0:MR, 0:P], ACT.Copy).then_inc(s_rh, 1)
    ph.scalar = scalar

    def vector(ve):
        order = Order(ve, s_ord)
        ve.wait_ge(s_small, 32)
        order.link(ve.memset(cum[:, :, :], 0.0))
        order.link(ve.memset(ranked[:, :, :], 0.0))
        with ve.Fori(0, NT // 2) as i:
            order.loop(i, 2 * 12)
            for u in range(2):
                feed.normalise(ve, i, u)
            for u in range(2):
                feed.low(ve, i, u)
            for u in range(2):
                ve.wait_ge(s_hg, i * 2 + u + 1)
                order.link(ve.tensor_tensor(sc[:, u, :], hg_ps[u][:, MR:RG], gb[:, :], ALU.add))
                order.link(ve.tensor_reduce(best[:, u:u + 1], sc[:, u, :], AX.X, ALU.max))
                ve.tensor_scalar(nbest[:, u:u + 1], best[:, u:u + 1], -1.0, None, ALU.mult).then_inc(s_nb, 1)
                order.link(ve.tensor_scalar(eq[:, u, :], sc[:, u, :], best[:, u:u + 1], None, ALU.is_equal))
                order.link(ve.tensor_copy(cum[:, u, 1:2], eq[:, u, 0:1]))
                order.link(ve.tensor_tensor(cum[:, u, 2:3], cum[:, u, 1:2], eq[:, u, 1:2], ALU.max))
                order.link(ve.tensor_tensor(cum[:, u, 3:4], cum[:, u, 2:3], eq[:, u, 2:3], ALU.max))
            for u in range(2):
                ve.wait_ge(s_ex, i * 2 + u + 1)
                order.link(ve.reciprocal(top[:, u:u + 1], total[:, u:u + 1]))
                order.link(ve.reciprocal(weight[:, u:u + 1], top[:, u:u + 1]))
                order.link(ve.tensor_tensor(weight[:, u:u + 1], weight[:, u:u + 1], top[:, u:u + 1], ALU.mult))
                order.link(ve.tensor_scalar(eq[:, u, :], cum[:, u, :], -1.0, 1.0, ALU.mult, ALU.add))
                order.link(ve.tensor_scalar(eq[:, u, :], eq[:, u, :], weight[:, u:u + 1], None, ALU.mult))
                for r in range(4):
                    c = slice(RANKS[r], RANKS[r + 1])
                    last = ve.tensor_scalar(ranked[:, u, c], hg_ps[u][:, c], eq[:, u, r:r + 1], None, ALU.mult)
                    last.then_inc(s_rk, 1)
            for u in range(2):
                ve.wait_ge(s_rh, i * 2 + u + 1)
                ve.tensor_tensor(rT[1][0:MR, u, :], rT_ps[u][0:MR, 0:P], rT[0][0:MR, u, :].bitcast(F32), ALU.subtract).then_inc(s_rl, 1)
            for u in range(2):
                ve.wait_ge(s_y, i * 2 + u + 1)
                xt = m.x[:, bass.ds(i * 2 + u, 1), :].rearrange("p o n -> p (o n)")
                ve.tensor_tensor(xt, xt, y_ps[u][:, :], ALU.add).then_inc(s_add, 1)
                ve.wait_ge(s_add, i * 2 + u + 1)
                tile_stats(ve, order, m, i * 2 + u)
            order.end(NT // 2)
        finish_stats(ve, order, m, m.s_ln[4])
    ph.vector = vector

    def tensor(pe):
        pe.sem_inc(feed.s_used, 2)
        pe.wait_ge(s_init, 2)
        with pe.Fori(0, NT // 2) as i:
            for u in range(2):
                feed.turn(pe, i, u)
            for u in range(2):
                pe.wait_ge(feed.s_lo, i * 2 + u + 1)
                pe.wait_ge(s_split, 1)
                for k in range(KT):
                    last = products(pe, hg_ps[u][:, 0:RG], [a[:, u, k, :] for a in feed.xT], [c[:, k, :] for c in ag],
                                    first=(k == 0), last=(k == KT - 1))
                last.then_inc(s_hg, 1)
            pe.wait_ge(s_split, 2)
            for u in range(2):
                for k in range(KT):
                    products(pe, y_ps[u][:, :], [a[:, u, k, :] for a in feed.xT], [c[:, k, :] for c in w],
                             first=(k == 0), last=False)
                pe.wait_ge(s_rk, i * 8 + u * 4 + 4)
                pe.transpose(rT_ps[u][:, 0:P], ranked[:, u, :], m.ident[:, :]).then_inc(s_rT, 1)
            pe.wait_ge(s_split, 3)
            for u in range(2):
                pe.wait_ge(s_rl, i * 2 + u + 1)
                products(pe, y_ps[u][:, :], [a[:, u, :] for a in rT], [b[:, :] for b in bb], first=False, last=True).then_inc(s_y, 1)
            pe.wait_ge(s_y, i * 2 + 2)
            pe.sem_inc(feed.s_used, 2)
    ph.tensor = tensor
    return ph


def gated(m, n, layer, full, rest, quantised):
    ph = Phase()
    TURNS = full // 2
    HALF = T // 2
    GU, W3 = 2 * KT * P, 2 * KT * P + D
    wgu = [m.sb(f"{n}_gate_up_{h}", [P, 2, GU], F32R) for h in ("high", "low")]
    wd = [m.sb(f"{n}_down_{h}", [P, 2, D], F32R) for h in ("high", "low")]
    xn = m.sb(f"{n}_xn", [P, 2, D])
    act_out, hid = m.sb(f"{n}_silu", [P, 2, HALF]), m.sb(f"{n}_hidden", [P, 2, HALF])
    hs = [m.sb(f"{n}_hidden_{h}", [P, 2, T], F32R) for h in ("high", "low")]
    raw = [m.raw[:, u * W3:(u + 1) * W3] for u in range(2)]
    if quantised:
        raw = [r.bitcast(I32) for r in raw]
        zero, scale = m.sb(f"{n}_zero", [P, 2, W3], I32), m.sb(f"{n}_scale", [P, 2, W3])
        wf = m.sb(f"{n}_weight", [P, 2, W3])
    src = (lambda u: wf[:, u, :]) if quantised else (lambda u: raw[u])
    xT_ps, g_ps, u_ps, y_ps = m.ps[0:2], m.ps[0:2], m.ps[2:4], m.ps[4:8]
    S = lambda h: m.layer_sem(f"{n}_{h}")
    s_w, s_taken = [S(f"w_loaded_{u}") for u in range(2)], S("w_taken")
    s_wf, s_gh, s_gl, s_dh, s_dl = S("dequantised"), S("gate_up_high"), S("gate_up_low"), S("down_high"), S("down_low")
    s_d0 = S("minus_zero")
    s_xn, s_xT, s_xh, s_xl = S("xn"), S("xn_turned"), S("xT_high"), S("xT_low")
    s_gate, s_up, s_silu, s_hid, s_hh, s_hl = S("gate"), S("up"), S("silu"), S("hidden"), S("hidden_high"), S("hidden_low")
    s_y, s_add, s_ord = S("y"), S("added"), S("dve_order")
    last_layer = layer + 1 == 8
    PER = 3 if quantised else 1

    def sync(sp):
        sp.wait_ge(m.s_ln[layer], 1)
        with sp.Fori(0, TURNS) as i:
            for u in range(2):
                t = i * 2 + u
                sp.wait_ge(s_taken, t + 1)
                one = lambda name: m.d[f"{n}_{name}"][bass.ds(t, 1)]
                sp.dma_start(raw[u], one("w").rearrange("o p n -> (o p) n")).then_inc(s_w[u], 16)
                if quantised:
                    sp.dma_start(zero[:, u, :], one("zero").to_broadcast([P, W3])).then_inc(s_w[u], 16)
                    sp.dma_start(scale[:, u, :], one("scale").to_broadcast([P, W3])).then_inc(s_w[u], 16)
        if rest:
            sp.wait_ge(s_taken, 2 * TURNS + 1)
            sp.dma_start(m.raw[:, 0:2 * KT * rest], m.d[f"{n}_rest_gate_up"]).then_inc(s_w[0], 16)
            sp.dma_start(m.raw[0:rest, GU:W3], m.d[f"{n}_rest_down"]).then_inc(s_w[0], 16)
    ph.sync = sync

    def gpsimd(pool):
        pool.wait_ge(m.s_ln[layer], 1)
        pool.sem_inc(s_taken, 2)

        def tile(i, u, width, prows):
            t = i * 2 + u
            gu = 2 * KT * width
            pool.wait_ge(s_gh, t + 1)
            pool.tensor_tensor(wgu[1][:, u, 0:gu], src(u)[:, 0:gu], wgu[0][:, u, 0:gu].bitcast(F32), ALU.subtract).then_inc(s_gl, 1)
            pool.wait_ge(s_dh, t + 1)
            pool.tensor_tensor(wd[1][0:prows, u, :], src(u)[0:prows, GU:W3], wd[0][0:prows, u, :].bitcast(F32), ALU.subtract).then_inc(s_dl, 1)
            pool.wait_ge(s_dl, t + 1)
            pool.wait_ge(s_gl, t + 1)
            pool.sem_inc(s_taken, 1)

        with pool.Fori(0, TURNS) as i:
            for u in range(2):
                tile(i, u, P, P)
        if rest:
            tile(TURNS, 0, rest, rest)
    ph.gpsimd = gpsimd

    def scalar(act):
        with act.Fori(0, NT // 2) as i:
            for u in range(2):
                act.wait_ge(s_xT, i * 2 + u + 1)
                act.activation(m.kvT[0][:, :, bass.ds((i * 2 + u) * P, P), 1], xT_ps[u][:, :].rearrange("p (k t) -> p k t", k=KT),
                               ACT.Copy).then_inc(s_xh, 1)

        def high_gate_up(i, u, width, loaded):
            t = i * 2 + u
            gu = 2 * KT * width
            if quantised:
                act.wait_ge(s_wf, t + 1)
            else:
                act.wait_ge(s_w[u], loaded)
            act.wait_ge(s_up, 2 * t + 1)
            act.activation(wgu[0][:, u, 0:gu], src(u)[:, 0:gu], ACT.Copy).then_inc(s_gh, 1)

        def high_down(i, u, prows):
            act.wait_ge(s_y, i * NT + 1)
            act.activation(wd[0][0:prows, u, :], src(u)[0:prows, GU:W3], ACT.Copy).then_inc(s_dh, 1)

        def silu(i, u, rows):
            t = i * 2 + u
            for h in range(2):
                act.wait_ge(s_gate, 2 * t + h + 1)
                act.activation(act_out[0:rows, h, :], g_ps[h][0:rows, :], ACT.Silu).then_inc(s_silu, 1)
                act.wait_ge(s_hid, 2 * t + h + 1)
                act.activation(hs[0][0:rows, u, h * HALF:(h + 1) * HALF], hid[0:rows, h, :], ACT.Copy).then_inc(s_hh, 1)

        high_gate_up(0, 0, P, 16)
        high_gate_up(0, 1, P, 16)
        high_down(0, 0, P)
        high_down(0, 1, P)
        with act.Fori(0, TURNS - 1) as i:
            for u in range(2):
                silu(i, u, P)
                high_gate_up(i + 1, u, P, (i + 2) * 16)
            for u in range(2):
                high_down(i + 1, u, P)
        silu(TURNS - 1, 0, P)
        if rest:
            high_gate_up(TURNS, 0, rest, TURNS * 16 + 32)
        silu(TURNS - 1, 1, P)
        if rest:
            high_down(TURNS, 0, rest)
            silu(TURNS, 0, rest)
    ph.scalar = scalar

    def vector(ve):
        order = Order(ve, s_ord)

        def dequantise(i, u):
            t = i * 2 + u
            ve.wait_ge(s_w[u], (i + 1) * 16 * PER)
            if not (isinstance(i, int) and i == 0):
                ve.wait_ge(s_gl, t - 1)
                ve.wait_ge(s_dl, t - 1)
            ve.tensor_tensor(wf[:, u, :], raw[u], zero[:, u, :], ALU.subtract).then_inc(s_d0, 1)
            ve.wait_ge(s_d0, t + 1)
            ve.tensor_tensor(wf[:, u, :], wf[:, u, :], scale[:, u, :], ALU.mult).then_inc(s_wf, 1)

        def hidden(i, u, rows):
            t = i * 2 + u
            for h in range(2):
                ve.wait_ge(s_silu, 2 * t + h + 1)
                ve.wait_ge(s_up, 2 * t + h + 5)
                ve.tensor_tensor(hid[0:rows, h, :], u_ps[h][0:rows, :], act_out[0:rows, h, :], ALU.mult).then_inc(s_hid, 1)
                ve.wait_ge(s_hh, 2 * t + h + 1)
                ve.tensor_tensor(hs[1][0:rows, u, h * HALF:(h + 1) * HALF], hid[0:rows, h, :],
                                 hs[0][0:rows, u, h * HALF:(h + 1) * HALF].bitcast(F32), ALU.subtract).then_inc(s_hl, 1)

        def add(i, final=False):
            for t in range(NT):
                ve.wait_ge(s_y, i * NT + t + 2)
                ve.tensor_tensor(m.x[:, t, :], m.x[:, t, :], y_ps[t % 4][:, :], ALU.add).then_inc(s_add, 1)
                if final:
                    ve.wait_ge(s_add, i * NT + t + 1)
                    tile_stats(ve, order, m, t)

        with ve.Fori(0, NT // 2) as i:
            for u in range(2):
                t = i * 2 + u
                ve.tensor_scalar(xn[:, u, :], m.x[:, bass.ds(t, 1), :].rearrange("p o n -> p (o n)"),
                                 m.mean[:, bass.ds(t, 1)], m.rstd[:, bass.ds(t, 1)], ALU.subtract, ALU.mult).then_inc(s_xn, 1)
            for u in range(2):
                ve.wait_ge(s_xh, i * 2 + u + 1)
                ve.tensor_tensor(m.kvT[1][:, :, bass.ds((i * 2 + u) * P, P), 1], xT_ps[u][:, :].rearrange("p (k t) -> p k t", k=KT),
                                 m.kvT[0][:, :, bass.ds((i * 2 + u) * P, P), 1].bitcast(F32), ALU.subtract).then_inc(s_xl, 1)
        if quantised:
            dequantise(0, 0)
            dequantise(0, 1)
        with ve.Fori(0, TURNS - 1 if quantised else TURNS) as i:
            for u in range(2):
                hidden(i, u, P)
                if quantised:
                    dequantise(i + 1, u)
            add(i)
        if quantised:
            hidden(TURNS - 1, 0, P)
            hidden(TURNS - 1, 1, P)
            add(TURNS - 1)
        if rest:
            hidden(TURNS, 0, rest)
            add(TURNS, final=not last_layer)
        ve.wait_ge(s_add, NT * (TURNS + (1 if rest else 0)))
        if last_layer:
            ve.tensor_copy(m.mean[:, :], m.mean_var[:, :, 0]).then_inc(m.s_ln[8], 1)
            return
        finish_stats(ve, order, m, m.s_ln[layer + 1])
    ph.vector = vector

    def tensor(pe):
        pe.sem_inc(s_up, 4)
        pe.sem_inc(s_y, 1)
        with pe.Fori(0, NT // 2) as i:
            for u in range(2):
                pe.wait_ge(s_xn, i * 2 + u + 1)
                for k in range(KT):
                    last = pe.transpose(xT_ps[u][:, k * P:(k + 1) * P], xn[:, u, k * P:(k + 1) * P], m.ident[:, :])
                last.then_inc(s_xT, 1)
        pe.wait_ge(s_xl, NT)

        def gate_up(i, u, width, peeled=False):
            t = i * 2 + u
            pe.wait_ge(s_gl, t + 1)
            for h in range(2):
                for j, (ps, done) in enumerate(((g_ps, s_gate), (u_ps, s_up))):
                    if u or peeled:
                        pe.wait_ge(s_silu if j == 0 else s_hid, 2 * t + h - 1)
                    for k in range(KT):
                        c = slice((j * KT + k) * width, (j * KT + k + 1) * width)
                        last = products(pe, ps[h][0:width, :], [w[:, u, c] for w in wgu],
                                        [a[:, k, h * HALF:(h + 1) * HALF, 1] for a in m.kvT], first=(k == 0), last=(k == KT - 1))
                    last.then_inc(done, 1)

        def down(i, rows, us):
            for t in range(NT):
                if t % 4 == 0:
                    pe.wait_ge(s_hl, i * 4 + 2 * us[-1] + t // 4 + 1)
                if t == 0:
                    pe.wait_ge(s_dl, i * 2 + us[-1] + 1)
                if t >= 4:
                    pe.wait_ge(s_add, i * NT + t - 3)
                for u in us:
                    last = products(pe, y_ps[t % 4][:, :], [a[0:rows, u, t * P:(t + 1) * P] for a in hs],
                                    [w[0:rows, u, :] for w in wd], first=(u == us[0]), last=(u == us[-1]))
                last.then_inc(s_y, 1)

        with pe.Fori(0, TURNS) as i:
            for u in range(2):
                gate_up(i, u, P)
            down(i, P, (0, 1))
            pe.wait_ge(s_add, (i + 1) * NT - 2)
        if rest:
            gate_up(TURNS, 0, rest, peeled=True)
            down(TURNS, rest, (0,))
    ph.tensor = tensor
    return ph


def gated_feedforward(m):
    return gated(m, "f2", 5, 10, 96, False)


def quantised_feedforward(m):
    return gated(m, "f3", 7, 14, 0, True)


def linear_attention(m):
    ph = Phase()
    ctx_raw = m.sb("n3_ctx", [P, 2, D])
    ek = m.sb("n3_k_exp", [P, 2, D])
    ekT = [m.sb(f"n3_kT_{h}", [P, 2, KT, P], F32R) for h in ("high", "low")]
    kvm = m.sb("n3_kv", [P, 2, P])
    kv = [m.sb(f"n3_kv_{h}", [P, 2, P], F32R) for h in ("high", "low")]
    xn = m.sb("n3_xn", [P, 2, D])
    eq = m.sb("n3_q_exp", [P, 2, D])
    qs = [m.sb(f"n3_q_{h}", [P, 2, D], F32R) for h in ("high", "low")]
    mx, nb, tot, rt = (m.sb(f"n3_{h}", [P, 2]) for h in ("max", "nbias", "total", "rtotal"))
    rden = m.sb("n3_rden", [P, 2, D])
    y = m.sb("n3_y", [P, 2, D])
    blocks = m.sb("n3_blocks", [P, P])
    blocks_r = m.sb("n3_blocks_r", [P, P], F32R)
    kT_ps, kv_ps, den_ps, y_ps = m.ps[0:2], m.ps[2:4], m.ps[4:6], m.ps[6:8]
    S = lambda h: m.layer_sem(f"n3_{h}")
    s_blk, s_c = S("blocks_loaded"), [S(f"ctx_loaded_{u}") for u in range(2)]
    s_nb, s_ek, s_kt, s_kh, s_kl = S("nbias"), S("k_exp"), S("kT"), S("kT_high"), S("kT_low")
    s_kv, s_kvm, s_kvh, s_kvl = S("kv"), S("kv_masked"), S("kv_high"), S("kv_low")
    s_xn, s_eq, s_qh, s_ql = S("xn"), S("q_exp"), S("q_high"), S("q_low")
    s_den, s_y, s_ord, s_add, s_blkr = S("den"), S("y"), S("dve_order"), S("added"), S("blocks_ready")

    def sync(sp):
        sp.wait_ge(m.s_ln[6], 1)
        sp.dma_start(blocks[:, :], m.d["blocks"]).then_inc(s_blk, 16)
        ctx_d = m.d["ctx"].rearrange("(t p) n -> p t n", p=P)
        with sp.Fori(0, NT // 2) as i:
            for u in range(2):
                sp.wait_ge(s_ek, i * 2 + u + 1)
                sp.dma_start(ctx_raw[:, u, :], ctx_d[:, bass.ds(i * 2 + u, 1), :].rearrange("p o n -> p (o n)")).then_inc(s_c[u], 16)
    ph.sync = sync

    def gpsimd(pool):
        with pool.Fori(0, NT // 2) as i:
            for u in range(2):
                pool.wait_ge(s_qh, i * 2 + u + 1)
                pool.tensor_tensor(qs[1][:, u, :], eq[:, u, :], qs[0][:, u, :].bitcast(F32), ALU.subtract).then_inc(s_ql, 1)
            for u in range(2):
                pool.wait_ge(s_kvh, i * 2 + u + 1)
                pool.tensor_tensor(kv[1][:, u, :], kvm[:, u, :], kv[0][:, u, :].bitcast(F32), ALU.subtract).then_inc(s_kvl, 1)
    ph.gpsimd = gpsimd

    def scalar(act):
        act.sem_inc(s_ek, 2)
        act.wait_ge(m.s_ln[6], 1)
        with act.Fori(0, NT // 2) as i:
            for u in range(2):
                act.wait_ge(s_nb, i * 2 + u + 1)
                act.activation(ek[:, u, :], ctx_raw[:, u, :], ACT.Exp, bias=nb[:, u:u + 1], accum_out=tot[:, u:u + 1]).then_inc(s_ek, 1)
            for u in range(2):
                act.wait_ge(s_xn, i * 2 + u + 1)
                act.activation(eq[:, u, :], xn[:, u, :], ACT.Exp).then_inc(s_eq, 1)
            for u in range(2):
                act.wait_ge(s_eq, i * 2 + u + 1)
                act.activation(qs[0][:, u, :], eq[:, u, :], ACT.Copy).then_inc(s_qh, 1)
            for u in range(2):
                act.wait_ge(s_kt, i * 2 + u + 1)
                act.activation(ekT[0][:, u, :, :], kT_ps[u][:, :].rearrange("p (k c) -> p k c", k=KT), ACT.Copy).then_inc(s_kh, 1)
            for u in range(2):
                act.wait_ge(s_kvm, i * 2 + u + 1)
                act.activation(kv[0][:, u, :], kvm[:, u, :], ACT.Copy).then_inc(s_kvh, 1)
    ph.scalar = scalar

    def vector(ve):
        order = Order(ve, s_ord)
        ve.wait_ge(s_blk, 16)
        ve.tensor_copy(blocks_r[:, :], blocks[:, :]).then_inc(s_blkr, 1)
        with ve.Fori(0, NT // 2) as i:
            order.loop(i, 2 * 4)
            for u in range(2):
                ve.wait_ge(s_c[u], (i + 1) * 16)
                order.link(ve.tensor_reduce(mx[:, u:u + 1], ctx_raw[:, u, :], AX.X, ALU.max))
                ve.tensor_scalar(nb[:, u:u + 1], mx[:, u:u + 1], -1.0, None, ALU.mult).then_inc(s_nb, 1)
            for u in range(2):
                t = i * 2 + u
                ve.tensor_scalar(xn[:, u, :], m.x[:, bass.ds(t, 1), :].rearrange("p o n -> p (o n)"),
                                 m.mean[:, bass.ds(t, 1)], m.rstd[:, bass.ds(t, 1)], ALU.subtract, ALU.mult).then_inc(s_xn, 1)
            for u in range(2):
                ve.wait_ge(s_ek, i * 2 + u + 3)
                order.link(ve.reciprocal(rt[:, u:u + 1], tot[:, u:u + 1]))
            for u in range(2):
                ve.wait_ge(s_kh, i * 2 + u + 1)
                ve.tensor_tensor(ekT[1][:, u, :, :], kT_ps[u][:, :].rearrange("p (k c) -> p k c", k=KT),
                                 ekT[0][:, u, :, :].bitcast(F32), ALU.subtract).then_inc(s_kl, 1)
            for u in range(2):
                ve.wait_ge(s_den, i * 2 + u + 1)
                order.done(ve.reciprocal(rden[:, u, :], den_ps[u][:, :]))
                ve.wait_ge(s_kv, i * 2 + u + 1)
                ve.scalar_tensor_tensor(kvm[:, u, :], kv_ps[u][:, 0:P], rt[:, u:u + 1], blocks[:, :], ALU.mult, ALU.mult).then_inc(s_kvm, 1)
            for u in range(2):
                t = i * 2 + u
                xt = m.x[:, bass.ds(t, 1), :].rearrange("p o n -> p (o n)")
                ve.wait_ge(s_y, t + 1)
                if u == 0:
                    order.wait()
                ve.tensor_tensor(y[:, u, :], y_ps[u][:, :], rden[:, u, :], ALU.mult).then_inc(s_add, 1)
                ve.wait_ge(s_add, i * 4 + u * 2 + 1)
                ve.tensor_tensor(xt, xt, y[:, u, :], ALU.add).then_inc(s_add, 1)
                ve.wait_ge(s_add, i * 4 + u * 2 + 2)
                tile_stats(ve, order, m, t)
            order.end(NT // 2)
        finish_stats(ve, order, m, m.s_ln[7])
    ph.vector = vector

    def tensor(pe):
        pe.wait_ge(s_blkr, 1)
        with pe.Fori(0, NT // 2) as i:
            for u in range(2):
                pe.wait_ge(s_ek, i * 2 + u + 3)
                for k in range(KT):
                    last = pe.transpose(kT_ps[u][:, k * P:(k + 1) * P], ek[:, u, k * P:(k + 1) * P], m.ident[:, :])
                last.then_inc(s_kt, 1)
            for u in range(2):
                pe.wait_ge(s_ql, i * 2 + u + 1)
                pe.matmul(den_ps[u][:, :], blocks_r[:, :], qs[0][:, u, :], start=True, stop=False)
                pe.matmul(den_ps[u][:, :], blocks_r[:, :], qs[1][:, u, :], start=False, stop=True).then_inc(s_den, 1)
            for u in range(2):
                pe.wait_ge(s_kl, i * 2 + u + 1)
                for k in range(KT):
                    last = products(pe, kv_ps[u][:, 0:P], [a[:, u, k, :] for a in ekT],
                                    [a[:, k, bass.ds((i * 2 + u) * P, P), 0] for a in m.kvT], first=(k == 0), last=(k == KT - 1))
                last.then_inc(s_kv, 1)
            for u in range(2):
                pe.wait_ge(s_kvl, i * 2 + u + 1)
                products(pe, y_ps[u][:, :], [a[:, u, :] for a in kv], [a[:, u, :] for a in qs]).then_inc(s_y, 1)
    ph.tensor = tensor
    return ph


LAYERS = [context_attention, clustered_linear, latent_attention, ranked_linear, rotary_attention, gated_feedforward, linear_attention, quantised_feedforward]


class Memory:

    def __init__(self, nc, ctx, dram):
        self.nc, self.ctx, self.d = nc, ctx, dram
        self.layer = ExitStack()
        self.layer_sems = [ExitStack()]
        keep = lambda n, s, dt=F32: ctx.enter_context(nc.sbuf_tensor(n, s, dt))
        self.x = keep("x_rows", [P, NT, D])
        self.kvT = [keep(f"kvT_{h}", [P, KT, T, 2], F32R) for h in ("high", "low")]
        self.ident = keep("ident", [P, P])
        self.stats = keep("ln_stats", [P, NT, 6])
        self.mean_var = keep("ln_mean_var", [P, NT, 2])
        self.var, self.rstd, self.mean = (keep(f"ln_{n}", [P, NT]) for n in ("var", "rstd", "mean"))
        self.bits = keep("rsqrt_bits", [P, 16], I32)
        self.half, self.tmp = keep("rsqrt_half", [P, 16]), keep("rsqrt_tmp", [P, 16])
        self.ps = [ctx.enter_context(nc.psum_tensor(f"bank{i}", [P, 512], F32)) for i in range(8)]
        self.s_ident = self.sem("ident_loaded")
        self.s_ln = {k: self.sem(f"l{k}_stats_ready") for k in range(1, len(LAYERS) + 1)}
        self.s_kv_ctx = self.sem("kvT_ctx_ready")
        self.s_left = [self.sem(f"layer_{k}_left") for k in range(len(LAYERS) - 2)]
        self.s_cleared, self.s_stored = self.sem("layer_semaphores_cleared"), self.sem("stored")
        self.raw = keep("raw_weights", [P, 5120])
        self.ones_row, self.ones_col = keep("ones_row", [1, P], F32R), keep("ones_col", [P, 1])
        self.zero = keep("zero", [P, 1])
        self.s_ones = self.sem("ones")
        self.own = [[]]

    def sb(self, name, shape, dt=F32):
        return self.layer.enter_context(self.nc.sbuf_tensor(name, shape, dt))

    def sem(self, name):
        return self.ctx.enter_context(self.nc.semaphore(name))

    def layer_sem(self, name):
        sem = self.layer_sems[-1].enter_context(self.nc.semaphore(name))
        self.own[-1].append(sem)
        return sem

    def next_layer(self):
        self.layer.close()
        self.layer_sems.append(ExitStack())
        self.own.append([])
        if len(self.layer_sems) >= 3:
            self.layer_sems[-3].close()


def build(nc, dram, out):
    with ExitStack() as ctx:
        m = Memory(nc, ctx, dram)
        layers = []
        for make in LAYERS:
            layers.append(make(m))
            m.next_layer()
        s_left, s_cleared, s_stored = m.s_left, m.s_cleared, m.s_stored

        def run(eng, part):
            for k, layer in enumerate(layers):
                if k >= 2:
                    eng.wait_ge(s_cleared, k - 1)
                part(layer)(eng)
                if k + 2 < len(layers):
                    eng.sem_inc(s_left[k], 1)

        block = ctx.enter_context(nc.Block())

        @block.sync
        def _(sp):
            for k, layer in enumerate(layers):
                if k >= 2:
                    sp.wait_ge(s_left[k - 2], 5)
                    for sem in m.own[k - 2]:
                        sp.sem_clear(sem)
                    sp.sem_inc(s_cleared, 1)
                layer.sync(sp)
                if k + 2 < len(layers):
                    sp.sem_inc(s_left[k], 1)
            sp.wait_ge(m.s_ln[len(LAYERS)], 1)
            sp.dma_start(out.rearrange("(t p) n -> p t n", p=P), m.x[:, :, :]).then_inc(s_stored, 16)
            sp.wait_ge(s_stored, 16)

        @block.scalar
        def _(act):
            run(act, lambda layer: layer.scalar)

        @block.vector
        def _(ve):
            ve.memset(m.ones_row[:, :].bitcast(F32), 1.0).then_inc(m.s_ones, 1)
            ve.memset(m.ones_col[:, :], 1.0).then_inc(m.s_ones, 1)
            ve.memset(m.zero[:, :], 0.0).then_inc(m.s_ones, 1)
            run(ve, lambda layer: layer.vector)

        @block.gpsimd
        def _(pool):
            pool.wait_ge(m.s_ones, 3)
            run(pool, lambda layer: layer.gpsimd)

        @block.tensor
        def _(pe):
            pe.wait_ge(m.s_ones, 3)
            run(pe, lambda layer: layer.tensor)


def lay_out(v):
    c = np.ascontiguousarray
    a = {k: np.asarray(x) for k, x in v.items()}
    rows = lambda z: c(z.reshape(T, D))
    d = {"x": rows(a["x"]), "ctx": rows(a["ctx_4096"]), "ctxT": c(a["ctx_4096"].reshape(T, D).T),
         "ident": np.eye(P, dtype=np.float32)}
    one_row = lambda z: c(z.reshape(1, -1))
    d["c0_w"], d["c0_centroids"] = c(a["L0_ffn_weight"].T), c(a["L0_ffn_centroids"].T)
    d["c0_bias"], d["c0_owner"] = one_row(a["L0_ffn_bias"]), one_row(a["L0_ffn_assignments"])
    for name, layer in (("a1", "L1"), ("a2", "L2")):
        wq, wk, wv, wo = (a[f"{layer}_xattn_W{s}"] for s in "qkvo")
        by_group = lambda w: w.reshape(KT, P, 8, -1).transpose(2, 1, 0, 3)
        wkv = np.concatenate([by_group(wk), by_group(wv)], axis=3)
        wog = wo.reshape(8, 4, P, D).transpose(0, 2, 1, 3)
        d[f"{name}_w"] = np.concatenate([by_group(wq).reshape(8, P, -1), wkv.reshape(8, P, -1), wog.reshape(8, P, -1)], axis=2)
    d["a1_norm_w"] = np.stack([a["L1_xattn_q_norm_w"], a["L1_xattn_k_norm_w"]], axis=1)
    f32 = np.float32
    phase = np.arange(C, dtype=f32)[:, None] * (f32(1.0) / f32(10000.0) ** (np.arange(0, P, 2, dtype=f32) / f32(P)))[None, :]
    cos, sin = np.tile(np.cos(phase), (1, 2)), np.sin(phase)
    d["cosT"], d["sinT"] = c(cos.T), c(np.concatenate([sin, -sin], axis=1).T)
    d["cosk"], d["sink"] = np.tile(cos, (2, 1)), np.tile(np.concatenate([-sin, sin], axis=1), (2, 1))
    mask = a["mask_1x1xSxS2_bk0"].reshape(C, C)
    d["mask"], d["maskT"] = c(mask), c(mask.T)
    d["r1_w"], d["r1_a_gate"] = c(a["L1_ffn_W"].T), c(np.concatenate([a["L1_ffn_A"].T, a["L1_ffn_gate_w"].T], axis=1))
    d["r1_b"], d["r1_gate_b"] = np.concatenate([a["L1_ffn_B"].T, one_row(a["L1_ffn_b"])]), one_row(a["L1_ffn_gate_b"])
    def tiles(w, k):
        return w.reshape(KT, P, k, P).transpose(2, 1, 0, 3).reshape(k, P, D)
    gate, up, down = a["L2_ffn_W_gate"].T, a["L2_ffn_W_up"].T, a["L2_ffn_W_down"].T
    full = gate.shape[1] // P
    edge = full * P
    d["f2_w"] = np.concatenate([tiles(gate[:, :edge], full), tiles(up[:, :edge], full), down[:edge].reshape(full, P, D)], axis=2)
    last = lambda w: w[:, edge:].reshape(KT, P, -1).transpose(1, 0, 2).reshape(P, -1)
    d["f2_rest_gate_up"], d["f2_rest_down"] = np.concatenate([last(gate), last(up)], axis=1), c(down[edge:])
    q = lambda name: a[f"L3_ffn_{name}"]
    full = q("gate_w").shape[1] // P
    d["f3_w"] = np.concatenate([tiles(q("gate_w"), full), tiles(q("up_w"), full), q("down_w").reshape(full, P, D)], axis=2)
    columns = lambda z: z.reshape(KT, full, P).transpose(1, 0, 2).reshape(full, D)
    for name, s in (("zero", "z"), ("scale", "s")):
        d[f"f3_{name}"] = np.concatenate([columns(q(f"gate_{s}")), columns(q(f"up_{s}")), q(f"down_{s}")], axis=1)
    d["blocks"] = np.kron(np.eye(P // 8, dtype=np.float32), np.ones((8, 8), np.float32))
    return d


def kernel(**inputs):
    import concourse.bacc as bacc
    from concourse.bass_utils import run_bass_kernel_spmd

    nc = bacc.Bacc("TRN2", target_bir_lowering=False, num_devices=1)
    arrays = {f"in_{name}": a for name, a in lay_out(inputs).items()}
    dram = {name[3:]: nc.dram_tensor(name, a.shape, mybir.dt.from_np(a.dtype), kind="ExternalInput").ap()
            for name, a in arrays.items()}
    out = nc.dram_tensor("out", (T, D), F32, kind="ExternalOutput").ap()
    build(nc, dram, out)
    r = run_bass_kernel_spmd(nc, [arrays], core_ids=[0])
    return r.results[0]["out"].reshape(B, C, N)
```
